# Optimizing a Trainium2 kernel written in Bass

```python
import numpy as np
import jax
import jax.numpy as jnp

def _softmax(x, axis=-1):
    return jax.nn.softmax(x, axis=axis)

def _gelu(x):
    return jax.nn.gelu(x, approximate=True)

def _silu(x):
    return jax.nn.silu(x)

def _sigmoid(x):
    return jax.nn.sigmoid(x)

def _layernorm(x, axis=-1, eps=1e-05):
    m = jnp.mean(x, axis=axis, keepdims=True)
    v = jnp.var(x, axis=axis, keepdims=True)
    return (x - m) / jnp.sqrt(v + eps)

def _scatter_add(tgt, idx, src, axis=0):
    return tgt.at[idx].add(src)

def _segment_sum(src, seg, n):
    return jax.ops.segment_sum(src, seg, n)
kernel_name = 'mk_decoder_postln_d1_seqx_r4_4f60dd'

def setup_inputs(seed: int=0):
    np.random.seed(seed)
    _w = jnp.asarray

    def _rec_inputs():
        import jax
        import jax.numpy as jnp
        _rk = jax.random.key(seed)
        x = -0.0003929 + 0.9999 * jax.random.normal(jax.random.fold_in(_rk, 1), (4, 512, 256), jnp.float32)
        _lenS = 512 - jax.random.randint(jax.random.fold_in(_rk, 7), (4,), 0, max(1, 512 // 4) + 1, jnp.int32)
        _lenS2 = 512 - jax.random.randint(jax.random.fold_in(_rk, 8), (4,), 0, max(1, 512 // 4) + 1, jnp.int32)
        _ctx_1024P = jax.random.normal(jax.random.fold_in(_rk, 11), (4, 16, 256), jnp.float32)
        _ctx_1024c = jax.random.dirichlet(jax.random.fold_in(_rk, 511), 0.3 * jnp.ones((16,), jnp.float32), (4, 512))
        _ctx_1024t = jnp.einsum('bsk,bkd->bsd', _ctx_1024c, _ctx_1024P)
        _ctx_1024t = _ctx_1024t * jax.lax.rsqrt(jnp.mean(jnp.square(_ctx_1024t)) + 1e-12) * 0.953939
        ctx_1024 = 2.81802e-05 + 1.00001 * (_ctx_1024t + 0.3 * jax.random.normal(jax.random.fold_in(_rk, 611), (4, 512, 256), jnp.float32))
        return (x, ctx_1024)
    x, ctx_1024 = _rec_inputs()

    def _L0_attn_setup():
        import jax, jax.numpy as jnp
        import numpy as np
        from jax.scipy.linalg import solve_triangular
        B, L, HID, H = (2, 512, 256, 4)
        DK, DV = (HID // H, HID // H)
        CHUNK = 32
        CONV_K, FIR_SK, FIR_LK, FIR_WK = (4, 3, 31, 64)
        GIN = HID + 15 * H
        GH = 2 * HID
        FLOOR_INIT = float(np.log(0.05 / 0.95))

        def _l2norm(x):
            return x / jnp.sqrt(jnp.sum(x * x, -1, keepdims=True) + 1e-06)

        def _dwconv_causal(x_blc, w_ck):
            K = w_ck.shape[-1]
            x = jnp.moveaxis(x_blc, 1, 2)
            x = jnp.pad(x, ((0, 0), (0, 0), (K - 1, 0)))
            y = jax.lax.conv_general_dilated(x, w_ck[:, None, :], (1,), 'VALID', feature_group_count=w_ck.shape[0], dimension_numbers=('NCH', 'OIH', 'NCH'))
            return jnp.moveaxis(y, 2, 1)

        def _delta_rule(q, k, v, beta):
            b, h, Ll, dk = q.shape
            dv = v.shape[-1]
            n = Ll // CHUNK
            q = _l2norm(q)
            k = _l2norm(k)
            v = v * beta[..., None]
            kb = k * beta[..., None]
            rs = lambda t: t.reshape(b, h, n, CHUNK, t.shape[-1])
            q, k, v, kb = (rs(q), rs(k), rs(v), rs(kb))
            tril_strict = jnp.tril(jnp.ones((CHUNK, CHUNK), bool), -1)
            tril = jnp.tril(jnp.ones((CHUNK, CHUNK), bool), 0)
            A = jnp.where(tril_strict, kb @ jnp.swapaxes(k, -1, -2), 0.0)
            eye = jnp.eye(CHUNK, dtype=q.dtype)
            inv = solve_triangular(eye + A, jnp.broadcast_to(eye, A.shape), lower=True)
            u = inv @ v
            w = inv @ kb
            qs, ks, us, ws = (jnp.moveaxis(t, 2, 0) for t in (q, k, u, w))
            S0 = jnp.zeros((b, h, dk, dv), q.dtype)

            def step(S, xs):
                q_i, k_i, u_i, w_i = xs
                attn = jnp.where(tril, q_i @ jnp.swapaxes(k_i, -1, -2), 0.0)
                u_adj = u_i - w_i @ S
                o_i = q_i @ S + attn @ u_adj
                S = S + jnp.swapaxes(k_i, -1, -2) @ u_adj
                return (S, o_i)
            S, o = jax.lax.scan(step, S0, (qs, ks, us, ws))
            o = jnp.moveaxis(o, 0, 2).reshape(b, h, Ll, dv)
            return (o, S)

        def _stats(x):
            mean = x.mean(-1)
            rms = jnp.sqrt(jnp.clip(jnp.mean(x * x, -1), 1e-08))
            mx = jnp.abs(x).max(-1)
            return jnp.concatenate([mean, rms, mx], -1)

        def _forward(hidden_states, q_w, k_w, v_w, b_w, convq_w, convk_w, convv_w, fir_s, fir_l, fir_wd, g1_w, g1_b, g2_w, g2_b, value_bias, log_temp, floor_logit, onorm_w, o_w):
            b, Ll, _ = hidden_states.shape
            q = jax.nn.silu(_dwconv_causal(hidden_states @ q_w.T, convq_w))
            k = jax.nn.silu(_dwconv_causal(hidden_states @ k_w.T, convk_w))
            v = jax.nn.silu(_dwconv_causal(hidden_states @ v_w.T, convv_w))
            tohd = lambda t: t.reshape(b, Ll, H, -1)
            q, k, v = (tohd(q), tohd(k), tohd(v))
            beta = jax.nn.sigmoid(hidden_states @ b_w.T)
            tr = lambda t: jnp.moveaxis(t, 1, 2)
            delta_out, _S = _delta_rule(tr(q), tr(k), tr(v), jnp.moveaxis(beta, 1, 2))
            delta_out = jnp.moveaxis(delta_out, 1, 2)

            def fir(x, filt):
                y = _dwconv_causal(x.reshape(b, Ll, H * DV), filt.reshape(H * DV, -1))
                return y.reshape(b, Ll, H, DV)
            short, long_, wide = (fir(v, fir_s), fir(v, fir_l), fir(v, fir_wd))
            gate_in = jnp.concatenate([hidden_states, _stats(short), _stats(long_), _stats(wide), _stats(delta_out), _stats(v)], -1)
            hdn = jax.nn.gelu(gate_in @ g1_w.T + g1_b, approximate=False)
            logits = (hdn @ g2_w.T + g2_b).reshape(b, Ll, H, 5)
            logits = logits.at[..., 4].add(value_bias)
            logits = logits / jnp.exp(log_temp)[None, None, :, None]
            p = jax.nn.softmax(logits, -1)
            f = jax.nn.sigmoid(floor_logit)[None, None, :, None]
            scale = 1.0 - 4.0 * f
            w_ctx = f + scale * p[..., :4]
            w_val = scale * p[..., 4:5]
            o = w_ctx[..., 0:1] * short + w_ctx[..., 1:2] * long_ + w_ctx[..., 2:3] * wide + w_ctx[..., 3:4] * delta_out + w_val * v
            o = o * jax.lax.rsqrt(jnp.mean(o * o, -1, keepdims=True) + 1e-05) * onorm_w
            return o.reshape(b, Ll, HID) @ o_w.T
        key = jax.random.key(seed)
        ks = jax.random.split(key, 16)
        rn = lambda i, shp, s: jax.random.normal(ks[i], shp, jnp.float32) * s
        fir_init = lambda i, K: jnp.zeros((H, DV, K), jnp.float32).at[..., -1].set(1.0) + rn(i, (H, DV, K), 0.02)
        g2_b = jnp.zeros((5 * H,), jnp.float32).at[4::5].set(4.0)
        return {'hidden_states': jax.random.normal(ks[0], (B, L, HID), jnp.float32), 'q_w': rn(1, (HID, HID), 0.02), 'k_w': rn(2, (HID, HID), 0.02), 'v_w': rn(3, (HID, HID), 0.02), 'b_w': rn(4, (H, HID), 0.02), 'convq_w': rn(5, (HID, CONV_K), 0.2), 'convk_w': rn(6, (HID, CONV_K), 0.2), 'convv_w': rn(7, (HID, CONV_K), 0.2), 'fir_s': fir_init(8, FIR_SK), 'fir_l': fir_init(9, FIR_LK), 'fir_wd': fir_init(10, FIR_WK), 'g1_w': rn(11, (GH, GIN), 0.02), 'g1_b': jnp.zeros((GH,), jnp.float32), 'g2_w': rn(12, (5 * H, GH), 0.02), 'g2_b': g2_b, 'value_bias': jnp.full((H,), 4.0, jnp.float32), 'log_temp': jnp.zeros((H,), jnp.float32), 'floor_logit': jnp.full((H,), FLOOR_INIT, jnp.float32), 'onorm_w': jnp.ones((DV,), jnp.float32), 'o_w': rn(13, (HID, HID), 0.02)}
    _L0_attn_all = _L0_attn_setup()
    _L0_attn_in = {k: v for k, v in _L0_attn_all.items() if k in ('q_w', 'k_w', 'v_w', 'b_w', 'convq_w', 'convk_w', 'convv_w', 'fir_s', 'fir_l', 'fir_wd', 'g1_w', 'g1_b', 'g2_w', 'g2_b', 'value_bias', 'log_temp', 'floor_logit', 'onorm_w', 'o_w')}
    del _L0_attn_all

    def _L0_xattn_setup():
        import math
        import jax, jax.numpy as jnp
        import numpy as np
        D_MODEL = 256
        N_HEADS = 16
        D_K = D_MODEL // N_HEADS

        def _autocorr_forward(queries, keys, values, Wq, bq, Wk, bk, Wv, bv, Wo, bo):
            B, L, D = queries.shape
            H, dk = (N_HEADS, D_K)
            q = (queries @ Wq.T + bq).reshape(B, L, H, dk)
            k = (keys @ Wk.T + bk).reshape(B, L, H, dk)
            v = (values @ Wv.T + bv).reshape(B, L, H, dk)
            qf = jnp.fft.rfft(q, axis=1)
            kf = jnp.fft.rfft(k, axis=1)
            corr = jnp.fft.irfft(qf * jnp.conj(kf), n=L, axis=1).mean(axis=-1)
            corr = corr.transpose(0, 2, 1)
            topk = min(max(1, int(math.log(L))), L)
            weights, delays = jax.lax.top_k(corr, topk)
            w = jax.nn.softmax(weights, axis=-1)
            idx = (jnp.arange(L)[None, None, None, :] - delays[..., None]) % L
            v_h = v.transpose(0, 2, 1, 3)
            gathered = jnp.take_along_axis(v_h[:, :, None], idx[..., None], axis=3)
            out = (w[..., None, None] * gathered).sum(axis=2)
            out = out.transpose(0, 2, 1, 3).reshape(B, L, D)
            return out @ Wo.T + bo
        key = jax.random.key(seed)
        ks = jax.random.split(key, 12)
        B, L, D = (8, 512, D_MODEL)
        scale = 1.0 / math.sqrt(D)
        inp = {'queries': jax.random.normal(ks[0], (B, L, D), jnp.float32), 'keys': jax.random.normal(ks[1], (B, L, D), jnp.float32), 'values': jax.random.normal(ks[2], (B, L, D), jnp.float32), 'Wq': jax.random.normal(ks[3], (D, D), jnp.float32) * scale, 'bq': jnp.zeros((D,), jnp.float32), 'Wk': jax.random.normal(ks[4], (D, D), jnp.float32) * scale, 'bk': jnp.zeros((D,), jnp.float32), 'Wv': jax.random.normal(ks[5], (D, D), jnp.float32) * scale, 'bv': jnp.zeros((D,), jnp.float32), 'Wo': jax.random.normal(ks[6], (D, D), jnp.float32) * scale, 'bo': jnp.zeros((D,), jnp.float32)}
        return inp
    _L0_xattn_all = _L0_xattn_setup()
    _L0_xattn_in = {k: v for k, v in _L0_xattn_all.items() if k in ('Wq', 'bq', 'Wk', 'bk', 'Wv', 'bv', 'Wo', 'bo')}
    del _L0_xattn_all

    def _L0_ffn_setup():
        import jax, jax.numpy as jnp
        import numpy as np
        DIM = 256
        HIDDEN = 768
        SCALE = 1.0 / 127.0

        def _dequant(w_int, dtype):
            return w_int.astype(dtype) * jnp.asarray(SCALE, dtype)
        key = jax.random.key(seed)
        k_x, k_g, k_u, k_d = jax.random.split(key, 4)
        x = jax.random.normal(k_x, (4, 512, DIM), dtype=jnp.float32)
        w_gate = jax.random.randint(k_g, (HIDDEN, DIM), -127, 128, dtype=jnp.int32)
        w_up = jax.random.randint(k_u, (HIDDEN, DIM), -127, 128, dtype=jnp.int32)
        w_down = jax.random.randint(k_d, (DIM, HIDDEN), -127, 128, dtype=jnp.int32)
        return {'x': x, 'w_gate': w_gate, 'w_up': w_up, 'w_down': w_down}
    _L0_ffn_all = _L0_ffn_setup()
    _L0_ffn_in = {k: v for k, v in _L0_ffn_all.items() if k in ('w_gate', 'w_up', 'w_down')}
    del _L0_ffn_all
    return {'x': x, 'ctx_1024': ctx_1024, 'L0_attn_q_w': _L0_attn_in['q_w'], 'L0_attn_k_w': _L0_attn_in['k_w'], 'L0_attn_v_w': _L0_attn_in['v_w'], 'L0_attn_b_w': _L0_attn_in['b_w'], 'L0_attn_convq_w': _L0_attn_in['convq_w'], 'L0_attn_convk_w': _L0_attn_in['convk_w'], 'L0_attn_convv_w': _L0_attn_in['convv_w'], 'L0_attn_fir_s': _L0_attn_in['fir_s'], 'L0_attn_fir_l': _L0_attn_in['fir_l'], 'L0_attn_fir_wd': _L0_attn_in['fir_wd'], 'L0_attn_g1_w': _L0_attn_in['g1_w'], 'L0_attn_g1_b': _L0_attn_in['g1_b'], 'L0_attn_g2_w': _L0_attn_in['g2_w'], 'L0_attn_g2_b': _L0_attn_in['g2_b'], 'L0_attn_value_bias': _L0_attn_in['value_bias'], 'L0_attn_log_temp': _L0_attn_in['log_temp'], 'L0_attn_floor_logit': _L0_attn_in['floor_logit'], 'L0_attn_onorm_w': _L0_attn_in['onorm_w'], 'L0_attn_o_w': _L0_attn_in['o_w'], 'L0_xattn_Wq': _L0_xattn_in['Wq'], 'L0_xattn_bq': _L0_xattn_in['bq'], 'L0_xattn_Wk': _L0_xattn_in['Wk'], 'L0_xattn_bk': _L0_xattn_in['bk'], 'L0_xattn_Wv': _L0_xattn_in['Wv'], 'L0_xattn_bv': _L0_xattn_in['bv'], 'L0_xattn_Wo': _L0_xattn_in['Wo'], 'L0_xattn_bo': _L0_xattn_in['bo'], 'L0_ffn_w_gate': _L0_ffn_in['w_gate'], 'L0_ffn_w_up': _L0_ffn_in['w_up'], 'L0_ffn_w_down': _L0_ffn_in['w_down']}

def reference(x, ctx_1024, L0_attn_q_w, L0_attn_k_w, L0_attn_v_w, L0_attn_b_w, L0_attn_convq_w, L0_attn_convk_w, L0_attn_convv_w, L0_attn_fir_s, L0_attn_fir_l, L0_attn_fir_wd, L0_attn_g1_w, L0_attn_g1_b, L0_attn_g2_w, L0_attn_g2_b, L0_attn_value_bias, L0_attn_log_temp, L0_attn_floor_logit, L0_attn_onorm_w, L0_attn_o_w, L0_xattn_Wq, L0_xattn_bq, L0_xattn_Wk, L0_xattn_bk, L0_xattn_Wv, L0_xattn_bv, L0_xattn_Wo, L0_xattn_bo, L0_ffn_w_gate, L0_ffn_w_up, L0_ffn_w_down):
    import jax
    import jax.numpy as jnp

    def _L0_attn_ref(hidden_states, q_w, k_w, v_w, b_w, convq_w, convk_w, convv_w, fir_s, fir_l, fir_wd, g1_w, g1_b, g2_w, g2_b, value_bias, log_temp, floor_logit, onorm_w, o_w):
        import jax, jax.numpy as jnp
        import numpy as np
        from jax.scipy.linalg import solve_triangular
        B, L, HID, H = (2, 512, 256, 4)
        DK, DV = (HID // H, HID // H)
        CHUNK = 32
        CONV_K, FIR_SK, FIR_LK, FIR_WK = (4, 3, 31, 64)
        GIN = HID + 15 * H
        GH = 2 * HID
        FLOOR_INIT = float(np.log(0.05 / 0.95))

        def _l2norm(x):
            return x / jnp.sqrt(jnp.sum(x * x, -1, keepdims=True) + 1e-06)

        def _dwconv_causal(x_blc, w_ck):
            K = w_ck.shape[-1]
            x = jnp.moveaxis(x_blc, 1, 2)
            x = jnp.pad(x, ((0, 0), (0, 0), (K - 1, 0)))
            y = jax.lax.conv_general_dilated(x, w_ck[:, None, :], (1,), 'VALID', feature_group_count=w_ck.shape[0], dimension_numbers=('NCH', 'OIH', 'NCH'))
            return jnp.moveaxis(y, 2, 1)

        def _delta_rule(q, k, v, beta):
            b, h, Ll, dk = q.shape
            dv = v.shape[-1]
            n = Ll // CHUNK
            q = _l2norm(q)
            k = _l2norm(k)
            v = v * beta[..., None]
            kb = k * beta[..., None]
            rs = lambda t: t.reshape(b, h, n, CHUNK, t.shape[-1])
            q, k, v, kb = (rs(q), rs(k), rs(v), rs(kb))
            tril_strict = jnp.tril(jnp.ones((CHUNK, CHUNK), bool), -1)
            tril = jnp.tril(jnp.ones((CHUNK, CHUNK), bool), 0)
            A = jnp.where(tril_strict, kb @ jnp.swapaxes(k, -1, -2), 0.0)
            eye = jnp.eye(CHUNK, dtype=q.dtype)
            inv = solve_triangular(eye + A, jnp.broadcast_to(eye, A.shape), lower=True)
            u = inv @ v
            w = inv @ kb
            qs, ks, us, ws = (jnp.moveaxis(t, 2, 0) for t in (q, k, u, w))
            S0 = jnp.zeros((b, h, dk, dv), q.dtype)

            def step(S, xs):
                q_i, k_i, u_i, w_i = xs
                attn = jnp.where(tril, q_i @ jnp.swapaxes(k_i, -1, -2), 0.0)
                u_adj = u_i - w_i @ S
                o_i = q_i @ S + attn @ u_adj
                S = S + jnp.swapaxes(k_i, -1, -2) @ u_adj
                return (S, o_i)
            S, o = jax.lax.scan(step, S0, (qs, ks, us, ws))
            o = jnp.moveaxis(o, 0, 2).reshape(b, h, Ll, dv)
            return (o, S)

        def _stats(x):
            mean = x.mean(-1)
            rms = jnp.sqrt(jnp.clip(jnp.mean(x * x, -1), 1e-08))
            mx = jnp.abs(x).max(-1)
            return jnp.concatenate([mean, rms, mx], -1)

        def _forward(hidden_states, q_w, k_w, v_w, b_w, convq_w, convk_w, convv_w, fir_s, fir_l, fir_wd, g1_w, g1_b, g2_w, g2_b, value_bias, log_temp, floor_logit, onorm_w, o_w):
            b, Ll, _ = hidden_states.shape
            q = jax.nn.silu(_dwconv_causal(hidden_states @ q_w.T, convq_w))
            k = jax.nn.silu(_dwconv_causal(hidden_states @ k_w.T, convk_w))
            v = jax.nn.silu(_dwconv_causal(hidden_states @ v_w.T, convv_w))
            tohd = lambda t: t.reshape(b, Ll, H, -1)
            q, k, v = (tohd(q), tohd(k), tohd(v))
            beta = jax.nn.sigmoid(hidden_states @ b_w.T)
            tr = lambda t: jnp.moveaxis(t, 1, 2)
            delta_out, _S = _delta_rule(tr(q), tr(k), tr(v), jnp.moveaxis(beta, 1, 2))
            delta_out = jnp.moveaxis(delta_out, 1, 2)

            def fir(x, filt):
                y = _dwconv_causal(x.reshape(b, Ll, H * DV), filt.reshape(H * DV, -1))
                return y.reshape(b, Ll, H, DV)
            short, long_, wide = (fir(v, fir_s), fir(v, fir_l), fir(v, fir_wd))
            gate_in = jnp.concatenate([hidden_states, _stats(short), _stats(long_), _stats(wide), _stats(delta_out), _stats(v)], -1)
            hdn = jax.nn.gelu(gate_in @ g1_w.T + g1_b, approximate=False)
            logits = (hdn @ g2_w.T + g2_b).reshape(b, Ll, H, 5)
            logits = logits.at[..., 4].add(value_bias)
            logits = logits / jnp.exp(log_temp)[None, None, :, None]
            p = jax.nn.softmax(logits, -1)
            f = jax.nn.sigmoid(floor_logit)[None, None, :, None]
            scale = 1.0 - 4.0 * f
            w_ctx = f + scale * p[..., :4]
            w_val = scale * p[..., 4:5]
            o = w_ctx[..., 0:1] * short + w_ctx[..., 1:2] * long_ + w_ctx[..., 2:3] * wide + w_ctx[..., 3:4] * delta_out + w_val * v
            o = o * jax.lax.rsqrt(jnp.mean(o * o, -1, keepdims=True) + 1e-05) * onorm_w
            return o.reshape(b, Ll, HID) @ o_w.T
        return _forward(hidden_states, q_w, k_w, v_w, b_w, convq_w, convk_w, convv_w, fir_s, fir_l, fir_wd, g1_w, g1_b, g2_w, g2_b, value_bias, log_temp, floor_logit, onorm_w, o_w)

    def _L0_xattn_ref(queries, keys, values, Wq, bq, Wk, bk, Wv, bv, Wo, bo):
        import math
        import jax, jax.numpy as jnp
        import numpy as np
        D_MODEL = 256
        N_HEADS = 16
        D_K = D_MODEL // N_HEADS

        def _autocorr_forward(queries, keys, values, Wq, bq, Wk, bk, Wv, bv, Wo, bo):
            B, L, D = queries.shape
            H, dk = (N_HEADS, D_K)
            q = (queries @ Wq.T + bq).reshape(B, L, H, dk)
            k = (keys @ Wk.T + bk).reshape(B, L, H, dk)
            v = (values @ Wv.T + bv).reshape(B, L, H, dk)
            qf = jnp.fft.rfft(q, axis=1)
            kf = jnp.fft.rfft(k, axis=1)
            corr = jnp.fft.irfft(qf * jnp.conj(kf), n=L, axis=1).mean(axis=-1)
            corr = corr.transpose(0, 2, 1)
            topk = min(max(1, int(math.log(L))), L)
            weights, delays = jax.lax.top_k(corr, topk)
            w = jax.nn.softmax(weights, axis=-1)
            idx = (jnp.arange(L)[None, None, None, :] - delays[..., None]) % L
            v_h = v.transpose(0, 2, 1, 3)
            gathered = jnp.take_along_axis(v_h[:, :, None], idx[..., None], axis=3)
            out = (w[..., None, None] * gathered).sum(axis=2)
            out = out.transpose(0, 2, 1, 3).reshape(B, L, D)
            return out @ Wo.T + bo
        return _autocorr_forward(queries, keys, values, Wq, bq, Wk, bk, Wv, bv, Wo, bo)

    def _L0_ffn_ref(x, w_gate, w_up, w_down):
        import jax, jax.numpy as jnp
        import numpy as np
        DIM = 256
        HIDDEN = 768
        SCALE = 1.0 / 127.0

        def _dequant(w_int, dtype):
            return w_int.astype(dtype) * jnp.asarray(SCALE, dtype)
        wg = _dequant(w_gate, x.dtype)
        wu = _dequant(w_up, x.dtype)
        wd = _dequant(w_down, x.dtype)
        gate = jnp.einsum('bsd,hd->bsh', x, wg)
        up = jnp.einsum('bsd,hd->bsh', x, wu)
        h = jax.nn.silu(gate) * up
        return jnp.einsum('bsh,dh->bsd', h, wd)
    x = _layernorm(x + _L0_attn_ref(x, L0_attn_q_w, L0_attn_k_w, L0_attn_v_w, L0_attn_b_w, L0_attn_convq_w, L0_attn_convk_w, L0_attn_convv_w, L0_attn_fir_s, L0_attn_fir_l, L0_attn_fir_wd, L0_attn_g1_w, L0_attn_g1_b, L0_attn_g2_w, L0_attn_g2_b, L0_attn_value_bias, L0_attn_log_temp, L0_attn_floor_logit, L0_attn_onorm_w, L0_attn_o_w), axis=-1)
    x = _layernorm(x + _L0_xattn_ref(x, ctx_1024, ctx_1024, L0_xattn_Wq, L0_xattn_bq, L0_xattn_Wk, L0_xattn_bk, L0_xattn_Wv, L0_xattn_bv, L0_xattn_Wo, L0_xattn_bo), axis=-1)
    x = _layernorm(x + _L0_ffn_ref(x, L0_ffn_w_gate, L0_ffn_w_up, L0_ffn_w_down), axis=-1)
    return x

_drawn_inputs = setup_inputs


def setup_inputs(seed=0):
    import zlib

    import numpy as np

    out = dict(_drawn_inputs(seed))
    spreads = {'L0_attn_g1_b': (0.0, 0.8),
     'L0_attn_value_bias': (4.0, 0.6),
     'L0_attn_log_temp': (0.0, 2.0),
     'L0_attn_floor_logit': (-2.944438934326172, 0.6),
     'L0_attn_onorm_w': (1.0, 0.2),
     'L0_xattn_bq': (0.0, 2.0),
     'L0_xattn_bk': (0.0, 2.0),
     'L0_xattn_bv': (0.0, 0.1),
     'L0_xattn_bo': (0.0, 0.1)}
    factors = {'L0_attn_q_w': 2.785,
     'L0_attn_k_w': 2.864,
     'L0_attn_b_w': 8.0,
     'L0_attn_convq_w': 3.022,
     'L0_attn_convk_w': 2.803,
     'L0_attn_g1_w': 8.0,
     'L0_attn_g2_w': 8.0}
    for name, (base, spread) in spreads.items():
        noise = np.random.default_rng([zlib.crc32(name.encode()), seed]).standard_normal(out[name].shape)
        drawn = base * np.exp(spread * noise) if base else spread * noise
        out[name] = jnp.asarray(drawn.astype(out[name].dtype))
    for name, factor in factors.items():
        out[name] = (out[name] * factor).astype(out[name].dtype)
    return out
```

```python
from contextlib import ExitStack

import numpy as np

import concourse.bass as bass
from concourse import mybir

F32 = mybir.dt.float32
I32 = mybir.dt.int32
ALU = mybir.AluOpType
ACT = mybir.ActivationFunctionType
AX = mybir.AxisListType

P = 128
B, L, D = 4, 512, 256
H, DK = 4, 64
KT = D // P
TT = L // P
BT = B * TT
NJ = L // DK
CONV_K, FIR_S, FIR_L, FIR_W = 4, 3, 31, 64
LEVELS = 7
GH = 2 * D
NG = 5
HID = 768
MF = HID // P
XH, XD = 16, 16
TOPK = 6
PIECE = 16
NPIECE = D // PIECE
HALF = L // 2
BIG = 3.0e38


def shape_constants():
    i = np.arange(P)
    c = {}
    c["ident"] = np.eye(P)
    c["mask_lower"] = (i[:, None] > i[None, :])
    c["mask_upper"] = (i[None, :] >= i[:, None])
    c["level0"] = -((i[:, None] % 2 == 1) & (i[None, :] == i[:, None] - 1)).astype(float)
    c["blocks"] = (i[:, None] // DK == i[None, :] // DK)
    lev = np.zeros((P, LEVELS - 1, P // 2))
    for k in range(1, LEVELS):
        even = i[(i >> k) % 2 == 0]
        lev[:, k - 1, :] = ((i[:, None] >> k) % 2 == 1) & ((i[:, None] >> (k + 1)) == (even[None, :] >> (k + 1)))
    c["levels"] = lev.reshape(P, -1)
    c["heads"] = (i[:, None] // DK == np.arange(2)[None, :])
    back = DK - 1 - i % DK
    c["fold"] = (back[:, None] == np.arange(DK)[None, :])
    c["fold_even"] = (back[:, None] == i[None, :])
    c["fold_odd"] = (back[:, None] + DK == i[None, :])
    c["twice_even"] = (i[:, None] == back[None, :])
    c["twice_odd"] = (i[:, None] == back[None, :] + DK)
    t = np.arange(HALF)
    f = np.arange(P)
    dft, inv = np.zeros((HALF, 4, P)), np.zeros((P, 4, HALF))
    for par in range(2):
        w = 2 * np.pi * ((2 * f + par)[None, :] * t[:, None] % L) / L
        dft[:, 2 * par], dft[:, 2 * par + 1] = np.cos(w), -np.sin(w)
        inv[:, 2 * par], inv[:, 2 * par + 1] = 2 * np.cos(w).T / L, -2 * np.sin(w).T / L
    dft[:, 1, 0] = (-1.0) ** t
    inv[0, 0], inv[0, 1] = 1.0 / L, (-1.0) ** t / L
    c["dft"] = dft.reshape(2, P, 4 * P).transpose(1, 0, 2).reshape(P, -1)
    c["idft"] = inv.reshape(P, -1)
    z = np.ones((P, 2, XH)); z[0, 0] = 0.0
    c["not_dc"] = z.reshape(P, -1)
    c["is_dc"] = (1.0 - z).reshape(P, -1)
    row = np.zeros((P, P)); row[0, 0] = L
    c["dc_row"] = row
    return {n: np.ascontiguousarray(a.astype(np.float32).reshape(P, -1)) for n, a in c.items()}


class Signal:

    def __init__(self, sem, per_round, base=0):
        self.sem, self.n, self.base = sem, per_round, base

    def at(self, rnd, k):
        return rnd * self.n + (self.base + k)


def carve(arena, sizes, at=0):
    out = {}
    for name, shape in sizes.items():
        n = int(np.prod(shape))
        v = arena[:, at:at + n]
        if len(shape) == 2:
            v = v.rearrange("p (a b) -> p a b", a=shape[0])
        elif len(shape) == 3:
            v = v.rearrange("p (a b c) -> p a b c", a=shape[0], b=shape[1])
        elif len(shape) == 4:
            v = v.rearrange("p (a b c d) -> p a b c d", a=shape[0], b=shape[1], c=shape[2])
        out[name] = v
        at += n
    assert at <= arena.shape[1], (at, arena.shape)
    return out


def over_last(ap, n):
    return ap.unsqueeze(len(ap.shape)).broadcast_to(list(ap.shape) + [n])


def over_tiles(ap, n):
    return ap.unsqueeze(1).broadcast_to([ap.shape[0], n] + list(ap.shape[1:]))


def layer_norm(dve, scratch, b, x, buf, sig, summed, dst, done):
    v = dve
    for t in range(TT):
        dve.wait_ge(sig[summed].sem, sig[summed].at(b, t // 2 + 1))
        v.bn_stats(buf["ln"][:, t, :], x[:, t, :]).then_inc(sig["ln_st"].sem, 1)
    dve.wait_ge(sig["ln_st"].sem, sig["ln_st"].at(b, TT))
    v.memset(scratch, 0.0)
    for t in range(TT):
        v.bn_aggr(buf["mv"][:, t, :], buf["ln"][:, t, :]).then_inc(sig["ln_st"].sem, 1)
    dve.wait_ge(sig["ln_st"].sem, sig["ln_st"].at(b, 2 * TT))
    v.tensor_scalar(buf["ve"], buf["mv"][:, :, 1], 1e-5, None, ALU.add).then_inc(sig["ln_st"].sem, 1)
    dve.wait_ge(sig["ln_rs"].sem, sig["ln_rs"].at(b, 1))
    for t in range(TT):
        v.tensor_scalar(dst(t), x[:, t, :], buf["mv"][:, t, 0:1], buf["rs"][:, t:t + 1], ALU.subtract,
                        ALU.mult).then_inc(sig[done].sem, 1)


def layer(nc, dr, out):
    ctx = ExitStack()
    with ctx:
        def sb(name, shape, dt=F32):
            return ctx.enter_context(nc.sbuf_tensor(name, shape, dt))

        def signals(stage, names, from_one):
            return {n: Signal(ctx.enter_context(nc.semaphore(f"{n}_{stage}")), k, int(n in from_one))
                    for n, k in names.items()}

        bank = [ctx.enter_context(nc.psum_tensor(f"bank{i}", [P, 512], F32)) for i in range(8)]

        v_win = sb("v_win", [P, B * NJ, D])
        short = sb("short", [P, BT, D])
        delta = sb("delta", [P, BT, D])
        arena = sb("arena", [P, 22800])
        v_tiles = v_win[:, :, :].rearrange("p (t two) c -> p t two c", two=2)

        const_shapes = {n: a.shape[1] for n, a in shape_constants().items()}
        const = {n: sb("c_" + n, [P, w]) for n, w in const_shapes.items()}
        ident = const["ident"]
        levels = const["levels"][:, :].rearrange("p (k c) -> p k c", k=LEVELS - 1)
        dft = const["dft"][:, :].rearrange("p (k f) -> p k f", k=2)
        idft = const["idft"][:, :].rearrange("p (k t) -> p k t", k=4)
        not_dc = const["not_dc"][:, :].rearrange("p (a h) -> p a h", a=2)
        is_dc = const["is_dc"][:, :].rearrange("p (a h) -> p a h", a=2)

        qkv_w = sb("qkv_w", [P, KT, 3 * D])
        beta_w = sb("beta_w", [P, KT, H])
        conv_w = sb("conv_w", [P, 6, CONV_K])
        short_w = sb("short_w", [P, KT, FIR_S])
        g1x_w = sb("g1x_w", [P, KT, GH])
        g1s_w = sb("g1s_w", [P, GH])
        g1_bias = sb("g1_bias", [P, GH // P])
        g2_w = sb("g2_w", [P, GH // P, NG * H])
        onorm = sb("onorm", [P, 1])
        ow_w = sb("ow_w", [P, KT, D])
        xq_w = sb("xq_w", [P, KT, D])
        xkv_w = sb("xkv_w", [P, KT, 2 * D])
        xo_w = sb("xo_w", [P, KT, D])
        xq_b = sb("xq_b", [1, D])
        xkv_b = sb("xkv_b", [1, 2 * D])
        xo_b = sb("xo_b", [P, D])
        g2_bias = sb("g2_bias", [P, NG * H])
        gate_par = sb("gate_par", [P, 3, H])
        inv_temp = sb("inv_temp", [P, H])
        inv_temp5 = sb("inv_temp5", [P, H, NG])
        floor = sb("floor", [P, H])
        keep = sb("keep", [P, H])
        half_exp = sb("half_exp", [P, 2, 16])

        loaded = Signal(ctx.enter_context(nc.semaphore("loaded")), 0)
        ready = Signal(ctx.enter_context(nc.semaphore("ready")), 0)
        scratch = sb("scratch", [P, 1])[:]
        n_loads = [0]

        A1 = carve(arena, {
            "xT": (KT, L), "acc": (2, L), "qT": (KT, L), "kT": (KT, L), "vT": (KT, DK + L), "sq": (4, L),
            "sh": (KT, L), "k_tok": (TT, D), "v_sc": (TT, D), "AL": (TT, H, P), "ALT": (TT, H, P),
            "atT": (TT, H, P), "X": (TT, H, P), "XT": (TT, H, P), "Z": (TT, H, P // 2), "R": (D,), "U": (D,),
            "S": (2, KT, P), "ss": (32,), "rn": (2, TT, H), "rec": (16,), "th": (16,), "C": (TT, H)})
        free_1 = ("beta_mm", "beta_th", "conv", "o_out", "s_out", "silu", "ss_eps", "u_out")
        s1 = signals(1, {
            "xT_in": 16, "proj": 6, "tap_last": 6, "conv": 18, "silu": 6, "squares": 4, "beta_mm": 1, "ssq_mm": 1,
            "v_turned": 4, "k_turned": 2, "sh_turned": 2, "v_out": 4, "k_out": 2, "sh_out": 2, "sh_conv": 6,
            "beta_th": 1, "ss_eps": 1, "norms": 1, "c_steps": 3, "gram": 4, "a_scaled": 16, "attn_mm": 4,
            "attn_out": 8, "v_scaled": 1, "x_first": 8, "a_turned": 4, "at_out": 4, "z_mm": 24, "z_out": 24,
            "w_mm": 24, "x_out": 24, "x_turned": 28, "xt_out": 24, "xt_last": 4, "ks_mm": 3, "r_out": 3,
            "u_mm": 4, "u_out": 4, "s_mm": 3, "s_out": 3, "o_mm": 4, "o_out": 4, "pads": 0}, free_1)

        def evens(ap, k):
            return ap.rearrange("p h (g two s) -> p (h g) two s", two=2, s=1 << k)[:, :, 0, :]

        with nc.Block() as block:
            @block.sync
            def _(sp):
                for n in free_1:
                    sp.sem_inc(s1[n].sem, 1)
                def load(dst, src):
                    sp.dma_start(dst, src).then_inc(loaded.sem, 16)
                    n_loads[0] += 1

                load(qkv_w[:], dr["qkv_wT"].rearrange("(k p) n -> p k n", p=P))
                load(beta_w[:], dr["b_wT"].rearrange("(k p) n -> p k n", p=P))
                load(conv_w[:], dr["conv_w"].rearrange("(m p) j -> p m j", p=P))
                load(short_w[:], dr["fir_s"].rearrange("(k p) j -> p k j", p=P))
                for n in const:
                    load(const[n][:], dr["c_" + n])
                load(g1x_w[:], dr["g1x_wT"].rearrange("(k p) n -> p k n", p=P))
                sp.wait_ge(s1["pads"].sem, 5)
                load(g1s_w[0:36, :], dr["g1s_wT"][0:36, :])
                load(g1s_w[64:88, :], dr["g1s_wT"][36:60, :])
                load(g1_bias[:], dr["g1_b"])
                load(g2_w[:], dr["g2_wT"].rearrange("(k p) n -> p k n", p=P))
                load(onorm[0:DK, :], dr["onorm"].rearrange("(p a) -> p a", a=1))
                load(onorm[DK:P, :], dr["onorm"].rearrange("(p a) -> p a", a=1))
                load(ow_w[:], dr["o_wT"].rearrange("(k p) n -> p k n", p=P))
                load(xq_w[:], dr["xq_wT"].rearrange("(k p) n -> p k n", p=P))
                load(xkv_w[:], dr["xkv_wT"].rearrange("(k p) n -> p k n", p=P))
                load(xo_w[:], dr["xo_wT"].rearrange("(k p) n -> p k n", p=P))
                load(xq_b[:], dr["xq_b"].rearrange("(a n) -> a n", a=1))
                load(xkv_b[:], dr["xkv_b"].rearrange("(a n) -> a n", a=1))
                load(xo_b[:], dr["xo_b"].partition_broadcast(P))
                load(g2_bias[:], dr["g2_b"].partition_broadcast(P))
                load(gate_par[:, :, :].rearrange("p a h -> p (a h)"), dr["gate_par"].partition_broadcast(P))
                with sp.Fori(0, B) as b:
                    sp.wait_ge(s1["beta_mm"].sem, s1["beta_mm"].at(b, 0))
                    sp.dma_start(A1["xT"], dr["xT"][b].rearrange("(k p) t -> p k t", p=P)).then_inc(s1["xT_in"].sem, 16)

            @block.tensor
            def _(pe):
                mm = nc.tensor.matmul
                pe.wait_ge(loaded.sem, 16 * n_loads[0])
                pe.wait_ge(s1["pads"].sem, 5)
                with pe.Fori(0, B) as b:
                    pe.wait_ge(s1["xT_in"].sem, s1["xT_in"].at(b, 16))
                    for m in range(6):
                        pe.wait_ge(s1["conv"].sem, s1["conv"].at(b, 3 * (m - 2) if m >= 3 else 0))
                        for k in range(KT):
                            i = mm(bank[m % 3][:], qkv_w[:, k, m * P:(m + 1) * P], A1["xT"][:, k, :],
                                   start=(k == 0), stop=(k == KT - 1))
                        i.then_inc(s1["proj"].sem, 1)
                    pe.wait_ge(s1["ss_eps"].sem, s1["ss_eps"].at(b, 0))
                    pe.wait_ge(s1["beta_th"].sem, s1["beta_th"].at(b, 0))
                    for t in range(TT):
                        for k in range(KT):
                            i = mm(bank[3][:, t * H:(t + 1) * H], A1["xT"][:, k, t * P:(t + 1) * P], beta_w[:, k, :],
                                   start=(k == 0), stop=(k == KT - 1))
                    i.then_inc(s1["beta_mm"].sem, 1)
                    pe.wait_ge(s1["squares"].sem, s1["squares"].at(b, 4))
                    pe.wait_ge(s1["beta_th"].sem, s1["beta_th"].at(b, 1))
                    for m in range(4):
                        for t in range(TT):
                            c = 16 + 16 * (m // 2) + t * H + 2 * (m % 2)
                            i = mm(bank[3][:, c:c + 2], A1["sq"][:, m, t * P:(t + 1) * P], const["heads"][:],
                                   start=True, stop=True)
                    i.then_inc(s1["ssq_mm"].sem, 1)
                    pe.wait_ge(s1["silu"].sem, s1["silu"].at(b, 6))
                    pe.wait_ge(s1["o_out"].sem, s1["o_out"].at(b, 0))
                    pe.wait_ge(s1["u_out"].sem, s1["u_out"].at(b, 0))
                    pe.wait_ge(s1["s_out"].sem, s1["s_out"].at(b, 0))
                    for i2 in range(2):
                        for t in range(2):
                            for k in range(KT):
                                i = nc.tensor.transpose(bank[4 + i2][:, t * D + k * P:t * D + (k + 1) * P],
                                                        A1["kT"][:, k, (2 * i2 + t) * P:(2 * i2 + t + 1) * P], ident[:])
                        i.then_inc(s1["k_turned"].sem, 1)
                    for w in range(4):
                        if w >= 2:
                            pe.wait_ge(s1["k_out"].sem, s1["k_out"].at(b, w - 1))
                        for j in range(2):
                            for k in range(KT):
                                c = (2 * w + j) * DK
                                i = nc.tensor.transpose(bank[4 + (w + 2) % 4][:, j * D + k * P:j * D + (k + 1) * P],
                                                        A1["vT"][:, k, c:c + P], ident[:])
                        i.then_inc(s1["v_turned"].sem, 1)
                    for t in range(TT):
                        if t == 0:
                            pe.wait_ge(s1["v_out"].sem, s1["v_out"].at(b, 4))
                        else:
                            pe.wait_ge(s1["a_scaled"].sem, s1["a_scaled"].at(b, H * t))
                        for h in range(H):
                            r, k = DK * (h % 2), h // 2
                            kk = A1["kT"][r:r + DK, k, t * P:(t + 1) * P]
                            i = mm(bank[4 + h % 2][:, k * P:(k + 1) * P], kk, kk, start=True, stop=True)
                        i.then_inc(s1["gram"].sem, 1)
                        pe.wait_ge(s1["conv"].sem, s1["conv"].at(b, 18))
                        if t:
                            pe.wait_ge(s1["attn_out"].sem, s1["attn_out"].at(b, 2 * t))
                        for h in range(H):
                            r, k = DK * (h % 2), h // 2
                            i = mm(bank[h % 2][:, k * P:(k + 1) * P], A1["kT"][r:r + DK, k, t * P:(t + 1) * P],
                                   A1["qT"][r:r + DK, k, t * P:(t + 1) * P], start=True, stop=True)
                        i.then_inc(s1["attn_mm"].sem, 1)
                    pe.wait_ge(s1["sh_conv"].sem, s1["sh_conv"].at(b, 6))
                    for i2 in range(2):
                        pe.wait_ge(s1["v_out"].sem, s1["v_out"].at(b, i2 + 1))
                        for t in range(2):
                            for k in range(KT):
                                i = nc.tensor.transpose(bank[6 + i2][:, t * D + k * P:t * D + (k + 1) * P],
                                                        A1["sh"][:, k, (2 * i2 + t) * P:(2 * i2 + t + 1) * P], ident[:])
                        i.then_inc(s1["sh_turned"].sem, 1)
                    for t in range(TT):
                        pe.wait_ge(s1["a_scaled"].sem, s1["a_scaled"].at(b, H * (t + 1)))
                        if t < 2:
                            pe.wait_ge(s1["sh_out"].sem, s1["sh_out"].at(b, t + 1))
                        else:
                            pe.wait_ge(s1["at_out"].sem, s1["at_out"].at(b, t - 1))
                        for h in range(H):
                            i = nc.tensor.transpose(bank[6 + t % 2][:, h * P:(h + 1) * P], A1["AL"][:, t, h, :], ident[:])
                        i.then_inc(s1["a_turned"].sem, 1)

                    def turn_x(k, t):
                        n = TT * k + t
                        if k == 0:
                            pe.wait_ge(s1["x_first"].sem, s1["x_first"].at(b, 2 * t + 2))
                        else:
                            pe.wait_ge(s1["x_out"].sem, s1["x_out"].at(b, n - TT + 1))
                        if n < 2:
                            pe.wait_ge(s1["at_out"].sem, s1["at_out"].at(b, n + 3))
                        elif n - 2 < TT * (LEVELS - 1):
                            pe.wait_ge(s1["xt_out"].sem, s1["xt_out"].at(b, n - 1))
                        else:
                            pe.wait_ge(s1["xt_last"].sem, s1["xt_last"].at(b, n - 1 - TT * (LEVELS - 1)))
                        for h in range(H):
                            i = nc.tensor.transpose(bank[6 + t % 2][:, h * P:(h + 1) * P], A1["X"][:, t, h, :], ident[:])
                        i.then_inc(s1["x_turned"].sem, 1)

                    for t in range(TT):
                        turn_x(0, t)
                    for k in range(1, LEVELS):
                        for t in range(TT):
                            n = TT * (k - 1) + t
                            pe.wait_ge(s1["xt_out"].sem, s1["xt_out"].at(b, n + 1))
                            if n >= 2:
                                pe.wait_ge(s1["z_out"].sem, s1["z_out"].at(b, n - 1))
                            else:
                                pe.wait_ge(s1["attn_out"].sem, s1["attn_out"].at(b, 2 * TT))
                            for h in range(H):
                                i = mm(bank[t % 2][:, h * DK:(h + 1) * DK], A1["ALT"][:, t, h, :],
                                       A1["X"][:, t, h, :].rearrange("p (g two s) -> p g two s", two=2, s=1 << k)[:, :, 0, :],
                                       start=True, stop=True)
                            i.then_inc(s1["z_mm"].sem, 1)
                        for t in range(TT):
                            n = TT * (k - 1) + t
                            pe.wait_ge(s1["z_out"].sem, s1["z_out"].at(b, n + 1))
                            if n >= 2:
                                pe.wait_ge(s1["x_out"].sem, s1["x_out"].at(b, n - 1))
                            else:
                                pe.wait_ge(s1["a_scaled"].sem, s1["a_scaled"].at(b, TT * H))
                            for h in range(H):
                                i = mm(bank[4 + t % 2][:, h * DK:(h + 1) * DK], A1["XT"][:, t, h, :], A1["Z"][:, t, h, :],
                                       start=True, stop=True)
                            i.then_inc(s1["w_mm"].sem, 1)
                        for t in range(TT):
                            turn_x(k, t)
                    for t in range(TT):
                        tok = slice(t * P, (t + 1) * P)
                        if t:
                            pe.wait_ge(s1["s_out"].sem, s1["s_out"].at(b, t))
                            if t > 1:
                                pe.wait_ge(s1["r_out"].sem, s1["r_out"].at(b, t - 1))
                            for p in range(KT):
                                i = mm(bank[2][:, p * P:(p + 1) * P], A1["kT"][:, p, tok], A1["S"][:, t % 2, p, :],
                                       start=True, stop=True)
                            i.then_inc(s1["ks_mm"].sem, 1)
                            pe.wait_ge(s1["r_out"].sem, s1["r_out"].at(b, t))
                            pe.wait_ge(s1["u_out"].sem, s1["u_out"].at(b, t))
                        else:
                            pe.wait_ge(s1["v_scaled"].sem, s1["v_scaled"].at(b, 1))
                            pe.wait_ge(s1["x_out"].sem, s1["x_out"].at(b, 24))
                        pe.wait_ge(s1["xt_last"].sem, s1["xt_last"].at(b, t + 1))
                        rhs = A1["R"] if t else A1["v_sc"][:, 0, :]
                        for h in range(H):
                            i = mm(bank[4][:, h * DK:(h + 1) * DK], A1["XT"][:, t, h, :], rhs[:, h * DK:(h + 1) * DK],
                                   start=True, stop=True)
                        i.then_inc(s1["u_mm"].sem, 1)
                        pe.wait_ge(s1["u_out"].sem, s1["u_out"].at(b, t + 1))
                        if t < TT - 1:
                            for p in range(KT):
                                i = mm(bank[5][:, p * P:(p + 1) * P], A1["k_tok"][:, t, p * P:(p + 1) * P],
                                       A1["U"][:, p * P:(p + 1) * P], start=(t == 0 and p == 0),
                                       stop=(t == TT - 2 and p == KT - 1), skip_group_check=True)
                            i.then_inc(s1["s_mm"].sem, 1)
                        if t >= 2:
                            pe.wait_ge(s1["o_out"].sem, s1["o_out"].at(b, t - 1))
                        else:
                            pe.wait_ge(s1["xt_last"].sem, s1["xt_last"].at(b, TT))
                        if t:
                            for p in range(KT):
                                mm(bank[6 + t % 2][:, p * P:(p + 1) * P], A1["qT"][:, p, tok], A1["S"][:, t % 2, p, :],
                                   start=(p == 0), stop=False, skip_group_check=True)
                        for h in range(H):
                            i = mm(bank[6 + t % 2][:, h * DK:(h + 1) * DK], A1["atT"][:, t, h, :],
                                   A1["U"][:, h * DK:(h + 1) * DK], start=(t == 0 and h == 0), stop=(h == H - 1),
                                   skip_group_check=True)
                        i.then_inc(s1["o_mm"].sem, 1)

            @block.scalar
            def _(act):
                a = nc.scalar.activation
                act.wait_ge(loaded.sem, 16 * n_loads[0])
                act.wait_ge(s1["pads"].sem, 5)
                a(inv_temp[:], gate_par[:, 1, :], ACT.Exp, scale=-1.0).then_inc(ready.sem, 1)
                a(floor[:], gate_par[:, 2, :], ACT.Tanh, scale=0.5).then_inc(ready.sem, 1)
                with act.Fori(0, B) as b:
                    def silu(m):
                        act.wait_ge(s1["conv"].sem, s1["conv"].at(b, 3 * m + 3))
                        dst = [A1["qT"], A1["kT"]][m // 2][:, m % 2, :] if m < 4 else A1["vT"][:, m - 4, DK:]
                        a(dst, A1["acc"][:, m % 2, :], ACT.Silu).then_inc(s1["silu"].sem, 1)

                    for m in range(6):
                        act.wait_ge(s1["proj"].sem, s1["proj"].at(b, m + 1))
                        act.wait_ge(s1["silu"].sem, s1["silu"].at(b, m - 1 if m >= 2 else 0))
                        a(A1["acc"][:, m % 2, :], bank[m % 3][:], ACT.Copy,
                          scale=conv_w[:, m, CONV_K - 1:CONV_K]).then_inc(s1["tap_last"].sem, 1)
                        if m:
                            silu(m - 1)
                    silu(5)
                    act.wait_ge(s1["beta_mm"].sem, s1["beta_mm"].at(b, 1))
                    a(A1["th"], bank[3][:, 0:16], ACT.Tanh, scale=0.5).then_inc(s1["beta_th"].sem, 1)
                    for m in range(4):
                        act.wait_ge(s1["silu"].sem, s1["silu"].at(b, m + 1))
                        a(A1["sq"][:, m, :], [A1["qT"], A1["kT"]][m // 2][:, m % 2, :],
                          ACT.Square).then_inc(s1["squares"].sem, 1)
                    for i2 in range(2):
                        act.wait_ge(s1["k_turned"].sem, s1["k_turned"].at(b, i2 + 1))
                        nc.scalar.copy(A1["k_tok"][:, 2 * i2:2 * i2 + 2, :],
                                       bank[4 + i2][:].rearrange("p (t c) -> p t c", t=2)).then_inc(s1["k_out"].sem, 1)
                    for w in range(4):
                        act.wait_ge(s1["v_turned"].sem, s1["v_turned"].at(b, w + 1))
                        nc.scalar.copy(v_win[:, bass.ds(b * NJ + 2 * w, 2), :],
                                       bank[4 + (w + 2) % 4][:].rearrange("p (t c) -> p t c", t=2))\
                            .then_inc(s1["v_out"].sem, 1)
                    for i2 in range(2):
                        act.wait_ge(s1["sh_turned"].sem, s1["sh_turned"].at(b, i2 + 1))
                        nc.scalar.copy(short[:, bass.ds(b * TT + 2 * i2, 2), :],
                                       bank[6 + i2][:].rearrange("p (t c) -> p t c", t=2)).then_inc(s1["sh_out"].sem, 1)
                    for t in range(TT):
                        act.wait_ge(s1["a_turned"].sem, s1["a_turned"].at(b, t + 1))
                        nc.scalar.copy(A1["ALT"][:, t, :, :], bank[6 + t % 2][:].rearrange("p (h c) -> p h c", h=H))\
                            .then_inc(s1["at_out"].sem, 1)
                    for n in range(TT * (LEVELS - 1)):
                        t = n % TT
                        act.wait_ge(s1["x_turned"].sem, s1["x_turned"].at(b, n + 1))
                        nc.scalar.copy(A1["XT"][:, t, :, :], bank[6 + t % 2][:].rearrange("p (h c) -> p h c", h=H))\
                            .then_inc(s1["xt_out"].sem, 1)
                    for t in range(TT):
                        act.wait_ge(s1["u_mm"].sem, s1["u_mm"].at(b, t + 1))
                        nc.scalar.copy(A1["U"], bank[4][:, 0:D]).then_inc(s1["u_out"].sem, 1)

            @block.vector
            def _(dve):
                v = nc.vector
                v.memset(g1s_w[32:64, :], 0.0).then_inc(s1["pads"].sem, 1)
                dve.wait_ge(loaded.sem, 16 * n_loads[0])
                dve.wait_ge(s1["pads"].sem, 5)
                dve.wait_ge(ready.sem, 2)
                v.tensor_copy(inv_temp5[:], over_last(inv_temp[:], NG)).then_inc(ready.sem, 1)
                v.tensor_scalar(floor[:], floor[:], 0.5, 0.5, ALU.mult, ALU.add).then_inc(ready.sem, 1)
                dve.wait_ge(ready.sem, 4)
                v.tensor_scalar(keep[:], floor[:], -4.0, 1.0, ALU.mult, ALU.add).then_inc(ready.sem, 1)
                g2b = g2_bias[:].rearrange("p (h g) -> p h g", g=NG)
                v.tensor_tensor(g2b[:, :, NG - 1], g2b[:, :, NG - 1], gate_par[:, 0, :], ALU.add).then_inc(ready.sem, 1)
                with dve.Fori(0, B) as b:
                    for m in range(6):
                        for j in range(1, CONV_K):
                            if j == 1:
                                dve.wait_ge(s1["tap_last"].sem, s1["tap_last"].at(b, m + 1))
                            else:
                                dve.wait_ge(s1["conv"].sem, s1["conv"].at(b, 3 * m + j - 1))
                            acc = A1["acc"][:, m % 2, j:L]
                            v.scalar_tensor_tensor(out=acc, in0=bank[m % 3][:, 0:L - j],
                                                   scalar=conv_w[:, m, CONV_K - 1 - j:CONV_K - j], in1=acc,
                                                   op0=ALU.mult, op1=ALU.add).then_inc(s1["conv"].sem, 1)
                    dve.wait_ge(s1["ssq_mm"].sem, s1["ssq_mm"].at(b, 1))
                    dve.wait_ge(s1["beta_th"].sem, s1["beta_th"].at(b, 1))
                    v.tensor_scalar(A1["ss"], bank[3][:, 16:48], 1e-6, None, ALU.add).then_inc(s1["ss_eps"].sem, 1)
                    v.tensor_scalar(A1["th"], A1["th"], 0.5, 0.5, ALU.mult, ALU.add).then_inc(s1["c_steps"].sem, 1)
                    dve.wait_ge(s1["ss_eps"].sem, s1["ss_eps"].at(b, 1))
                    v.reciprocal(A1["rec"], A1["ss"][:, 16:32]).then_inc(s1["c_steps"].sem, 1)
                    dve.wait_ge(s1["c_steps"].sem, s1["c_steps"].at(b, 2))
                    v.tensor_tensor(A1["C"].rearrange("p t h -> p (t h)"), A1["rec"], A1["th"],
                                    ALU.mult).then_inc(s1["c_steps"].sem, 1)
                    dve.wait_ge(s1["c_steps"].sem, s1["c_steps"].at(b, 3))
                    for t in range(TT):
                        dve.wait_ge(s1["gram"].sem, s1["gram"].at(b, t + 1))
                        for h in range(H):
                            v.scalar_tensor_tensor(out=A1["AL"][:, t, h, :], in0=bank[4 + h % 2][:, (h // 2) * P:(h // 2 + 1) * P],
                                                   scalar=A1["C"][:, t, h:h + 1], in1=const["mask_lower"][:],
                                                   op0=ALU.mult, op1=ALU.mult).then_inc(s1["a_scaled"].sem, 1)
                        dve.wait_ge(s1["attn_mm"].sem, s1["attn_mm"].at(b, t + 1))
                        for e in range(2):
                            v.tensor_tensor(A1["atT"][:, t, e::2, :], bank[e][:, 0:D].rearrange("p (h c) -> p h c", h=2),
                                            over_tiles(const["mask_upper"][:], 2), ALU.mult).then_inc(s1["attn_out"].sem, 1)
                    dve.wait_ge(s1["silu"].sem, s1["silu"].at(b, 6))
                    for k in range(KT):
                        for j in range(FIR_S):
                            src = A1["vT"][:, k, DK - j:DK - j + L]
                            w = short_w[:, k, FIR_S - 1 - j:FIR_S - j]
                            if j == 0:
                                v.tensor_scalar(A1["sh"][:, k, :], src, w, None, ALU.mult).then_inc(s1["sh_conv"].sem, 1)
                                continue
                            dve.wait_ge(s1["sh_conv"].sem, s1["sh_conv"].at(b, FIR_S * k + j))
                            v.scalar_tensor_tensor(out=A1["sh"][:, k, :], in0=src, scalar=w, in1=A1["sh"][:, k, :],
                                                   op0=ALU.mult, op1=ALU.add).then_inc(s1["sh_conv"].sem, 1)
                    dve.wait_ge(s1["v_out"].sem, s1["v_out"].at(b, 4))
                    dve.wait_ge(s1["norms"].sem, s1["norms"].at(b, 1))
                    v.tensor_tensor(A1["v_sc"].rearrange("p t (h c) -> p t h c", h=H),
                                    v_tiles[:, bass.ds(b * TT, TT), 1, :].rearrange("p t (h c) -> p t h c", h=H),
                                    over_last(A1["rn"][:, 1, :, :], DK), ALU.mult).then_inc(s1["v_scaled"].sem, 1)
                    for k in range(1, LEVELS):
                        for t in range(TT):
                            n = TT * (k - 1) + t
                            dve.wait_ge(s1["z_mm"].sem, s1["z_mm"].at(b, n + 1))
                            v.tensor_tensor(A1["Z"][:, t, :, :], bank[t % 2][:, 0:D].rearrange("p (h c) -> p h c", h=H),
                                            over_tiles(levels[:, k - 1, :], H), ALU.mult).then_inc(s1["z_out"].sem, 1)
                        for t in range(TT):
                            n = TT * (k - 1) + t
                            dve.wait_ge(s1["w_mm"].sem, s1["w_mm"].at(b, n + 1))
                            x = evens(A1["X"][:, t, :, :], k)
                            v.tensor_tensor(x, x, bank[4 + t % 2][:, 0:D].rearrange("p (g s) -> p g s", s=1 << k),
                                            ALU.subtract).then_inc(s1["x_out"].sem, 1)
                    for t in range(TT):
                        dve.wait_ge(s1["x_turned"].sem, s1["x_turned"].at(b, TT * (LEVELS - 1) + t + 1))
                        v.tensor_tensor(A1["XT"][:, t, :, :], bank[6 + t % 2][:].rearrange("p (h c) -> p h c", h=H),
                                        over_last(A1["C"][:, t, :], P), ALU.mult).then_inc(s1["xt_last"].sem, 1)
                    for t in range(TT):
                        if t:
                            dve.wait_ge(s1["ks_mm"].sem, s1["ks_mm"].at(b, t))
                            v.tensor_tensor(A1["R"], A1["v_sc"][:, t, :], bank[2][:, 0:D],
                                            ALU.subtract).then_inc(s1["r_out"].sem, 1)
                        if t < TT - 1:
                            dve.wait_ge(s1["s_mm"].sem, s1["s_mm"].at(b, t + 1))
                            v.tensor_tensor(A1["S"][:, (t + 1) % 2, :, :], bank[5][:, 0:D].rearrange("p (k c) -> p k c", k=KT),
                                            over_tiles(const["blocks"][:], KT), ALU.mult).then_inc(s1["s_out"].sem, 1)
                        dve.wait_ge(s1["o_mm"].sem, s1["o_mm"].at(b, t + 1))
                        v.tensor_tensor(delta[:, b * TT + t, :].rearrange("p (h c) -> p h c", h=H),
                                        bank[6 + t % 2][:, 0:D].rearrange("p (h c) -> p h c", h=H),
                                        over_last(A1["rn"][:, 0, t, :], DK), ALU.mult).then_inc(s1["o_out"].sem, 1)

            @block.gpsimd
            def _(pool):
                g = nc.gpsimd
                g.memset(half_exp[:, 0, :], -0.5).then_inc(s1["pads"].sem, 1)
                g.memset(A1["vT"][:, 0, 0:DK], 0.0).then_inc(s1["pads"].sem, 1)
                g.memset(A1["vT"][:, 1, 0:DK], 0.0).then_inc(s1["pads"].sem, 1)
                g.memset(half_exp[:, 1, :], 0.5).then_inc(s1["pads"].sem, 1)
                pool.wait_ge(s1["pads"].sem, 5)
                pool.wait_ge(loaded.sem, 16 * n_loads[0])
                with pool.Fori(0, B) as b:
                    pool.wait_ge(s1["ss_eps"].sem, s1["ss_eps"].at(b, 1))
                    g.tensor_tensor(A1["rn"].rearrange("p a t h -> p (a t h)"), A1["ss"],
                                    half_exp[:, :, :].rearrange("p a n -> p (a n)"), ALU.pow).then_inc(s1["norms"].sem, 1)
                    for t in range(TT):
                        pool.wait_ge(s1["a_scaled"].sem, s1["a_scaled"].at(b, H * (t + 1)))
                        g.tensor_tensor(A1["X"][:, t, :, :], A1["AL"][:, t, :, :], over_tiles(const["level0"][:], H),
                                        ALU.mult).then_inc(s1["x_first"].sem, 1)
                        pool.wait_ge(s1["x_first"].sem, s1["x_first"].at(b, 2 * t + 1))
                        g.tensor_tensor(A1["X"][:, t, :, :], A1["X"][:, t, :, :], over_tiles(ident[:], H),
                                        ALU.add).then_inc(s1["x_first"].sem, 1)

        wl = arena[:, 0:B * NJ * D].rearrange("p (j c) -> p j c", c=D)
        toep = [arena[:, B * NJ * D + i * 2 * DK * PIECE:B * NJ * D + (i + 1) * 2 * DK * PIECE]
                .rearrange("p (f c) -> p f c", c=PIECE) for i in range(2)]
        free_2 = ("fir_mm", "fir_out")
        s2 = signals(2, {"toep_in0": 32, "toep_in1": 32, "fir_mm": 2, "fir_out": 2}, free_2)
        toep_in = [s2["toep_in0"], s2["toep_in1"]]
        with nc.Block() as block:
            @block.sync
            def _(sp):
                for n in free_2:
                    sp.sem_inc(s2[n].sem, 1)
                with sp.Fori(0, NPIECE // 2) as i:
                    for h in range(2):
                        sp.wait_ge(s2["fir_mm"].sem, s2["fir_mm"].at(i, h - 1 if h else 0))
                        for f in range(2):
                            src = dr[("toep_w", "toep_l")[f]][i * 2 + h]
                            src = bass.AP(src.tensor, src.offset, [[PIECE, P], [1, DK * PIECE]])
                            sp.dma_start(toep[h][:, f * DK:(f + 1) * DK, :].rearrange("p f c -> p (f c)"), src)\
                                .then_inc(toep_in[h].sem, 16)

            @block.tensor
            def _(pe):
                with pe.Fori(0, NPIECE // 2) as i:
                    for h in range(2):
                        pe.wait_ge(toep_in[h].sem, toep_in[h].at(i, 32))
                        pe.wait_ge(s2["fir_out"].sem, s2["fir_out"].at(i, h - 1 if h else 0))
                        for c in range(PIECE):
                            mm = nc.tensor.matmul(bank[h][:, c * B * NJ:(c + 1) * B * NJ], toep[h][:, :, c],
                                                  v_win[:, :, i * (2 * PIECE) + h * PIECE + c],
                                                  start=True, stop=True)
                        mm.then_inc(s2["fir_mm"].sem, 1)

            @block.vector
            def _(dve):
                with dve.Fori(0, NPIECE // 2) as i:
                    for h in range(2):
                        dve.wait_ge(s2["fir_mm"].sem, s2["fir_mm"].at(i, h + 1))
                        nc.vector.tensor_copy(wl[:, :, bass.ds(i * (2 * PIECE) + h * PIECE, PIECE)],
                                              bank[h][:].rearrange("p (c j) -> p j c", c=PIECE))\
                            .then_inc(s2["fir_out"].sem, 1)

        A3 = carve(arena, {
            "xT": (KT, L), "x": (TT, D), "st": (TT * 3, 3, H), "tw": (NJ, 3, H), "sw": (NJ, 24), "statT": (L,),
            "hdnT": (GH // P, L), "lg": (TT, H, NG), "mx": (TT, H), "w": (TT, H, NG), "wsel": (2, TT, H),
            "sqb": (2, 2048), "pwl": (TT, 2, D), "pv": (TT, D), "ps": (TT, D), "ssh": (TT * H,),
            "rh": (TT * H,), "ln": (TT, 6), "mv": (TT, 2), "ve": (TT,), "rs": (TT,)}, at=B * NJ * D)
        on, onT, xr = A3["pv"], A3["pwl"].rearrange("p t a c -> p (t a c)")[:, 0:KT * L].rearrange("p (k t) -> p k t", k=KT), A3["ps"]
        free_3 = ("hdn_mm", "lg_steps", "oT_out", "o_norm", "sq_used", "res", "w_sel")
        s3 = signals(3, {
            "x3_in": 32, "sq_out": 4, "red": 8, "sq_used": 4, "small": 4, "roots": 2, "sw_out": 2, "st_turned": 2, "st_out": 2,
            "hdn_mm": 4, "gelu": 4, "lg_mm": 1, "lg_steps": 9, "lg_exp": 1, "w_twice": 1, "w_sel": 2, "p_wl": 2,
            "p_v": 1, "p_sum": 4, "mix_mm": 2, "mix_sq": 2, "mix_ss": 3, "r_head": 1, "o_norm": 2, "o_turned": 2,
            "oT_out": 2, "y_mm": 2, "res": 2, "ln_st": 9, "ln_rs": 1, "x1_out": 4, "zeros3": 0}, free_3)

        def branch(n, b):
            if n == 0:
                src = wl[:, bass.ds(b * NJ, NJ), :]
            elif n == 3:
                src = v_tiles[:, bass.ds(b * TT, TT), 1, :]
            else:
                src = [short, delta][n - 1][:, bass.ds(b * TT, TT), :]
            return src.rearrange("p t (h c) -> p t h c", h=H)

        def stat(n, s):
            if n == 0:
                return A3["tw"][:, :, s, :]
            return A3["st"].rearrange("p (t r) s h -> p t r s h", r=3)[:, :, n - 1, s, :]

        with nc.Block() as block:
            @block.sync
            def _(sp):
                for n in free_3:
                    sp.sem_inc(s3[n].sem, 1)
                with sp.Fori(0, B) as b:
                    sp.wait_ge(s3["hdn_mm"].sem, s3["hdn_mm"].at(b, 0))
                    sp.dma_start(A3["xT"], dr["xT"][b].rearrange("(k p) t -> p k t", p=P)).then_inc(s3["x3_in"].sem, 16)
                    sp.wait_ge(s3["res"].sem, s3["res"].at(b, 0))
                    sp.dma_start(A3["x"], dr["x"][b].rearrange("(t p) d -> p t d", p=P)).then_inc(s3["x3_in"].sem, 16)

            @block.tensor
            def _(pe):
                mm = nc.tensor.matmul
                pe.wait_ge(s3["zeros3"].sem, 2)
                with pe.Fori(0, B) as b:
                    pe.wait_ge(s3["sw_out"].sem, s3["sw_out"].at(b, 2))
                    pe.wait_ge(s3["roots"].sem, s3["roots"].at(b, 2))
                    pe.wait_ge(s3["oT_out"].sem, s3["oT_out"].at(b, 0))
                    for j in range(NJ):
                        i = mm(bank[1][64:88, j * DK:(j + 1) * DK], A3["sw"][:, j, :], const["fold"][:],
                               start=True, stop=True)
                    i.then_inc(s3["st_turned"].sem, 1)
                    for t in range(TT):
                        i = nc.tensor.transpose(bank[0][0:36, t * P:(t + 1) * P],
                                                A3["st"][:, 3 * t:3 * t + 3, :, :].rearrange("p r s h -> p (r s h)"), ident[:])
                    i.then_inc(s3["st_turned"].sem, 1)
                    pe.wait_ge(s3["st_out"].sem, s3["st_out"].at(b, 2))
                    pe.wait_ge(s3["x3_in"].sem, s3["x3_in"].at(b, 32))
                    pe.wait_ge(s3["res"].sem, s3["res"].at(b, 0))
                    for m in range(GH // P):
                        if m >= 2:
                            pe.wait_ge(s3["gelu"].sem, s3["gelu"].at(b, m - 1))
                        for k in range(KT):
                            mm(bank[2 + m % 2][:], g1x_w[:, k, m * P:(m + 1) * P], A3["xT"][:, k, :],
                               start=(k == 0), stop=False)
                        mm(bank[2 + m % 2][:], g1s_w[0:88, m * P:(m + 1) * P], A3["statT"][0:88, :],
                           start=False, stop=True).then_inc(s3["hdn_mm"].sem, 1)
                    pe.wait_ge(s3["gelu"].sem, s3["gelu"].at(b, GH // P))
                    pe.wait_ge(s3["lg_steps"].sem, s3["lg_steps"].at(b, 0))
                    for t in range(TT):
                        for k in range(GH // P):
                            i = mm(bank[4][:, t * NG * H:(t + 1) * NG * H], A3["hdnT"][:, k, t * P:(t + 1) * P],
                                   g2_w[:, k, :], start=(k == 0), stop=(k == GH // P - 1))
                    i.then_inc(s3["lg_mm"].sem, 1)
                    pe.wait_ge(s3["lg_steps"].sem, s3["lg_steps"].at(b, 9))
                    pe.wait_ge(s3["w_sel"].sem, s3["w_sel"].at(b, 0))
                    wcol = A3["w"].rearrange("p t h g -> p (t h g)")
                    mm(bank[5][:, 0:80], const["twice_even"][:], wcol, start=True, stop=True)
                    mm(bank[5][:, 80:160], const["twice_odd"][:], wcol, start=True, stop=True)\
                        .then_inc(s3["w_twice"].sem, 1)
                    pe.wait_ge(s3["p_wl"].sem, s3["p_wl"].at(b, 2))
                    pe.wait_ge(s3["p_sum"].sem, s3["p_sum"].at(b, 4))
                    pe.wait_ge(s3["o_norm"].sem, s3["o_norm"].at(b, 0))
                    for t in range(TT):
                        o = bank[6 + t // 2][:, (t % 2) * D:(t % 2 + 1) * D]
                        mm(o, ident[:], A3["ps"][:, t, :], start=True, stop=False)
                        mm(o, const["fold_even"][:], A3["pwl"][:, t, 0, :], start=False, stop=False)
                        i = mm(o, const["fold_odd"][:], A3["pwl"][:, t, 1, :], start=False, stop=True)
                        if t % 2:
                            i.then_inc(s3["mix_mm"].sem, 1)
                    pe.wait_ge(s3["o_norm"].sem, s3["o_norm"].at(b, 2))
                    for k in range(KT):
                        for t in range(TT):
                            i = nc.tensor.transpose(bank[k][:, t * P:(t + 1) * P], on[:, t, k * P:(k + 1) * P], ident[:])
                        i.then_inc(s3["o_turned"].sem, 1)
                    pe.wait_ge(s3["oT_out"].sem, s3["oT_out"].at(b, 2))
                    for t in range(TT):
                        for k in range(KT):
                            i = mm(bank[2 + t // 2][:, (t % 2) * D:(t % 2 + 1) * D], onT[:, k, t * P:(t + 1) * P],
                                   ow_w[:, k, :], start=(k == 0), stop=(k == KT - 1))
                        if t % 2:
                            i.then_inc(s3["y_mm"].sem, 1)

            @block.scalar
            def _(act):
                a = nc.scalar.activation
                act.wait_ge(s3["zeros3"].sem, 2)
                with act.Fori(0, B) as b:
                    for n in range(4):
                        act.wait_ge(s3["sq_used"].sem, s3["sq_used"].at(b, n - 1 if n >= 2 else 0))
                        T = NJ if n == 0 else TT
                        a(A3["sqb"][:, n % 2, 0:T * D].rearrange("p (t h c) -> p t h c", t=T, h=H), branch(n, b),
                          ACT.Square).then_inc(s3["sq_out"].sem, 1)
                    act.wait_ge(s3["small"].sem, s3["small"].at(b, 4))
                    a(A3["tw"][:, :, 1, :], A3["tw"][:, :, 1, :], ACT.Sqrt).then_inc(s3["roots"].sem, 1)
                    a(A3["st"][:, :, 1, :], A3["st"][:, :, 1, :], ACT.Sqrt).then_inc(s3["roots"].sem, 1)
                    act.wait_ge(s3["st_turned"].sem, s3["st_turned"].at(b, 1))
                    nc.scalar.copy(A3["statT"][64:88, :], bank[1][64:88, :]).then_inc(s3["st_out"].sem, 1)
                    act.wait_ge(s3["st_turned"].sem, s3["st_turned"].at(b, 2))
                    nc.scalar.copy(A3["statT"][0:36, :], bank[0][0:36, :]).then_inc(s3["st_out"].sem, 1)
                    for m in range(GH // P):
                        act.wait_ge(s3["hdn_mm"].sem, s3["hdn_mm"].at(b, m + 1))
                        a(A3["hdnT"][:, m, :], bank[2 + m % 2][:], ACT.Gelu, bias=g1_bias[:, m:m + 1])\
                            .then_inc(s3["gelu"].sem, 1)
                    act.wait_ge(s3["lg_steps"].sem, s3["lg_steps"].at(b, 4))
                    a(A3["lg"], A3["lg"], ACT.Exp).then_inc(s3["lg_exp"].sem, 1)
                    for i2 in range(2):
                        act.wait_ge(s3["mix_mm"].sem, s3["mix_mm"].at(b, i2 + 1))
                        a(A3["sqb"][:, i2, 0:2 * D], bank[6 + i2][:], ACT.Square).then_inc(s3["mix_sq"].sem, 1)
                    for k in range(KT):
                        act.wait_ge(s3["o_turned"].sem, s3["o_turned"].at(b, k + 1))
                        a(onT[:, k, :], bank[k][:], ACT.Copy, scale=onorm[:, 0:1]).then_inc(s3["oT_out"].sem, 1)

            @block.vector
            def _(dve):
                v = nc.vector
                dve.wait_ge(s3["zeros3"].sem, 2)
                with dve.Fori(0, B) as b:
                    for n in range(4):
                        T = NJ if n == 0 else TT
                        v.tensor_reduce(stat(n, 0), branch(n, b), AX.X, ALU.add).then_inc(s3["red"].sem, 1)
                        v.tensor_reduce(stat(n, 2), branch(n, b), AX.X, ALU.max,
                                        apply_absolute_value=True).then_inc(s3["red"].sem, 1)
                        dve.wait_ge(s3["sq_out"].sem, s3["sq_out"].at(b, n + 1))
                        v.tensor_reduce(stat(n, 1), A3["sqb"][:, n % 2, 0:T * D].rearrange("p (t h c) -> p t h c", t=T, h=H),
                                        AX.X, ALU.add).then_inc(s3["sq_used"].sem, 1)
                    dve.wait_ge(s3["red"].sem, s3["red"].at(b, 8))
                    dve.wait_ge(s3["sq_used"].sem, s3["sq_used"].at(b, 4))
                    for s in (A3["tw"], A3["st"]):
                        v.tensor_scalar(s[:, :, 0, :], s[:, :, 0, :], 1.0 / DK, None, ALU.mult).then_inc(s3["small"].sem, 1)
                        v.tensor_scalar(s[:, :, 1, :], s[:, :, 1, :], 1.0 / DK, 1e-8, ALU.mult, ALU.max)\
                            .then_inc(s3["small"].sem, 1)
                    dve.wait_ge(s3["roots"].sem, s3["roots"].at(b, 1))
                    dve.wait_ge(s3["small"].sem, s3["small"].at(b, 4))
                    tw = A3["tw"].rearrange("p j s h -> p j (s h)")
                    v.tensor_copy(A3["sw"][0:DK, :, 0:12], tw[0:DK, :, :]).then_inc(s3["sw_out"].sem, 1)
                    v.tensor_copy(A3["sw"][DK:P, :, 12:24], tw[DK:P, :, :]).then_inc(s3["sw_out"].sem, 1)
                    lg, w = A3["lg"], A3["w"]
                    flat = lambda x: x.rearrange("p t h g -> p t (h g)")
                    groups = lambda x: x.rearrange("p t h g -> p (t h) g")
                    mx = A3["mx"].rearrange("p t h -> p (t h)")
                    dve.wait_ge(s3["lg_mm"].sem, s3["lg_mm"].at(b, 1))
                    v.tensor_tensor(flat(lg), bank[4][:, 0:80].rearrange("p (t n) -> p t n", t=TT),
                                    over_tiles(g2_bias[:], TT), ALU.add).then_inc(s3["lg_steps"].sem, 1)
                    dve.wait_ge(s3["lg_steps"].sem, s3["lg_steps"].at(b, 1))
                    v.tensor_tensor(flat(lg), flat(lg), over_tiles(inv_temp5[:, :, :].rearrange("p h g -> p (h g)"), TT),
                                    ALU.mult).then_inc(s3["lg_steps"].sem, 1)
                    dve.wait_ge(s3["lg_steps"].sem, s3["lg_steps"].at(b, 2))
                    v.tensor_reduce(mx, groups(lg), AX.X, ALU.max).then_inc(s3["lg_steps"].sem, 1)
                    dve.wait_ge(s3["lg_steps"].sem, s3["lg_steps"].at(b, 3))
                    v.tensor_tensor(groups(lg), groups(lg), over_last(mx, NG), ALU.subtract).then_inc(s3["lg_steps"].sem, 1)
                    dve.wait_ge(s3["lg_exp"].sem, s3["lg_exp"].at(b, 1))
                    v.tensor_reduce(mx, groups(lg), AX.X, ALU.add).then_inc(s3["lg_steps"].sem, 1)
                    dve.wait_ge(s3["lg_steps"].sem, s3["lg_steps"].at(b, 5))
                    v.reciprocal(mx, mx).then_inc(s3["lg_steps"].sem, 1)
                    dve.wait_ge(s3["lg_steps"].sem, s3["lg_steps"].at(b, 6))
                    v.tensor_tensor(A3["mx"], A3["mx"], over_tiles(keep[:], TT), ALU.mult).then_inc(s3["lg_steps"].sem, 1)
                    dve.wait_ge(s3["lg_steps"].sem, s3["lg_steps"].at(b, 7))
                    v.tensor_tensor(groups(w), groups(lg), over_last(mx, NG), ALU.mult).then_inc(s3["lg_steps"].sem, 1)
                    dve.wait_ge(s3["lg_steps"].sem, s3["lg_steps"].at(b, 8))
                    w4 = w[:, :, :, 0:NG - 1]
                    v.tensor_tensor(w4, w4, over_tiles(over_last(floor[:], NG - 1), TT), ALU.add)\
                        .then_inc(s3["lg_steps"].sem, 1)
                    dve.wait_ge(s3["lg_steps"].sem, s3["lg_steps"].at(b, 9))
                    v.tensor_tensor(A3["pv"].rearrange("p t (h c) -> p t h c", h=H), branch(3, b),
                                    over_last(w[:, :, :, 4], DK), ALU.mult).then_inc(s3["p_v"].sem, 1)
                    dve.wait_ge(s3["w_twice"].sem, s3["w_twice"].at(b, 1))
                    tw2 = bank[5][:, 0:160].rearrange("p (j h g) -> p j h g", h=H, g=NG)
                    ws = A3["wsel"].rearrange("p a t h -> p (a t) h")
                    v.tensor_copy(ws[0:DK], tw2[0:DK, :, :, 2]).then_inc(s3["w_sel"].sem, 1)
                    v.tensor_copy(ws[DK:P], tw2[DK:P, :, :, 1]).then_inc(s3["w_sel"].sem, 1)
                    dve.wait_ge(s3["w_sel"].sem, s3["w_sel"].at(b, 2))
                    for a in range(2):
                        v.tensor_tensor(A3["pwl"][:, :, a, :].rearrange("p t (h c) -> p t h c", h=H),
                                        wl.rearrange("p (t a) (h c) -> p t a h c", a=2, h=H)[:, bass.ds(b * TT, TT), a, :, :],
                                        over_last(A3["wsel"][:, a, :, :], DK), ALU.mult).then_inc(s3["p_wl"].sem, 1)
                    for i2 in range(2):
                        dve.wait_ge(s3["mix_sq"].sem, s3["mix_sq"].at(b, i2 + 1))
                        v.tensor_reduce(A3["ssh"][:, i2 * 8:i2 * 8 + 8],
                                        A3["sqb"][:, i2, 0:2 * D].rearrange("p (g c) -> p g c", c=DK), AX.X, ALU.add)\
                            .then_inc(s3["mix_ss"].sem, 1)
                    dve.wait_ge(s3["mix_ss"].sem, s3["mix_ss"].at(b, 2))
                    v.tensor_scalar(A3["ssh"], A3["ssh"], 1.0 / DK, 1e-5, ALU.mult, ALU.add).then_inc(s3["mix_ss"].sem, 1)
                    dve.wait_ge(s3["r_head"].sem, s3["r_head"].at(b, 1))
                    for i2 in range(2):
                        v.tensor_tensor(on[:, 2 * i2:2 * i2 + 2, :].rearrange("p t (h c) -> p (t h) c", h=H),
                                        bank[6 + i2][:].rearrange("p (g c) -> p g c", c=DK),
                                        over_last(A3["rh"][:, i2 * 8:i2 * 8 + 8], DK), ALU.mult).then_inc(s3["o_norm"].sem, 1)
                    for i2 in range(2):
                        dve.wait_ge(s3["y_mm"].sem, s3["y_mm"].at(b, i2 + 1))
                        v.tensor_tensor(xr[:, 2 * i2:2 * i2 + 2, :], A3["x"][:, 2 * i2:2 * i2 + 2, :],
                                        bank[2 + i2][:].rearrange("p (t c) -> p t c", t=2), ALU.add).then_inc(s3["res"].sem, 1)
                    layer_norm(dve, scratch, b, xr, A3, s3, "res", lambda t: delta[:, b * TT + t, :], "x1_out")

            @block.gpsimd
            def _(pool):
                g = nc.gpsimd
                g.memset(A3["sw"], 0.0).then_inc(s3["zeros3"].sem, 1)
                g.memset(A3["statT"], 0.0).then_inc(s3["zeros3"].sem, 1)
                with pool.Fori(0, B) as b:
                    pool.wait_ge(s3["lg_steps"].sem, s3["lg_steps"].at(b, 9))
                    ps, pd = A3["ps"], A3["sqb"][:, 0, 0:TT * D].rearrange("p (t c) -> p t c", t=TT)
                    heads = lambda x: x.rearrange("p t (h c) -> p t h c", h=H)
                    g.tensor_tensor(heads(ps), branch(1, b), over_last(A3["w"][:, :, :, 0], DK), ALU.mult)\
                        .then_inc(s3["p_sum"].sem, 1)
                    g.tensor_tensor(heads(pd), branch(2, b), over_last(A3["w"][:, :, :, 3], DK), ALU.mult)\
                        .then_inc(s3["p_sum"].sem, 1)
                    pool.wait_ge(s3["p_sum"].sem, s3["p_sum"].at(b, 2))
                    g.tensor_tensor(ps, ps, pd, ALU.add).then_inc(s3["p_sum"].sem, 1)
                    pool.wait_ge(s3["p_sum"].sem, s3["p_sum"].at(b, 3))
                    pool.wait_ge(s3["p_v"].sem, s3["p_v"].at(b, 1))
                    g.tensor_tensor(ps, ps, A3["pv"], ALU.add).then_inc(s3["p_sum"].sem, 1)
                    pool.wait_ge(s3["mix_ss"].sem, s3["mix_ss"].at(b, 3))
                    g.tensor_tensor(A3["rh"], A3["ssh"], half_exp[:, 0, :], ALU.pow).then_inc(s3["r_head"].sem, 1)
                    pool.wait_ge(s3["ln_st"].sem, s3["ln_st"].at(b, 9))
                    g.tensor_tensor(A3["rs"], A3["ve"], half_exp[:, 0, 0:TT], ALU.pow).then_inc(s3["ln_rs"].sem, 1)

        A4 = carve(arena, {
            "xeo": (2, 2, D), "ctx": (TT, D), "ceo": (2, 2, D), "XFT": (KT, 512), "CFT": (KT, 512), "QF": (4, D),
            "KVF": (4, 2 * D), "PR": (4, 2, D), "RD": (4, 2, XH), "CC": (2, 2, XH), "t1": (2, XH), "t2": (2, XH),
            "t3": (2, XH), "t4": (2, XH), "Es": (HALF,), "co": (L + 2,), "m8": (8,), "mr": (8,), "nb": (1,),
            "rep": (L + 2,), "ex": (L,), "e6": (TOPK,), "s6": (1,), "r6": (1,), "aeo": (L,), "AT": (4, XH),
            "AF": (3, 2, XH), "OF": (4, D), "Eb": (KT, HALF), "oT": (KT, L), "x1b": (TT, D), "xr": (TT, D),
            "ln": (TT, 6), "mv": (TT, 2), "ve": (TT,), "rs": (TT,)})
        free_4 = ("af", "at4_out", "ceo", "cf_mm", "co_out", "es_out", "ot_out", "res4", "x2_out")
        s4 = signals(4, {
            "ctx_in": 16, "xeo": 2, "ceo": 2, "xf_mm": 2, "cf_mm": 2, "xf_out": 2, "cf_out": 2, "qf_mm": 2, "kvf_mm": 4,
            "qf_out": 2, "kvf_out": 4, "prod_v": 2, "prod_g": 2, "corr_red": 1, "cc": 6, "corr_mm": 1, "es_out": 1,
            "co_out": 2, "top": 3, "rep_out": 1, "exps": 2, "a_steps": 5, "a_turned4": 1, "at4_out": 1, "af_mm": 1, "af": 5,
            "of_v": 2, "of_g": 2, "of": 2, "ot_mm": 2, "eb_out": 2, "ot_out": 4, "y4_mm": 2, "x1b_out": 1, "res4": 2,
            "ln_st": 9, "ln_rs": 1, "x2_out": 4, "sentinels": 0}, free_4)
        ab = lambda i: A4["PR"][:, i, :, :]
        with nc.Block() as block:
            @block.sync
            def _(sp):
                for n in free_4:
                    sp.sem_inc(s4[n].sem, 1)
                with sp.Fori(0, B) as b:
                    sp.wait_ge(s4["ceo"].sem, s4["ceo"].at(b, 0))
                    sp.dma_start(A4["ctx"], dr["ctx"][b].rearrange("(t p) d -> p t d", p=P)).then_inc(s4["ctx_in"].sem, 16)

            @block.tensor
            def _(pe):
                mm = nc.tensor.matmul
                pe.wait_ge(s4["sentinels"].sem, 2)
                with pe.Fori(0, B) as b:
                    for src, go, done, first, free in ((A4["ceo"], "ceo", "cf_mm", 2, "at4_out"), (A4["xeo"], "xeo", "xf_mm", 0, "res4")):
                        pe.wait_ge(s4[go].sem, s4[go].at(b, 2))
                        pe.wait_ge(s4[free].sem, s4[free].at(b, 0))
                        pe.wait_ge(s4["es_out"].sem, s4["es_out"].at(b, 0))
                        pe.wait_ge(s4["co_out"].sem, s4["co_out"].at(b, 0))
                        for d in range(KT):
                            for par in range(2):
                                for k in range(2):
                                    i = mm(bank[first + d][:, par * 256:(par + 1) * 256], src[:, par, k, d * P:(d + 1) * P],
                                           dft[:, k, par * 256:(par + 1) * 256], start=(k == 0), stop=(k == 1))
                            i.then_inc(s4[done].sem, 1)
                    pe.wait_ge(s4["xf_out"].sem, s4["xf_out"].at(b, 2))
                    pe.wait_ge(s4["af"].sem, s4["af"].at(b, 0))
                    pe.wait_ge(s4["ot_out"].sem, s4["ot_out"].at(b, 0))
                    for f in range(4):
                        o = bank[4 + f // 2][:, (f % 2) * D:(f % 2 + 1) * D]
                        for k in range(KT):
                            i = mm(o, A4["XFT"][:, k, f * P:(f + 1) * P], xq_w[:, k, :], start=(k == 0),
                                   stop=(k == KT - 1 and f > 0))
                        if f == 0:
                            i = mm(o, const["dc_row"][0:1, :], xq_b[:], start=False, stop=True)
                        if f % 2:
                            i.then_inc(s4["qf_mm"].sem, 1)
                    pe.wait_ge(s4["cf_out"].sem, s4["cf_out"].at(b, 2))
                    pe.wait_ge(s4["res4"].sem, s4["res4"].at(b, 0))
                    for f in range(4):
                        o = bank[(6 + f) % 8][:]
                        for k in range(KT):
                            i = mm(o, A4["CFT"][:, k, f * P:(f + 1) * P], xkv_w[:, k, :], start=(k == 0),
                                   stop=(k == KT - 1 and f > 0))
                        if f == 0:
                            i = mm(o, const["dc_row"][0:1, :], xkv_b[:], start=False, stop=True)
                        i.then_inc(s4["kvf_mm"].sem, 1)
                    pe.wait_ge(s4["cc"].sem, s4["cc"].at(b, 6))
                    for par in range(2):
                        for ri in range(2):
                            i = mm(bank[2][0:XH, par * HALF:(par + 1) * HALF], A4["CC"][:, ri, par, :],
                                   idft[:, 2 * par + ri, :], start=(ri == 0), stop=(ri == 1))
                    i.then_inc(s4["corr_mm"].sem, 1)
                    pe.wait_ge(s4["a_steps"].sem, s4["a_steps"].at(b, 5))
                    for k in range(4):
                        i = mm(bank[3][:, k * XH:(k + 1) * XH], A4["aeo"][0:XH, k * P:(k + 1) * P],
                               ident[0:XH, 0:XH], start=True, stop=True)
                    i.then_inc(s4["a_turned4"].sem, 1)
                    pe.wait_ge(s4["at4_out"].sem, s4["at4_out"].at(b, 1))
                    pe.wait_ge(s4["qf_out"].sem, s4["qf_out"].at(b, 2))
                    for f in range(4):
                        for k in range(2):
                            i = mm(bank[4][:, f * XH:(f + 1) * XH], dft[:, k, f * P:(f + 1) * P],
                                   A4["AT"][:, 2 * (f // 2) + k, :], start=(k == 0), stop=(k == 1))
                    i.then_inc(s4["af_mm"].sem, 1)
                    pe.wait_ge(s4["of"].sem, s4["of"].at(b, 2))
                    pe.wait_ge(s4["kvf_out"].sem, s4["kvf_out"].at(b, 4))
                    for m in range(KT):
                        for par in range(2):
                            for ri in range(2):
                                i = mm(bank[5 + m][:, par * HALF:(par + 1) * HALF], A4["OF"][:, 2 * par + ri, m * P:(m + 1) * P],
                                       idft[:, 2 * par + ri, :], start=(ri == 0), stop=(ri == 1))
                        i.then_inc(s4["ot_mm"].sem, 1)
                    pe.wait_ge(s4["ot_out"].sem, s4["ot_out"].at(b, 4))
                    for t in range(TT):
                        for k in range(KT):
                            i = mm(bank[[7, 0][t // 2]][:, (t % 2) * D:(t % 2 + 1) * D], A4["oT"][:, k, t * P:(t + 1) * P],
                                   xo_w[:, k, :], start=(k == 0), stop=(k == KT - 1))
                        if t % 2:
                            i.then_inc(s4["y4_mm"].sem, 1)

            @block.scalar
            def _(act):
                a = nc.scalar.activation
                act.wait_ge(s4["sentinels"].sem, 2)
                with act.Fori(0, B) as b:
                    for d in range(KT):
                        act.wait_ge(s4["cf_mm"].sem, s4["cf_mm"].at(b, d + 1))
                        nc.scalar.copy(A4["CFT"][:, d, :], bank[2 + d][:]).then_inc(s4["cf_out"].sem, 1)
                    for d in range(KT):
                        act.wait_ge(s4["xf_mm"].sem, s4["xf_mm"].at(b, d + 1))
                        nc.scalar.copy(A4["XFT"][:, d, :], bank[d][:]).then_inc(s4["xf_out"].sem, 1)
                    for i2 in range(2):
                        act.wait_ge(s4["qf_mm"].sem, s4["qf_mm"].at(b, i2 + 1))
                        nc.scalar.copy(A4["QF"][:, 2 * i2:2 * i2 + 2, :], bank[4 + i2][:].rearrange("p (t c) -> p t c", t=2))\
                            .then_inc(s4["qf_out"].sem, 1)
                    for f in range(4):
                        act.wait_ge(s4["kvf_mm"].sem, s4["kvf_mm"].at(b, f + 1))
                        nc.scalar.copy(A4["KVF"][:, f, :], bank[(6 + f) % 8][:]).then_inc(s4["kvf_out"].sem, 1)
                    act.wait_ge(s4["corr_mm"].sem, s4["corr_mm"].at(b, 1))
                    nc.scalar.copy(A4["Es"][0:XH, :], bank[2][0:XH, 0:HALF]).then_inc(s4["es_out"].sem, 1)
                    act.wait_ge(s4["top"].sem, s4["top"].at(b, 3))
                    a(A4["ex"][0:XH, :], A4["co"][0:XH, 0:L], ACT.Exp, bias=A4["nb"][0:XH, :], scale=1.0 / XD)\
                        .then_inc(s4["exps"].sem, 1)
                    a(A4["e6"][0:XH, :], A4["m8"][0:XH, 0:TOPK], ACT.Exp, bias=A4["nb"][0:XH, :], scale=1.0 / XD,
                      accum_out=A4["s6"][0:XH, :]).then_inc(s4["exps"].sem, 1)
                    for m in range(KT):
                        act.wait_ge(s4["ot_mm"].sem, s4["ot_mm"].at(b, m + 1))
                        nc.scalar.copy(A4["Eb"][:, m, :], bank[5 + m][:, 0:HALF]).then_inc(s4["eb_out"].sem, 1)

            def spectra(i):
                return {"qr": A4["QF"][:, 0::2, :], "qi": A4["QF"][:, 1::2, :],
                        "kr": A4["KVF"][:, 0::2, 0:D], "ki": A4["KVF"][:, 1::2, 0:D],
                        "vr": A4["KVF"][:, 0::2, D:2 * D], "vi": A4["KVF"][:, 1::2, D:2 * D]}[i]

            @block.vector
            def _(dve):
                v = nc.vector
                dve.wait_ge(s4["sentinels"].sem, 2)
                with dve.Fori(0, B) as b:
                    x1 = delta[:, bass.ds(b * TT, TT), :]
                    dve.wait_ge(s4["x2_out"].sem, s4["x2_out"].at(b, 0))
                    v.tensor_tensor(A4["xeo"][:, 0, :, :], x1[:, 0:2, :], x1[:, 2:4, :], ALU.add).then_inc(s4["xeo"].sem, 1)
                    v.tensor_tensor(A4["xeo"][:, 1, :, :], x1[:, 0:2, :], x1[:, 2:4, :], ALU.subtract).then_inc(s4["xeo"].sem, 1)
                    dve.wait_ge(s4["qf_out"].sem, s4["qf_out"].at(b, 2))
                    dve.wait_ge(s4["kvf_out"].sem, s4["kvf_out"].at(b, 4))
                    v.tensor_tensor(ab(0), spectra("qr"), spectra("kr"), ALU.mult).then_inc(s4["prod_v"].sem, 1)
                    v.tensor_tensor(ab(1), spectra("qi"), spectra("ki"), ALU.mult).then_inc(s4["prod_v"].sem, 1)
                    dve.wait_ge(s4["prod_v"].sem, s4["prod_v"].at(b, 2))
                    dve.wait_ge(s4["prod_g"].sem, s4["prod_g"].at(b, 2))
                    v.tensor_reduce(A4["RD"].rearrange("p a e h -> p (a e h)"),
                                    A4["PR"].rearrange("p a e (h c) -> p (a e h) c", c=XD), AX.X, ALU.add)\
                        .then_inc(s4["corr_red"].sem, 1)
                    dve.wait_ge(s4["corr_red"].sem, s4["corr_red"].at(b, 1))
                    rd = lambda i: A4["RD"][:, i, :, :]
                    steps = [(A4["t1"], rd(1), not_dc, ALU.mult), (A4["t2"], rd(2), rd(3), ALU.subtract),
                             (A4["t4"], rd(1), is_dc, ALU.mult), (A4["CC"][:, 0, :, :], rd(0), A4["t1"], ALU.add),
                             (A4["t3"], A4["t2"], not_dc, ALU.mult), (A4["CC"][:, 1, :, :], A4["t3"], A4["t4"], ALU.add)]
                    for n, (o, x, y, op) in enumerate(steps):
                        if n >= 3:
                            dve.wait_ge(s4["cc"].sem, s4["cc"].at(b, n if n == 5 else n - 1))
                        v.tensor_tensor(o, x, y, op).then_inc(s4["cc"].sem, 1)
                    dve.wait_ge(s4["corr_mm"].sem, s4["corr_mm"].at(b, 1))
                    dve.wait_ge(s4["es_out"].sem, s4["es_out"].at(b, 1))
                    es, od = A4["Es"][0:XH, :], bank[2][0:XH, HALF:L]
                    v.tensor_tensor(A4["co"][0:XH, 0:HALF], es, od, ALU.add).then_inc(s4["co_out"].sem, 1)
                    v.tensor_tensor(A4["co"][0:XH, HALF:L], es, od, ALU.subtract).then_inc(s4["co_out"].sem, 1)
                    dve.wait_ge(s4["co_out"].sem, s4["co_out"].at(b, 2))
                    v.memset(scratch, 0.0)
                    v.max(A4["m8"][0:XH, :], A4["co"][0:XH, 0:L]).then_inc(s4["top"].sem, 1)
                    dve.wait_ge(s4["top"].sem, s4["top"].at(b, 1))
                    v.tensor_copy(A4["mr"][0:XH, 0:TOPK], A4["m8"][0:XH, 0:TOPK]).then_inc(s4["top"].sem, 1)
                    dve.wait_ge(s4["top"].sem, s4["top"].at(b, 2))
                    v.tensor_scalar(A4["nb"][0:XH, :], A4["m8"][0:XH, 0:1], -1.0 / XD, None, ALU.mult)\
                        .then_inc(s4["top"].sem, 1)
                    v.match_replace(A4["rep"][0:XH, :], A4["mr"][0:XH, :], A4["co"][0:XH, :], BIG)\
                        .then_inc(s4["rep_out"].sem, 1)
                    dve.wait_ge(s4["rep_out"].sem, s4["rep_out"].at(b, 1))
                    dve.wait_ge(s4["exps"].sem, s4["exps"].at(b, 2))
                    v.reciprocal(A4["r6"][0:XH, :], A4["s6"][0:XH, :]).then_inc(s4["a_steps"].sem, 1)
                    v.scalar_tensor_tensor(out=A4["rep"][0:XH, 0:L], in0=A4["rep"][0:XH, 0:L], scalar=BIG,
                                           in1=A4["ex"][0:XH, :], op0=ALU.is_ge, op1=ALU.mult).then_inc(s4["a_steps"].sem, 1)
                    dve.wait_ge(s4["a_steps"].sem, s4["a_steps"].at(b, 2))
                    v.tensor_scalar(A4["rep"][0:XH, 0:L], A4["rep"][0:XH, 0:L], A4["r6"][0:XH, :], None, ALU.mult)\
                        .then_inc(s4["a_steps"].sem, 1)
                    dve.wait_ge(s4["a_steps"].sem, s4["a_steps"].at(b, 3))
                    lo, hi = A4["rep"][0:XH, 0:HALF], A4["rep"][0:XH, HALF:L]
                    v.tensor_tensor(A4["aeo"][0:XH, 0:HALF], lo, hi, ALU.add).then_inc(s4["a_steps"].sem, 1)
                    v.tensor_tensor(A4["aeo"][0:XH, HALF:L], lo, hi, ALU.subtract).then_inc(s4["a_steps"].sem, 1)
                    dve.wait_ge(s4["a_turned4"].sem, s4["a_turned4"].at(b, 1))
                    v.tensor_copy(A4["AT"].rearrange("p k h -> p (k h)"), bank[3][:, 0:4 * XH]).then_inc(s4["at4_out"].sem, 1)
                    dve.wait_ge(s4["af_mm"].sem, s4["af_mm"].at(b, 1))
                    af = bank[4][:, 0:4 * XH].rearrange("p (a ri h) -> p a ri h", a=2, ri=2)
                    a1, a2, a3 = (A4["AF"][:, n, :, :] for n in range(3))
                    v.tensor_copy(a1, af[:, :, 0, :]).then_inc(s4["af"].sem, 1)
                    v.tensor_tensor(a2, af[:, :, 1, :], not_dc, ALU.mult).then_inc(s4["af"].sem, 1)
                    v.tensor_tensor(A4["t1"], af[:, :, 1, :], is_dc, ALU.mult).then_inc(s4["af"].sem, 1)
                    v.tensor_tensor(A4["t2"], af[:, :, 0, :], not_dc, ALU.mult).then_inc(s4["af"].sem, 1)
                    dve.wait_ge(s4["af"].sem, s4["af"].at(b, 4))
                    v.tensor_tensor(a3, A4["t1"], A4["t2"], ALU.add).then_inc(s4["af"].sem, 1)
                    hd = lambda x: x.rearrange("p e (h c) -> p e h c", c=XD)
                    v.tensor_tensor(hd(ab(0)), hd(spectra("vr")), over_last(a1, XD), ALU.mult).then_inc(s4["of_v"].sem, 1)
                    dve.wait_ge(s4["af"].sem, s4["af"].at(b, 5))
                    v.tensor_tensor(hd(ab(2)), hd(spectra("vi")), over_last(a3, XD), ALU.mult).then_inc(s4["of_v"].sem, 1)
                    dve.wait_ge(s4["of_v"].sem, s4["of_v"].at(b, 2))
                    dve.wait_ge(s4["of_g"].sem, s4["of_g"].at(b, 2))
                    v.tensor_tensor(A4["OF"][:, 0::2, :], ab(0), ab(1), ALU.subtract).then_inc(s4["of"].sem, 1)
                    v.tensor_tensor(A4["OF"][:, 1::2, :], ab(2), ab(3), ALU.add).then_inc(s4["of"].sem, 1)
                    for m in range(KT):
                        dve.wait_ge(s4["eb_out"].sem, s4["eb_out"].at(b, m + 1))
                        eb, od = A4["Eb"][:, m, :], bank[5 + m][:, HALF:L]
                        v.tensor_tensor(A4["oT"][:, m, 0:HALF], eb, od, ALU.add).then_inc(s4["ot_out"].sem, 1)
                        v.tensor_tensor(A4["oT"][:, m, HALF:L], eb, od, ALU.subtract).then_inc(s4["ot_out"].sem, 1)
                    dve.wait_ge(s4["x1b_out"].sem, s4["x1b_out"].at(b, 1))
                    for i2 in range(2):
                        dve.wait_ge(s4["y4_mm"].sem, s4["y4_mm"].at(b, i2 + 1))
                        v.tensor_tensor(A4["xr"][:, 2 * i2:2 * i2 + 2, :], A4["x1b"][:, 2 * i2:2 * i2 + 2, :],
                                        bank[[7, 0][i2]][:].rearrange("p (t c) -> p t c", t=2), ALU.add)\
                            .then_inc(s4["res4"].sem, 1)
                    layer_norm(dve, scratch, b, A4["xr"], A4, s4, "res4", lambda t: short[:, b * TT + t, :], "x2_out")

            @block.gpsimd
            def _(pool):
                g = nc.gpsimd
                g.memset(A4["co"][:, L:L + 2], -BIG).then_inc(s4["sentinels"].sem, 1)
                g.memset(A4["mr"], -BIG).then_inc(s4["sentinels"].sem, 1)
                with pool.Fori(0, B) as b:
                    c = A4["ctx"]
                    pool.wait_ge(s4["ctx_in"].sem, s4["ctx_in"].at(b, 16))
                    pool.wait_ge(s4["cf_mm"].sem, s4["cf_mm"].at(b, 0))
                    g.tensor_tensor(A4["ceo"][:, 0, :, :], c[:, 0:2, :], c[:, 2:4, :], ALU.add).then_inc(s4["ceo"].sem, 1)
                    g.tensor_tensor(A4["ceo"][:, 1, :, :], c[:, 0:2, :], c[:, 2:4, :], ALU.subtract).then_inc(s4["ceo"].sem, 1)
                    pool.wait_ge(s4["res4"].sem, s4["res4"].at(b, 0))
                    g.tensor_tensor(A4["x1b"], delta[:, bass.ds(b * TT, TT), :], over_tiles(xo_b[:], TT), ALU.add)\
                        .then_inc(s4["x1b_out"].sem, 1)
                    pool.wait_ge(s4["qf_out"].sem, s4["qf_out"].at(b, 2))
                    pool.wait_ge(s4["kvf_out"].sem, s4["kvf_out"].at(b, 4))
                    g.tensor_tensor(ab(2), spectra("qi"), spectra("kr"), ALU.mult).then_inc(s4["prod_g"].sem, 1)
                    g.tensor_tensor(ab(3), spectra("qr"), spectra("ki"), ALU.mult).then_inc(s4["prod_g"].sem, 1)
                    pool.wait_ge(s4["af"].sem, s4["af"].at(b, 5))
                    a2 = A4["AF"][:, 1, :, :]
                    hd = lambda x: x.rearrange("p e (h c) -> p e h c", c=XD)
                    g.tensor_tensor(hd(ab(1)), hd(spectra("vi")), over_last(a2, XD), ALU.mult).then_inc(s4["of_g"].sem, 1)
                    g.tensor_tensor(hd(ab(3)), hd(spectra("vr")), over_last(a2, XD), ALU.mult).then_inc(s4["of_g"].sem, 1)
                    pool.wait_ge(s4["ln_st"].sem, s4["ln_st"].at(b, 9))
                    g.tensor_tensor(A4["rs"], A4["ve"], half_exp[:, 0, 0:TT], ALU.pow).then_inc(s4["ln_rs"].sem, 1)

        A5 = carve(arena, {"wi": (3, KT * HID), "wg": (KT, HID), "wu": (KT, HID), "wd": (MF, D),
                           "x2": (TT, D), "x2T": (KT, L), "sg": (2, L), "hT": (MF, L), "xr": (TT, D), "y": (TT, D),
                           "ln": (TT, 6), "mv": (TT, 2), "ve": (TT,), "rs": (TT,)})
        free_5 = ("h_out", "res5", "stored")
        s5 = signals(5, {"w_in": 0, "w_f32": 0, "x2_copy": 1, "x_turned5": 2, "x2T_out": 2, "gate_mm": 6, "up_mm": 6,
                      "gate_silu": 6, "h_out": 6, "y5_mm": 2, "res5": 2, "ln_st": 9, "ln_rs": 1, "y_out": 4,
                      "stored": 16}, free_5)
        with nc.Block() as block:
            @block.sync
            def _(sp):
                for n in free_5:
                    sp.sem_inc(s5[n].sem, 1)
                wi = A5["wi"].bitcast(I32)
                for n, (name, k) in enumerate((("w_gateT", KT), ("w_upT", KT), ("w_downT", MF))):
                    sp.dma_start(wi[:, n, :].rearrange("p (k n) -> p k n", k=k),
                                 dr[name].rearrange("(k p) n -> p k n", p=P)).then_inc(s5["w_in"].sem, 16)
                with sp.Fori(0, B) as b:
                    sp.wait_ge(s5["y_out"].sem, s5["y_out"].at(b, 4))
                    sp.dma_start(out[b].rearrange("(t p) d -> p t d", p=P), A5["y"]).then_inc(s5["stored"].sem, 16)
                sp.wait_ge(s5["stored"].sem, s5["stored"].at(B, 0))

            @block.tensor
            def _(pe):
                mm = nc.tensor.matmul
                pe.wait_ge(s5["w_f32"].sem, 3)
                with pe.Fori(0, B) as b:
                    pe.wait_ge(s5["x2_copy"].sem, s5["x2_copy"].at(b, 1))
                    for k in range(KT):
                        for t in range(TT):
                            i = nc.tensor.transpose(bank[k][:, t * P:(t + 1) * P], A5["x2"][:, t, k * P:(k + 1) * P], ident[:])
                        i.then_inc(s5["x_turned5"].sem, 1)
                    pe.wait_ge(s5["x2T_out"].sem, s5["x2T_out"].at(b, 2))
                    for m in range(MF):
                        for w, first, done in (("wg", 2, "gate_mm"), ("wu", 4, "up_mm")):
                            pe.wait_ge(s5["h_out"].sem, s5["h_out"].at(b, m - 1 if m >= 2 else 0))
                            for k in range(KT):
                                i = mm(bank[first + m % 2][:], A5[w][:, k, m * P:(m + 1) * P], A5["x2T"][:, k, :],
                                       start=(k == 0), stop=(k == KT - 1))
                            i.then_inc(s5[done].sem, 1)
                    pe.wait_ge(s5["h_out"].sem, s5["h_out"].at(b, MF))
                    pe.wait_ge(s5["res5"].sem, s5["res5"].at(b, 0))
                    for t in range(TT):
                        for m in range(MF):
                            i = mm(bank[6 + t // 2][:, (t % 2) * D:(t % 2 + 1) * D], A5["hT"][:, m, t * P:(t + 1) * P],
                                   A5["wd"][:, m, :], start=(m == 0), stop=(m == MF - 1))
                        if t % 2:
                            i.then_inc(s5["y5_mm"].sem, 1)

            @block.scalar
            def _(act):
                act.wait_ge(s5["w_in"].sem, 48)
                wi = A5["wi"].bitcast(I32)
                for n, w in enumerate(("wg", "wu", "wd")):
                    nc.scalar.activation(A5[w].rearrange("p k n -> p (k n)"), wi[:, n, :], ACT.Copy, scale=1.0 / 127.0)\
                        .then_inc(s5["w_f32"].sem, 1)
                with act.Fori(0, B) as b:
                    for k in range(KT):
                        act.wait_ge(s5["x_turned5"].sem, s5["x_turned5"].at(b, k + 1))
                        nc.scalar.copy(A5["x2T"][:, k, :], bank[k][:]).then_inc(s5["x2T_out"].sem, 1)
                    for m in range(MF):
                        act.wait_ge(s5["gate_mm"].sem, s5["gate_mm"].at(b, m + 1))
                        act.wait_ge(s5["h_out"].sem, s5["h_out"].at(b, m - 1 if m >= 2 else 0))
                        nc.scalar.activation(A5["sg"][:, m % 2, :], bank[2 + m % 2][:], ACT.Silu)\
                            .then_inc(s5["gate_silu"].sem, 1)

            @block.vector
            def _(dve):
                v = nc.vector
                with dve.Fori(0, B) as b:
                    for m in range(MF):
                        dve.wait_ge(s5["gate_silu"].sem, s5["gate_silu"].at(b, m + 1))
                        dve.wait_ge(s5["up_mm"].sem, s5["up_mm"].at(b, m + 1))
                        v.tensor_tensor(A5["hT"][:, m, :], A5["sg"][:, m % 2, :], bank[4 + m % 2][:], ALU.mult)\
                            .then_inc(s5["h_out"].sem, 1)
                    for i2 in range(2):
                        dve.wait_ge(s5["y5_mm"].sem, s5["y5_mm"].at(b, i2 + 1))
                        v.tensor_tensor(A5["xr"][:, 2 * i2:2 * i2 + 2, :], A5["x2"][:, 2 * i2:2 * i2 + 2, :],
                                        bank[6 + i2][:].rearrange("p (t c) -> p t c", t=2), ALU.add).then_inc(s5["res5"].sem, 1)
                    dve.wait_ge(s5["stored"].sem, s5["stored"].at(b, 0))
                    layer_norm(dve, scratch, b, A5["xr"], A5, s5, "res5", lambda t: A5["y"][:, t, :], "y_out")

            @block.gpsimd
            def _(pool):
                with pool.Fori(0, B) as b:
                    pool.wait_ge(s5["res5"].sem, s5["res5"].at(b, 0))
                    nc.gpsimd.tensor_copy(A5["x2"], short[:, bass.ds(b * TT, TT), :]).then_inc(s5["x2_copy"].sem, 1)
                    pool.wait_ge(s5["ln_st"].sem, s5["ln_st"].at(b, 9))
                    nc.gpsimd.tensor_tensor(A5["rs"], A5["ve"], half_exp[:, 0, 0:TT], ALU.pow).then_inc(s5["ln_rs"].sem, 1)


def kernel(**inputs):
    import concourse.bacc as _bacc
    from concourse.bass_utils import run_bass_kernel_spmd as _run

    def turned(name):
        return np.ascontiguousarray(np.asarray(inputs[name]).T)

    a = {n: np.asarray(v) for n, v in inputs.items()}
    g1 = a["L0_attn_g1_w"]
    order = [0, 3, 4, 2, 1]
    g1s = np.concatenate([g1[:, D + 12 * i:D + 12 * i + 12] for i in order], axis=1)

    def hankel(name):
        w = a[name].reshape(D, -1)
        z = np.zeros((P - 1 + DK, D), w.dtype)
        z[P - w.shape[1]:P] = w.T
        return np.ascontiguousarray(z.reshape(-1, NPIECE, PIECE).transpose(1, 0, 2))

    arrays = {
        "x": a["x"], "xT": np.ascontiguousarray(a["x"].transpose(0, 2, 1)), "ctx": a["ctx_1024"],
        "qkv_wT": np.concatenate([turned(f"L0_attn_{n}_w") for n in "qkv"], axis=1),
        "b_wT": turned("L0_attn_b_w"),
        "conv_w": np.concatenate([a[f"L0_attn_conv{n}_w"] for n in "qkv"], axis=0),
        "fir_s": a["L0_attn_fir_s"].reshape(D, -1),
        "toep_w": hankel("L0_attn_fir_wd"), "toep_l": hankel("L0_attn_fir_l"),
        "g1x_wT": np.ascontiguousarray(g1[:, 0:D].T), "g1s_wT": np.ascontiguousarray(g1s.T), "g1_b": a["L0_attn_g1_b"].reshape(-1, P).T,
        "g2_wT": turned("L0_attn_g2_w"), "g2_b": a["L0_attn_g2_b"], "onorm": a["L0_attn_onorm_w"],
        "o_wT": turned("L0_attn_o_w"),
        "gate_par": np.concatenate([a["L0_attn_value_bias"], a["L0_attn_log_temp"], a["L0_attn_floor_logit"]]),
        "xq_wT": turned("L0_xattn_Wq"), "xq_b": a["L0_xattn_bq"],
        "xkv_wT": np.concatenate([turned("L0_xattn_Wk"), turned("L0_xattn_Wv")], axis=1),
        "xkv_b": np.concatenate([a["L0_xattn_bk"], a["L0_xattn_bv"]]),
        "xo_wT": turned("L0_xattn_Wo"), "xo_b": a["L0_xattn_bo"],
        "w_gateT": turned("L0_ffn_w_gate"), "w_upT": turned("L0_ffn_w_up"), "w_downT": turned("L0_ffn_w_down"),
    }
    arrays.update({"c_" + n: v for n, v in shape_constants().items()})
    arrays = {n: np.ascontiguousarray(v) for n, v in arrays.items()}
    nc = _bacc.Bacc("TRN2", target_bir_lowering=False, num_devices=1)
    dr = {n: nc.dram_tensor("in_" + n, v.shape, mybir.dt.from_np(v.dtype), kind="ExternalInput").ap()
          for n, v in arrays.items()}
    out = nc.dram_tensor("out_0", (B, L, D), F32, kind="ExternalOutput").ap()
    layer(nc, dr, out)
    r = _run(nc, [{"in_" + n: v for n, v in arrays.items()}], core_ids=[0])
    return r.results[0]["out_0"]
```

```python
from contextlib import ExitStack

import numpy as np

import concourse.bass as bass
from concourse import mybir

F32 = mybir.dt.float32
I32 = mybir.dt.int32
ALU = mybir.AluOpType
ACT = mybir.ActivationFunctionType
AX = mybir.AxisListType

P = 128
B, L, D = 4, 512, 256
H, DK = 4, 64
KT = D // P
TT = L // P
BT = B * TT
NJ = L // DK
CONV_K, FIR_S, FIR_L, FIR_W = 4, 3, 31, 64
LEVELS = 7
GH = 2 * D
NG = 5
HID = 768
MF = HID // P
XH, XD = 16, 16
TOPK = 6
PIECE = 8
NPIECE = D // PIECE
PER_BATCH = NPIECE // B
TOEP_BUFS = 4
HALF = L // 2
BIG = 3.0e38


def shape_constants():
    i = np.arange(P)
    c = {}
    c["ident"] = np.eye(P)
    c["mask_lower"] = (i[:, None] > i[None, :])
    c["mask_upper"] = (i[None, :] >= i[:, None])
    c["level0"] = -((i[:, None] % 2 == 1) & (i[None, :] == i[:, None] - 1)).astype(float)
    c["blocks"] = (i[:, None] // DK == i[None, :] // DK)
    lev = np.zeros((P, LEVELS - 1, P // 2))
    for k in range(1, LEVELS):
        even = i[(i >> k) % 2 == 0]
        lev[:, k - 1, :] = ((i[:, None] >> k) % 2 == 1) & ((i[:, None] >> (k + 1)) == (even[None, :] >> (k + 1)))
    c["levels"] = lev.reshape(P, -1)
    c["heads"] = (i[:, None] // DK == np.arange(2)[None, :])
    back = DK - 1 - i % DK
    c["fold"] = (back[:, None] == np.arange(DK)[None, :])
    c["fold_even"] = (back[:, None] == i[None, :])
    c["fold_odd"] = (back[:, None] + DK == i[None, :])
    c["twice_even"] = (i[:, None] == back[None, :])
    c["twice_odd"] = (i[:, None] == back[None, :] + DK)
    t = np.arange(HALF)
    f = np.arange(P)
    dft, inv = np.zeros((HALF, 4, P)), np.zeros((P, 4, HALF))
    for par in range(2):
        w = 2 * np.pi * ((2 * f + par)[None, :] * t[:, None] % L) / L
        dft[:, 2 * par], dft[:, 2 * par + 1] = np.cos(w), -np.sin(w)
        inv[:, 2 * par], inv[:, 2 * par + 1] = 2 * np.cos(w).T / L, -2 * np.sin(w).T / L
    dft[:, 1, 0] = (-1.0) ** t
    inv[0, 0], inv[0, 1] = 1.0 / L, (-1.0) ** t / L
    c["dft"] = dft.reshape(2, P, 4 * P).transpose(1, 0, 2).reshape(P, -1)
    c["idft"] = inv.reshape(P, -1)
    z = np.ones((P, 2, XH)); z[0, 0] = 0.0
    c["not_dc"] = z.reshape(P, -1)
    c["is_dc"] = (1.0 - z).reshape(P, -1)
    row = np.zeros((P, P)); row[0, 0] = L
    c["dc_row"] = row
    return {n: np.ascontiguousarray(a.astype(np.float32).reshape(P, -1)) for n, a in c.items()}


LATE_CONST = ("dft", "idft")


class Signal:

    def __init__(self, sem, per_round, base=0):
        self.sem, self.n, self.base = sem, per_round, base

    def at(self, rnd, k):
        return rnd * self.n + (self.base + k)


def carve(arena, sizes, at=0):
    out = {}
    for name, shape in sizes.items():
        n = int(np.prod(shape))
        v = arena[:, at:at + n]
        if len(shape) == 2:
            v = v.rearrange("p (a b) -> p a b", a=shape[0])
        elif len(shape) == 3:
            v = v.rearrange("p (a b c) -> p a b c", a=shape[0], b=shape[1])
        elif len(shape) == 4:
            v = v.rearrange("p (a b c d) -> p a b c d", a=shape[0], b=shape[1], c=shape[2])
        out[name] = v
        at += n
    assert at <= arena.shape[1], (at, arena.shape)
    return out


def over_last(ap, n):
    return ap.unsqueeze(len(ap.shape)).broadcast_to(list(ap.shape) + [n])


def over_tiles(ap, n):
    return ap.unsqueeze(1).broadcast_to([ap.shape[0], n] + list(ap.shape[1:]))


def layer_norm(dve, scratch, b, x, buf, sig, summed, dst, done):
    v = dve
    for t in range(TT):
        dve.wait_ge(sig[summed].sem, sig[summed].at(b, t // 2 + 1))
        v.bn_stats(buf["ln"][:, t, :], x[:, t, :]).then_inc(sig["ln_st"].sem, 1)
    dve.wait_ge(sig["ln_st"].sem, sig["ln_st"].at(b, TT))
    v.memset(scratch, 0.0)
    for t in range(TT):
        v.bn_aggr(buf["mv"][:, t, :], buf["ln"][:, t, :]).then_inc(sig["ln_st"].sem, 1)
    dve.wait_ge(sig["ln_st"].sem, sig["ln_st"].at(b, 2 * TT))
    v.tensor_scalar(buf["ve"], buf["mv"][:, :, 1], 1e-5, None, ALU.add).then_inc(sig["ln_st"].sem, 1)
    dve.wait_ge(sig["ln_rs"].sem, sig["ln_rs"].at(b, 1))
    for t in range(TT):
        v.tensor_scalar(dst(t), x[:, t, :], buf["mv"][:, t, 0:1], buf["rs"][:, t:t + 1], ALU.subtract,
                        ALU.mult).then_inc(sig[done].sem, 1)


def layer(nc, dr, out):
    ctx = ExitStack()
    with ctx:
        def sb(name, shape, dt=F32):
            return ctx.enter_context(nc.sbuf_tensor(name, shape, dt))

        def signals(stage, names, from_one):
            return {n: Signal(ctx.enter_context(nc.semaphore(f"{n}_{stage}")), k, int(n in from_one))
                    for n, k in names.items()}

        bank = [ctx.enter_context(nc.psum_tensor(f"bank{i}", [P, 512], F32)) for i in range(8)]

        v_win = sb("v_win", [P, B * NJ, D])
        short = sb("short", [P, BT, D])
        delta = sb("delta", [P, BT, D])
        arena = sb("arena", [P, 29600])
        v_tiles = v_win[:, :, :].rearrange("p (t two) c -> p t two c", two=2)

        const_shapes = {n: a.shape[1] for n, a in shape_constants().items() if n not in LATE_CONST}
        const = {n: sb("c_" + n, [P, w]) for n, w in const_shapes.items()}
        ident = const["ident"]
        levels = const["levels"][:, :].rearrange("p (k c) -> p k c", k=LEVELS - 1)
        late = carve(v_win[:, :, :].rearrange("p t c -> p (t c)"), {
            "dft": (2, 4 * P), "idft": (4, HALF), "xq_w": (KT, D), "xkv_w": (KT, 2 * D), "xo_w": (KT, D)})
        dft, idft, xq_w, xkv_w, xo_w = (late[n] for n in ("dft", "idft", "xq_w", "xkv_w", "xo_w"))
        not_dc = const["not_dc"][:, :].rearrange("p (a h) -> p a h", a=2)
        is_dc = const["is_dc"][:, :].rearrange("p (a h) -> p a h", a=2)

        qkv_w = sb("qkv_w", [P, KT, 3 * D])
        beta_w = sb("beta_w", [P, KT, H])
        conv_w = sb("conv_w", [P, 6, CONV_K])
        short_w = sb("short_w", [P, KT, FIR_S])
        g1x_w = sb("g1x_w", [P, KT, GH])
        g1s_w = sb("g1s_w", [P, GH])
        g1_bias = sb("g1_bias", [P, GH // P])
        g2_w = sb("g2_w", [P, GH // P, NG * H])
        onorm = sb("onorm", [P, 1])
        ow_w = sb("ow_w", [P, KT, D])
        xq_b = sb("xq_b", [1, D])
        xkv_b = sb("xkv_b", [1, 2 * D])
        xo_b = sb("xo_b", [P, D])
        g2_bias = sb("g2_bias", [P, NG * H])
        gate_par = sb("gate_par", [P, 3, H])
        inv_temp = sb("inv_temp", [P, H])
        inv_temp5 = sb("inv_temp5", [P, H, NG])
        floor = sb("floor", [P, H])
        keep = sb("keep", [P, H])
        half_exp = sb("half_exp", [P, 2, 16])

        first_loaded = Signal(ctx.enter_context(nc.semaphore("first_loaded")), 0)
        late_loaded = Signal(ctx.enter_context(nc.semaphore("late_loaded")), 0)
        loaded = Signal(ctx.enter_context(nc.semaphore("loaded")), 0)
        ready = Signal(ctx.enter_context(nc.semaphore("ready")), 0)
        scratch = sb("scratch", [P, 1])[:]
        n_loads = [0]

        A1 = carve(arena, {"xT": (KT, L), "acc": (KT, L), "vT": (KT, DK + L), "sh": (KT, L)})
        free_1 = ("v_out", "sh_out")
        s1 = signals(1, {
            "xT_in": 16, "proj": 2, "tap_last": 2, "conv": 6, "silu": 2, "v_turned": 4, "sh_turned": 2, "v_out": 4,
            "sh_out": 2, "sh_conv": 6, "pads": 0}, free_1)

        def tap_one(nc, acc, src, m, j):
            return nc.vector.scalar_tensor_tensor(out=acc[:, j:L], in0=src[:, 0:L - j],
                                                  scalar=conv_w[:, m, CONV_K - 1 - j:CONV_K - j], in1=acc[:, j:L],
                                                  op0=ALU.mult, op1=ALU.add)

        with nc.Block() as block:
            @block.sync
            def _(sp):
                for n in free_1:
                    sp.sem_inc(s1[n].sem, 1)

                def load_xT(b):
                    sp.dma_start(A1["xT"], dr["xT"][b].rearrange("(k p) t -> p k t", p=P)).then_inc(s1["xT_in"].sem, 16)

                def load(dst, src):
                    sp.dma_start(dst, src).then_inc(loaded.sem, 16)
                    n_loads[0] += 1

                load_xT(0)
                sp.dma_start(qkv_w[:], dr["qkv_wT"].rearrange("(k p) n -> p k n", p=P)).then_inc(first_loaded.sem, 16)
                sp.dma_start(conv_w[:], dr["conv_w"].rearrange("(m p) j -> p m j", p=P)).then_inc(first_loaded.sem, 16)
                sp.dma_start(short_w[:], dr["fir_s"].rearrange("(k p) j -> p k j", p=P)).then_inc(first_loaded.sem, 16)
                sp.dma_start(ident[:], dr["c_ident"]).then_inc(first_loaded.sem, 16)
                load(beta_w[:], dr["b_wT"].rearrange("(k p) n -> p k n", p=P))
                for n in const:
                    if n != "ident":
                        load(const[n][:], dr["c_" + n])
                load(g1x_w[:], dr["g1x_wT"].rearrange("(k p) n -> p k n", p=P))
                sp.wait_ge(s1["pads"].sem, 5)
                load(g1s_w[0:36, :], dr["g1s_wT"][0:36, :])
                load(g1s_w[64:88, :], dr["g1s_wT"][36:60, :])
                load(g1_bias[:], dr["g1_b"])
                load(g2_w[:], dr["g2_wT"].rearrange("(k p) n -> p k n", p=P))
                load(onorm[0:DK, :], dr["onorm"].rearrange("(p a) -> p a", a=1))
                load(onorm[DK:P, :], dr["onorm"].rearrange("(p a) -> p a", a=1))
                load(ow_w[:], dr["o_wT"].rearrange("(k p) n -> p k n", p=P))
                load(xq_b[:], dr["xq_b"].rearrange("(a n) -> a n", a=1))
                load(xkv_b[:], dr["xkv_b"].rearrange("(a n) -> a n", a=1))
                load(xo_b[:], dr["xo_b"].partition_broadcast(P))
                load(g2_bias[:], dr["g2_b"].partition_broadcast(P))
                load(gate_par[:, :, :].rearrange("p a h -> p (a h)"), dr["gate_par"].partition_broadcast(P))
                with sp.Fori(0, B - 1) as b:
                    sp.wait_ge(s1["proj"].sem, s1["proj"].at(b, 2))
                    load_xT(b + 1)

            @block.tensor
            def _(pe):
                def project(b):
                    pe.wait_ge(s1["xT_in"].sem, s1["xT_in"].at(b, 16))
                    for m in range(KT):
                        for k in range(KT):
                            i = nc.tensor.matmul(bank[m][:], qkv_w[:, k, (m + 4) * P:(m + 5) * P], A1["xT"][:, k, :],
                                                 start=(k == 0), stop=(k == KT - 1))
                        i.then_inc(s1["proj"].sem, 1)

                def turn(b, more):
                    pe.wait_ge(s1["silu"].sem, s1["silu"].at(b, 2))
                    for w in range(4):
                        pe.wait_ge(s1["v_out"].sem, s1["v_out"].at(b, w - 3) if w == 3 else s1["v_out"].at(b, 0))
                        for j in range(2):
                            for k in range(KT):
                                c = (2 * w + j) * DK
                                i = nc.tensor.transpose(bank[4 + w][:, j * D + k * P:j * D + (k + 1) * P],
                                                        A1["vT"][:, k, c:c + P], ident[:])
                        i.then_inc(s1["v_turned"].sem, 1)
                    if more:
                        pe.wait_ge(s1["conv"].sem, s1["conv"].at(b, 6))
                        project(b + 1)
                    pe.wait_ge(s1["sh_conv"].sem, s1["sh_conv"].at(b, 6))
                    pe.wait_ge(s1["sh_out"].sem, s1["sh_out"].at(b, 0))
                    for i2 in range(2):
                        for t in range(2):
                            for k in range(KT):
                                i = nc.tensor.transpose(bank[2 + i2][:, t * D + k * P:t * D + (k + 1) * P],
                                                        A1["sh"][:, k, (2 * i2 + t) * P:(2 * i2 + t + 1) * P], ident[:])
                        i.then_inc(s1["sh_turned"].sem, 1)

                pe.wait_ge(first_loaded.sem, 16 * 4)
                pe.wait_ge(s1["pads"].sem, 5)
                project(0)
                with pe.Fori(0, B - 1) as b:
                    turn(b, True)
                turn(B - 1, False)

            @block.scalar
            def _(act):
                a = nc.scalar.activation
                act.wait_ge(first_loaded.sem, 16 * 4)
                with act.Fori(0, B) as b:
                    for m in range(KT):
                        act.wait_ge(s1["proj"].sem, s1["proj"].at(b, m + 1))
                        a(A1["acc"][:, m, :], bank[m][:], ACT.Copy, scale=conv_w[:, m + 4, CONV_K - 1:CONV_K])\
                            .then_inc(s1["tap_last"].sem, 1)
                    for m in range(KT):
                        act.wait_ge(s1["conv"].sem, s1["conv"].at(b, 3 * m + 3))
                        a(A1["vT"][:, m, DK:], A1["acc"][:, m, :], ACT.Silu).then_inc(s1["silu"].sem, 1)
                    for w in range(4):
                        act.wait_ge(s1["v_turned"].sem, s1["v_turned"].at(b, w + 1))
                        nc.scalar.copy(v_win[:, bass.ds(b * NJ + 2 * w, 2), :],
                                       bank[4 + w][:].rearrange("p (t c) -> p t c", t=2)).then_inc(s1["v_out"].sem, 1)
                    for i2 in range(2):
                        act.wait_ge(s1["sh_turned"].sem, s1["sh_turned"].at(b, i2 + 1))
                        nc.scalar.copy(short[:, bass.ds(b * TT + 2 * i2, 2), :],
                                       bank[2 + i2][:].rearrange("p (t c) -> p t c", t=2)).then_inc(s1["sh_out"].sem, 1)
                act.wait_ge(loaded.sem, 16 * n_loads[0])
                a(inv_temp[:], gate_par[:, 1, :], ACT.Exp, scale=-1.0).then_inc(ready.sem, 1)
                a(floor[:], gate_par[:, 2, :], ACT.Tanh, scale=0.5).then_inc(ready.sem, 1)

            @block.vector
            def _(dve):
                v = nc.vector
                v.memset(g1s_w[32:64, :], 0.0).then_inc(s1["pads"].sem, 1)
                dve.wait_ge(first_loaded.sem, 16 * 4)
                dve.wait_ge(s1["pads"].sem, 5)
                with dve.Fori(0, B) as b:
                    for m in range(KT):
                        for j in range(1, CONV_K):
                            if j == 1:
                                dve.wait_ge(s1["tap_last"].sem, s1["tap_last"].at(b, m + 1))
                            else:
                                dve.wait_ge(s1["conv"].sem, s1["conv"].at(b, 3 * m + j - 1))
                            tap_one(nc, A1["acc"][:, m, :], bank[m], m + 4, j).then_inc(s1["conv"].sem, 1)
                    dve.wait_ge(s1["silu"].sem, s1["silu"].at(b, 2))
                    for k in range(KT):
                        for j in range(FIR_S):
                            src = A1["vT"][:, k, DK - j:DK - j + L]
                            w = short_w[:, k, FIR_S - 1 - j:FIR_S - j]
                            if j == 0:
                                dve.wait_ge(s1["sh_out"].sem, s1["sh_out"].at(b, 0))
                                v.tensor_scalar(A1["sh"][:, k, :], src, w, None, ALU.mult).then_inc(s1["sh_conv"].sem, 1)
                                continue
                            dve.wait_ge(s1["sh_conv"].sem, s1["sh_conv"].at(b, FIR_S * k + j))
                            v.scalar_tensor_tensor(out=A1["sh"][:, k, :], in0=src, scalar=w, in1=A1["sh"][:, k, :],
                                                   op0=ALU.mult, op1=ALU.add).then_inc(s1["sh_conv"].sem, 1)
                dve.wait_ge(loaded.sem, 16 * n_loads[0])
                dve.wait_ge(ready.sem, 2)
                v.tensor_copy(inv_temp5[:], over_last(inv_temp[:], NG)).then_inc(ready.sem, 1)
                v.tensor_scalar(floor[:], floor[:], 0.5, 0.5, ALU.mult, ALU.add).then_inc(ready.sem, 1)
                dve.wait_ge(ready.sem, 4)
                v.tensor_scalar(keep[:], floor[:], -4.0, 1.0, ALU.mult, ALU.add).then_inc(ready.sem, 1)
                g2b = g2_bias[:].rearrange("p (h g) -> p h g", g=NG)
                v.tensor_tensor(g2b[:, :, NG - 1], g2b[:, :, NG - 1], gate_par[:, 0, :], ALU.add).then_inc(ready.sem, 1)

            @block.gpsimd
            def _(pool):
                g = nc.gpsimd
                g.memset(A1["vT"][:, 0, 0:DK], 0.0).then_inc(s1["pads"].sem, 1)
                g.memset(A1["vT"][:, 1, 0:DK], 0.0).then_inc(s1["pads"].sem, 1)
                g.memset(half_exp[:, 0, :], -0.5).then_inc(s1["pads"].sem, 1)
                g.memset(half_exp[:, 1, :], 0.5).then_inc(s1["pads"].sem, 1)

        WL = B * NJ * D
        wl = arena[:, 0:WL].rearrange("p (j c) -> p j c", c=D)
        TOEP = 2 * DK * PIECE
        toep = [arena[:, WL + i * TOEP:WL + (i + 1) * TOEP].rearrange("p (f c) -> p f c", c=PIECE) for i in range(TOEP_BUFS)]
        A2 = carve(arena, {
            "xT": (KT, L), "acc": (4, L), "qT": (KT, L), "kT": (KT, L), "k_tok": (TT, D), "v_sc": (TT, D),
            "AL": (TT, H, P), "ALT": (TT, H, P), "atT": (TT, H, P), "X": (TT, H, P), "R": (D,), "U": (D,),
            "S": (2, KT, P), "ss": (32,), "rn": (2, TT, H), "rec": (16,), "th": (16,), "C": (TT, H)},
            at=WL + TOEP_BUFS * TOEP)
        A2["XT"] = A2["AL"]
        A2["sq"] = A2["ALT"].rearrange("p t h c -> p t (h c)")
        A2["Z"] = A2["acc"][:, 0:2, :].rearrange("p a c -> p (a c)").rearrange("p (t h c) -> p t h c", t=TT, h=H)
        free_2 = ("o_out",)
        s2 = signals(2, {
            "xT_in": 16, "proj": 4, "tap_last": 4, "conv": 12, "silu": 4, "squares": 4, "beta_mm": 1, "ssq_mm": 1,
            "k_turned": 2, "k_out": 2, "beta_th": 1, "ss_eps": 1, "norms": 1, "c_steps": 3, "gram": 4, "a_scaled": 16,
            "attn_mm": 4, "attn_out": 8, "v_scaled": 1, "x_first": 8, "a_turned": 4, "at_out": 4, "z_mm": 12,
            "z_out": 12, "w_mm": 12, "x_out": 12, "x_turned": 28, "xt_out": 24, "xt_last": 4, "ks_mm": 3, "r_out": 3,
            "u_mm": 4, "u_out": 4, "s_mm": 3, "s_out": 3, "o_mm": 4, "o_out": 4, "fir_mm": PER_BATCH,
            "fir_out": PER_BATCH}, free_2)
        toep_in = [Signal(ctx.enter_context(nc.semaphore(f"toep_in{i}")), 32 * PER_BATCH // TOEP_BUFS)
                   for i in range(TOEP_BUFS)]
        TURN_BANKS = (2, 6, 7)
        turn_bank = lambda i: bank[TURN_BANKS[i % 3]]
        pair_half = lambda first, t: bank[first + t // 2][:, (t % 2) * D:(t % 2 + 1) * D]

        def evens(ap, k):
            return ap.rearrange("p h (g two s) -> p (h g) two s", two=2, s=1 << k)[:, :, 0, :]

        with nc.Block() as block:
            @block.sync
            def _(sp):
                for n in free_2:
                    sp.sem_inc(s2[n].sem, 1)

                def load_xT(b):
                    sp.dma_start(A2["xT"], dr["xT"][b].rearrange("(k p) t -> p k t", p=P)).then_inc(s2["xT_in"].sem, 16)

                def load_toep(i, piece):
                    for f in range(2):
                        src = dr[("toep_w", "toep_l")[f]][piece]
                        src = bass.AP(src.tensor, src.offset, [[PIECE, P], [1, DK * PIECE]])
                        sp.dma_start(toep[i][:, f * DK:(f + 1) * DK, :].rearrange("p f c -> p (f c)"), src)\
                            .then_inc(toep_in[i].sem, 16)

                def round_(b, more):
                    if more:
                        sp.wait_ge(s2["beta_mm"].sem, s2["beta_mm"].at(b, 1))
                        load_xT(b + 1)
                    for n in range(PER_BATCH):
                        if more or n + TOEP_BUFS < PER_BATCH:
                            sp.wait_ge(s2["fir_mm"].sem, s2["fir_mm"].at(b, n + 1))
                            load_toep(n % TOEP_BUFS, b * PER_BATCH + (n + TOEP_BUFS))

                load_xT(0)
                for n in range(TOEP_BUFS):
                    load_toep(n, n)
                with sp.Fori(0, B - 1) as b:
                    round_(b, True)
                round_(B - 1, False)

            @block.tensor
            def _(pe):
                mm = nc.tensor.matmul

                def project(b, m):
                    if m == 0:
                        pe.wait_ge(s2["xT_in"].sem, s2["xT_in"].at(b, 16))
                    if m >= 2:
                        pe.wait_ge(s2["conv"].sem, s2["conv"].at(b, 3 * (m - 1)))
                    for k in range(KT):
                        i = mm(bank[m % 2][:], qkv_w[:, k, m * P:(m + 1) * P], A2["xT"][:, k, :],
                               start=(k == 0), stop=(k == KT - 1))
                    i.then_inc(s2["proj"].sem, 1)

                def beta(b):
                    for t in range(TT):
                        for k in range(KT):
                            i = mm(bank[2][:, t * H:(t + 1) * H], A2["xT"][:, k, t * P:(t + 1) * P], beta_w[:, k, :],
                                   start=(k == 0), stop=(k == KT - 1))
                    i.then_inc(s2["beta_mm"].sem, 1)

                def filter_piece(b, n):
                    pe.wait_ge(toep_in[n % TOEP_BUFS].sem, toep_in[n % TOEP_BUFS].at(b, 32 * (n // TOEP_BUFS + 1)))
                    if n:
                        pe.wait_ge(s2["fir_out"].sem, s2["fir_out"].at(b, n))
                    for c in range(PIECE):
                        i = mm(bank[3][:, c * B * NJ:(c + 1) * B * NJ], toep[n % TOEP_BUFS][:, :, c],
                               v_win[:, :, b * (PER_BATCH * PIECE) + (n * PIECE + c)], start=True, stop=True)
                    i.then_inc(s2["fir_mm"].sem, 1)

                def turn_free(b, i):
                    i -= 3
                    if i < 0:
                        pe.wait_ge(s2["a_scaled"].sem, s2["a_scaled"].at(b, H * TT))
                        return
                    if i < TT:
                        pe.wait_ge(s2["at_out"].sem, s2["at_out"].at(b, i + 1))
                    elif i < TT + 24:
                        pe.wait_ge(s2["xt_out"].sem, s2["xt_out"].at(b, i + 1 - TT))
                    else:
                        pe.wait_ge(s2["xt_last"].sem, s2["xt_last"].at(b, i + 1 - TT - 24))

                def turn_x(b, k, t):
                    n = TT * k + t
                    if k == 0:
                        pe.wait_ge(s2["x_first"].sem, s2["x_first"].at(b, 2 * t + 2))
                    else:
                        pe.wait_ge(s2["x_out"].sem, s2["x_out"].at(b, n // 2 - 1))
                    turn_free(b, TT + n)
                    for h in range(H):
                        i = nc.tensor.transpose(turn_bank(TT + n)[:, h * P:(h + 1) * P], A2["X"][:, t, h, :], ident[:])
                    i.then_inc(s2["x_turned"].sem, 1)

                def round_(b, more):
                    filter_piece(b, 0)
                    pe.wait_ge(s2["silu"].sem, s2["silu"].at(b, 2))
                    pe.wait_ge(s2["o_out"].sem, s2["o_out"].at(b, 0))
                    for i2 in range(2):
                        for t in range(2):
                            for k in range(KT):
                                i = nc.tensor.transpose(bank[4 + i2][:, t * D + k * P:t * D + (k + 1) * P],
                                                        A2["kT"][:, k, (2 * i2 + t) * P:(2 * i2 + t + 1) * P], ident[:])
                        i.then_inc(s2["k_turned"].sem, 1)
                    pe.wait_ge(s2["squares"].sem, s2["squares"].at(b, 4))
                    pe.wait_ge(s2["beta_th"].sem, s2["beta_th"].at(b, 1))
                    for m in range(4):
                        for t in range(TT):
                            c = 16 + 16 * (1 - m // 2) + t * H + 2 * (m % 2)
                            i = mm(bank[2][:, c:c + 2], A2["sq"][:, m, t * P:(t + 1) * P], const["heads"][:],
                                   start=True, stop=True)
                    i.then_inc(s2["ssq_mm"].sem, 1)
                    pe.wait_ge(s2["k_out"].sem, s2["k_out"].at(b, 2))
                    for t in range(TT):
                        if t >= 2:
                            pe.wait_ge(s2["a_scaled"].sem, s2["a_scaled"].at(b, H * (t - 1)))
                        for h in range(H):
                            r, k = DK * (h % 2), h // 2
                            kk = A2["kT"][r:r + DK, k, t * P:(t + 1) * P]
                            i = mm(bank[4 + 2 * (t % 2) + h % 2][:, k * P:(k + 1) * P], kk, kk, start=True, stop=True)
                        i.then_inc(s2["gram"].sem, 1)
                        if t:
                            pe.wait_ge(s2["attn_out"].sem, s2["attn_out"].at(b, 2 * t))
                        for h in range(H):
                            r, k = DK * (h % 2), h // 2
                            i = mm(bank[h % 2][:, k * P:(k + 1) * P], A2["kT"][r:r + DK, k, t * P:(t + 1) * P],
                                   A2["qT"][r:r + DK, k, t * P:(t + 1) * P], start=True, stop=True)
                        i.then_inc(s2["attn_mm"].sem, 1)
                    for t in range(TT):
                        pe.wait_ge(s2["a_scaled"].sem, s2["a_scaled"].at(b, H * (t + 1)))
                        turn_free(b, t)
                        for h in range(H):
                            i = nc.tensor.transpose(turn_bank(t)[:, h * P:(h + 1) * P], A2["AL"][:, t, h, :], ident[:])
                        i.then_inc(s2["a_turned"].sem, 1)
                    filter_piece(b, 1)
                    for k in range(1, LEVELS):
                        for t in range(TT):
                            n = TT * (k - 1) + t
                            if k == 1:
                                pe.wait_ge(s2["x_first"].sem, s2["x_first"].at(b, 2 * t + 2))
                                pe.wait_ge(s2["at_out"].sem, s2["at_out"].at(b, t + 1))
                                pe.wait_ge(s2["attn_out"].sem, s2["attn_out"].at(b, 2 * TT))
                            else:
                                pe.wait_ge(s2["x_out"].sem, s2["x_out"].at(b, n // 2 - 1))
                            for h in range(H):
                                i = mm(pair_half(0, t)[:, h * DK:(h + 1) * DK], A2["ALT"][:, t, h, :],
                                       A2["X"][:, t, h, :].rearrange("p (g two s) -> p g two s", two=2, s=1 << k)[:, :, 0, :],
                                       start=True, stop=True)
                            if t % 2:
                                i.then_inc(s2["z_mm"].sem, 1)
                                turn_x(b, k - 1, t - 1)
                                turn_x(b, k - 1, t)
                        for t in range(TT):
                            n = TT * (k - 1) + t
                            pe.wait_ge(s2["z_out"].sem, s2["z_out"].at(b, n // 2 + 1))
                            pe.wait_ge(s2["xt_out"].sem, s2["xt_out"].at(b, n + 1))
                            for h in range(H):
                                i = mm(pair_half(4, t)[:, h * DK:(h + 1) * DK], A2["XT"][:, t, h, :], A2["Z"][:, t, h, :],
                                       start=True, stop=True)
                            if t % 2:
                                i.then_inc(s2["w_mm"].sem, 1)
                        filter_piece(b, 1 + k)
                    for t in range(TT):
                        turn_x(b, LEVELS - 1, t)
                    for t in range(TT):
                        tok = slice(t * P, (t + 1) * P)
                        if more:
                            project(b + 1, t)
                        if t:
                            pe.wait_ge(s2["s_out"].sem, s2["s_out"].at(b, t))
                            for p in range(KT):
                                i = mm(bank[2][:, p * P:(p + 1) * P], A2["kT"][:, p, tok], A2["S"][:, t % 2, p, :],
                                       start=True, stop=True)
                            i.then_inc(s2["ks_mm"].sem, 1)
                            pe.wait_ge(s2["r_out"].sem, s2["r_out"].at(b, t))
                            pe.wait_ge(s2["u_out"].sem, s2["u_out"].at(b, t))
                        else:
                            pe.wait_ge(s2["v_scaled"].sem, s2["v_scaled"].at(b, 1))
                            pe.wait_ge(s2["x_out"].sem, s2["x_out"].at(b, 12))
                        pe.wait_ge(s2["xt_last"].sem, s2["xt_last"].at(b, t + 1))
                        rhs = A2["R"] if t else A2["v_sc"][:, 0, :]
                        for h in range(H):
                            i = mm(bank[4][:, h * DK:(h + 1) * DK], A2["XT"][:, t, h, :], rhs[:, h * DK:(h + 1) * DK],
                                   start=True, stop=True)
                        i.then_inc(s2["u_mm"].sem, 1)
                        pe.wait_ge(s2["u_out"].sem, s2["u_out"].at(b, t + 1))
                        if t < TT - 1:
                            for p in range(KT):
                                i = mm(bank[5][:, p * P:(p + 1) * P], A2["k_tok"][:, t, p * P:(p + 1) * P],
                                       A2["U"][:, p * P:(p + 1) * P], start=(t == 0 and p == 0),
                                       stop=(t == TT - 2 and p == KT - 1), skip_group_check=True)
                            i.then_inc(s2["s_mm"].sem, 1)
                        if t >= 2:
                            pe.wait_ge(s2["o_out"].sem, s2["o_out"].at(b, t - 1))
                        else:
                            pe.wait_ge(s2["xt_last"].sem, s2["xt_last"].at(b, TT))
                        if t:
                            for p in range(KT):
                                mm(bank[6 + t % 2][:, p * P:(p + 1) * P], A2["qT"][:, p, tok], A2["S"][:, t % 2, p, :],
                                   start=(p == 0), stop=False, skip_group_check=True)
                        for h in range(H):
                            i = mm(bank[6 + t % 2][:, h * DK:(h + 1) * DK], A2["atT"][:, t, h, :],
                                   A2["U"][:, h * DK:(h + 1) * DK], start=(t == 0 and h == 0), stop=(h == H - 1),
                                   skip_group_check=True)
                        i.then_inc(s2["o_mm"].sem, 1)
                    pe.wait_ge(s2["fir_out"].sem, s2["fir_out"].at(b, PER_BATCH))
                    if more:
                        beta(b + 1)

                for m in range(4):
                    project(0, m)
                beta(0)
                with pe.Fori(0, B - 1) as b:
                    round_(b, True)
                round_(B - 1, False)

            @block.scalar
            def _(act):
                a = nc.scalar.activation

                def tap_last(b, m):
                    act.wait_ge(s2["proj"].sem, s2["proj"].at(b, m + 1))
                    a(A2["acc"][:, m, :], bank[m % 2][:], ACT.Copy, scale=conv_w[:, m, CONV_K - 1:CONV_K])\
                        .then_inc(s2["tap_last"].sem, 1)

                def filter_out(b, n):
                    act.wait_ge(s2["fir_mm"].sem, s2["fir_mm"].at(b, n + 1))
                    nc.scalar.copy(wl[:, :, bass.ds(b * (PER_BATCH * PIECE) + n * PIECE, PIECE)],
                                   bank[3][:, 0:D].rearrange("p (c j) -> p j c", c=PIECE)).then_inc(s2["fir_out"].sem, 1)

                def beta_tanh(b):
                    act.wait_ge(s2["beta_mm"].sem, s2["beta_mm"].at(b, 1))
                    a(A2["th"], bank[2][:, 0:16], ACT.Tanh, scale=0.5).then_inc(s2["beta_th"].sem, 1)

                def round_(b, more):
                    act.wait_ge(s2["o_out"].sem, s2["o_out"].at(b, 0))
                    for half in range(2):
                        for m in (2 * half, 2 * half + 1):
                            act.wait_ge(s2["conv"].sem, s2["conv"].at(b, 3 * m + 3))
                            a([A2["kT"], A2["qT"]][half][:, m % 2, :], A2["acc"][:, m, :], ACT.Silu)\
                                .then_inc(s2["silu"].sem, 1)
                        for m in (2 * half, 2 * half + 1):
                            act.wait_ge(s2["silu"].sem, s2["silu"].at(b, m + 1))
                            a(A2["sq"][:, m, :], [A2["kT"], A2["qT"]][half][:, m % 2, :],
                              ACT.Square).then_inc(s2["squares"].sem, 1)
                    for i2 in range(2):
                        act.wait_ge(s2["k_turned"].sem, s2["k_turned"].at(b, i2 + 1))
                        nc.scalar.copy(A2["k_tok"][:, 2 * i2:2 * i2 + 2, :],
                                       bank[4 + i2][:].rearrange("p (t c) -> p t c", t=2)).then_inc(s2["k_out"].sem, 1)
                    filter_out(b, 0)
                    for t in range(TT):
                        act.wait_ge(s2["a_turned"].sem, s2["a_turned"].at(b, t + 1))
                        nc.scalar.copy(A2["ALT"][:, t, :, :], turn_bank(t)[:].rearrange("p (h c) -> p h c", h=H))\
                            .then_inc(s2["at_out"].sem, 1)
                    for n in range(TT * (LEVELS - 1)):
                        if n % TT == 0:
                            filter_out(b, n // TT + 1)
                        act.wait_ge(s2["x_turned"].sem, s2["x_turned"].at(b, n + 1))
                        nc.scalar.copy(A2["XT"][:, n % TT, :, :], turn_bank(TT + n)[:].rearrange("p (h c) -> p h c", h=H))\
                            .then_inc(s2["xt_out"].sem, 1)
                    filter_out(b, PER_BATCH - 1)
                    if more:
                        act.wait_ge(s2["w_mm"].sem, s2["w_mm"].at(b, 12))
                    for t in range(TT):
                        if more:
                            tap_last(b + 1, t)
                        act.wait_ge(s2["u_mm"].sem, s2["u_mm"].at(b, t + 1))
                        nc.scalar.copy(A2["U"], bank[4][:, 0:D]).then_inc(s2["u_out"].sem, 1)
                    if more:
                        beta_tanh(b + 1)

                for m in range(4):
                    tap_last(0, m)
                beta_tanh(0)
                with act.Fori(0, B - 1) as b:
                    round_(b, True)
                round_(B - 1, False)

            @block.vector
            def _(dve):
                v = nc.vector

                def conv(b, m):
                    for j in range(1, CONV_K):
                        if j == 1:
                            dve.wait_ge(s2["tap_last"].sem, s2["tap_last"].at(b, m + 1))
                        else:
                            dve.wait_ge(s2["conv"].sem, s2["conv"].at(b, 3 * m + j - 1))
                        tap_one(nc, A2["acc"][:, m, :], bank[m % 2], m, j).then_inc(s2["conv"].sem, 1)

                def round_(b, more):
                    dve.wait_ge(s2["beta_th"].sem, s2["beta_th"].at(b, 1))
                    v.tensor_scalar(A2["th"], A2["th"], 0.5, 0.5, ALU.mult, ALU.add).then_inc(s2["c_steps"].sem, 1)
                    dve.wait_ge(s2["ssq_mm"].sem, s2["ssq_mm"].at(b, 1))
                    v.tensor_scalar(A2["ss"], bank[2][:, 16:48], 1e-6, None, ALU.add).then_inc(s2["ss_eps"].sem, 1)
                    dve.wait_ge(s2["ss_eps"].sem, s2["ss_eps"].at(b, 1))
                    v.reciprocal(A2["rec"], A2["ss"][:, 16:32]).then_inc(s2["c_steps"].sem, 1)
                    dve.wait_ge(s2["c_steps"].sem, s2["c_steps"].at(b, 2))
                    v.tensor_tensor(A2["C"].rearrange("p t h -> p (t h)"), A2["rec"], A2["th"],
                                    ALU.mult).then_inc(s2["c_steps"].sem, 1)
                    dve.wait_ge(s2["c_steps"].sem, s2["c_steps"].at(b, 3))
                    for t in range(TT):
                        dve.wait_ge(s2["gram"].sem, s2["gram"].at(b, t + 1))
                        for h in range(H):
                            v.scalar_tensor_tensor(out=A2["AL"][:, t, h, :],
                                                   in0=bank[4 + 2 * (t % 2) + h % 2][:, (h // 2) * P:(h // 2 + 1) * P],
                                                   scalar=A2["C"][:, t, h:h + 1], in1=const["mask_lower"][:],
                                                   op0=ALU.mult, op1=ALU.mult).then_inc(s2["a_scaled"].sem, 1)
                        dve.wait_ge(s2["attn_mm"].sem, s2["attn_mm"].at(b, t + 1))
                        for e in range(2):
                            v.tensor_tensor(A2["atT"][:, t, e::2, :], bank[e][:, 0:D].rearrange("p (h c) -> p h c", h=2),
                                            over_tiles(const["mask_upper"][:], 2), ALU.mult).then_inc(s2["attn_out"].sem, 1)
                        dve.wait_ge(s2["a_scaled"].sem, s2["a_scaled"].at(b, H * (t + 1)))
                        v.tensor_tensor(A2["X"][:, t, :, :], A2["AL"][:, t, :, :], over_tiles(const["level0"][:], H),
                                        ALU.mult).then_inc(s2["x_first"].sem, 1)
                        dve.wait_ge(s2["x_first"].sem, s2["x_first"].at(b, 2 * t + 1))
                        v.tensor_tensor(A2["X"][:, t, :, :], A2["X"][:, t, :, :], over_tiles(ident[:], H),
                                        ALU.add).then_inc(s2["x_first"].sem, 1)
                    for k in range(1, LEVELS):
                        for i in range(2):
                            dve.wait_ge(s2["z_mm"].sem, s2["z_mm"].at(b, 2 * k - 1 + i))
                            v.tensor_tensor(A2["Z"][:, 2 * i:2 * i + 2, :, :].rearrange("p t h c -> p (t h) c"),
                                            bank[i][:].rearrange("p (g c) -> p g c", c=DK),
                                            over_tiles(levels[:, k - 1, :], 2 * H), ALU.mult).then_inc(s2["z_out"].sem, 1)
                        for i in range(2):
                            dve.wait_ge(s2["w_mm"].sem, s2["w_mm"].at(b, 2 * k - 1 + i))
                            x = evens(A2["X"][:, 2 * i:2 * i + 2, :, :].rearrange("p t h c -> p (t h) c"), k)
                            v.tensor_tensor(x, x, bank[4 + i][:].rearrange("p (g s) -> p g s", s=1 << k),
                                            ALU.subtract).then_inc(s2["x_out"].sem, 1)
                    for t in range(TT):
                        dve.wait_ge(s2["x_turned"].sem, s2["x_turned"].at(b, TT * (LEVELS - 1) + t + 1))
                        v.tensor_tensor(A2["XT"][:, t, :, :], turn_bank(TT * LEVELS + t)[:].rearrange("p (h c) -> p h c", h=H),
                                        over_last(A2["C"][:, t, :], P), ALU.mult).then_inc(s2["xt_last"].sem, 1)
                    for t in range(TT):
                        if t:
                            dve.wait_ge(s2["ks_mm"].sem, s2["ks_mm"].at(b, t))
                            v.tensor_tensor(A2["R"], A2["v_sc"][:, t, :], bank[2][:, 0:D],
                                            ALU.subtract).then_inc(s2["r_out"].sem, 1)
                        if more:
                            conv(b + 1, t)
                        if t < TT - 1:
                            dve.wait_ge(s2["s_mm"].sem, s2["s_mm"].at(b, t + 1))
                            v.tensor_tensor(A2["S"][:, (t + 1) % 2, :, :], bank[5][:, 0:D].rearrange("p (k c) -> p k c", k=KT),
                                            over_tiles(const["blocks"][:], KT), ALU.mult).then_inc(s2["s_out"].sem, 1)
                        if t == 0:
                            dve.wait_ge(s2["norms"].sem, s2["norms"].at(b, 1))
                        dve.wait_ge(s2["o_mm"].sem, s2["o_mm"].at(b, t + 1))
                        v.tensor_tensor(delta[:, b * TT + t, :].rearrange("p (h c) -> p h c", h=H),
                                        bank[6 + t % 2][:, 0:D].rearrange("p (h c) -> p h c", h=H),
                                        over_last(A2["rn"][:, 0, t, :], DK), ALU.mult).then_inc(s2["o_out"].sem, 1)

                for m in range(4):
                    conv(0, m)
                with dve.Fori(0, B - 1) as b:
                    round_(b, True)
                round_(B - 1, False)

            @block.gpsimd
            def _(pool):
                g = nc.gpsimd
                with pool.Fori(0, B) as b:
                    pool.wait_ge(s2["ss_eps"].sem, s2["ss_eps"].at(b, 1))
                    g.tensor_tensor(A2["rn"].rearrange("p a t h -> p (a t h)"), A2["ss"],
                                    half_exp[:, :, :].rearrange("p a n -> p (a n)"), ALU.pow).then_inc(s2["norms"].sem, 1)
                    pool.wait_ge(s2["norms"].sem, s2["norms"].at(b, 1))
                    g.tensor_tensor(A2["v_sc"].rearrange("p t (h c) -> p t h c", h=H),
                                    v_tiles[:, bass.ds(b * TT, TT), 1, :].rearrange("p t (h c) -> p t h c", h=H),
                                    over_last(A2["rn"][:, 1, :, :], DK), ALU.mult).then_inc(s2["v_scaled"].sem, 1)

        A3 = carve(arena, {
            "xT": (KT, L), "x": (TT, D), "st": (TT * 3, 3, H), "tw": (NJ, 3, H), "sw": (NJ, 24), "statT": (L,),
            "hdnT": (GH // P, L), "lg": (TT, H, NG), "mx": (TT, H), "w": (TT, H, NG), "wsel": (2, TT, H),
            "sqb": (2, 2048), "pwl": (TT, 2, D), "pv": (TT, D), "ps": (TT, D), "ssh": (TT * H,),
            "rh": (TT * H,), "ln": (TT, 6), "mv": (TT, 2), "ve": (TT,), "rs": (TT,)}, at=B * NJ * D)
        on, onT, xr = A3["pv"], A3["pwl"].rearrange("p t a c -> p (t a c)")[:, 0:KT * L].rearrange("p (k t) -> p k t", k=KT), A3["ps"]
        free_3 = ("hdn_mm", "lg_steps", "oT_out", "o_norm", "sq_used", "res", "w_sel")
        s3 = signals(3, {
            "x3_in": 32, "sq_out": 4, "red": 8, "sq_used": 4, "small": 4, "roots": 2, "sw_out": 2, "st_turned": 2, "st_out": 2,
            "hdn_mm": 4, "gelu": 4, "lg_mm": 1, "lg_steps": 9, "lg_exp": 1, "w_twice": 1, "w_sel": 2, "p_wl": 2,
            "p_v": 1, "p_sum": 4, "mix_mm": 2, "mix_sq": 2, "mix_ss": 3, "r_head": 1, "o_norm": 2, "o_turned": 2,
            "oT_out": 2, "y_mm": 2, "res": 2, "ln_st": 9, "ln_rs": 1, "x1_out": 4, "zeros3": 0}, free_3)

        def branch(n, b):
            if n == 0:
                src = wl[:, bass.ds(b * NJ, NJ), :]
            elif n == 3:
                src = v_tiles[:, bass.ds(b * TT, TT), 1, :]
            else:
                src = [short, delta][n - 1][:, bass.ds(b * TT, TT), :]
            return src.rearrange("p t (h c) -> p t h c", h=H)

        def stat(n, s):
            if n == 0:
                return A3["tw"][:, :, s, :]
            return A3["st"].rearrange("p (t r) s h -> p t r s h", r=3)[:, :, n - 1, s, :]

        with nc.Block() as block:
            @block.sync
            def _(sp):
                for n in free_3:
                    sp.sem_inc(s3[n].sem, 1)
                with sp.Fori(0, B) as b:
                    sp.wait_ge(s3["hdn_mm"].sem, s3["hdn_mm"].at(b, 0))
                    sp.dma_start(A3["xT"], dr["xT"][b].rearrange("(k p) t -> p k t", p=P)).then_inc(s3["x3_in"].sem, 16)
                    sp.wait_ge(s3["res"].sem, s3["res"].at(b, 0))
                    sp.dma_start(A3["x"], dr["x"][b].rearrange("(t p) d -> p t d", p=P)).then_inc(s3["x3_in"].sem, 16)
                sp.wait_ge(s3["p_v"].sem, s3["p_v"].at(B, 0))
                for n in LATE_CONST:
                    sp.dma_start(late[n].rearrange("p k f -> p (k f)"), dr["c_" + n]).then_inc(late_loaded.sem, 16)
                for n in ("xq_w", "xkv_w", "xo_w"):
                    sp.dma_start(late[n], dr[n + "T"].rearrange("(k p) n -> p k n", p=P)).then_inc(late_loaded.sem, 16)

            @block.tensor
            def _(pe):
                mm = nc.tensor.matmul
                pe.wait_ge(s3["zeros3"].sem, 2)
                with pe.Fori(0, B) as b:
                    pe.wait_ge(s3["sw_out"].sem, s3["sw_out"].at(b, 2))
                    pe.wait_ge(s3["roots"].sem, s3["roots"].at(b, 2))
                    pe.wait_ge(s3["oT_out"].sem, s3["oT_out"].at(b, 0))
                    for j in range(NJ):
                        i = mm(bank[1][64:88, j * DK:(j + 1) * DK], A3["sw"][:, j, :], const["fold"][:],
                               start=True, stop=True)
                    i.then_inc(s3["st_turned"].sem, 1)
                    for t in range(TT):
                        i = nc.tensor.transpose(bank[0][0:36, t * P:(t + 1) * P],
                                                A3["st"][:, 3 * t:3 * t + 3, :, :].rearrange("p r s h -> p (r s h)"), ident[:])
                    i.then_inc(s3["st_turned"].sem, 1)
                    pe.wait_ge(s3["st_out"].sem, s3["st_out"].at(b, 2))
                    pe.wait_ge(s3["x3_in"].sem, s3["x3_in"].at(b, 32))
                    pe.wait_ge(s3["res"].sem, s3["res"].at(b, 0))
                    for m in range(GH // P):
                        if m >= 2:
                            pe.wait_ge(s3["gelu"].sem, s3["gelu"].at(b, m - 1))
                        for k in range(KT):
                            mm(bank[2 + m % 2][:], g1x_w[:, k, m * P:(m + 1) * P], A3["xT"][:, k, :],
                               start=(k == 0), stop=False)
                        mm(bank[2 + m % 2][:], g1s_w[0:88, m * P:(m + 1) * P], A3["statT"][0:88, :],
                           start=False, stop=True).then_inc(s3["hdn_mm"].sem, 1)
                    pe.wait_ge(s3["gelu"].sem, s3["gelu"].at(b, GH // P))
                    pe.wait_ge(s3["lg_steps"].sem, s3["lg_steps"].at(b, 0))
                    for t in range(TT):
                        for k in range(GH // P):
                            i = mm(bank[4][:, t * NG * H:(t + 1) * NG * H], A3["hdnT"][:, k, t * P:(t + 1) * P],
                                   g2_w[:, k, :], start=(k == 0), stop=(k == GH // P - 1))
                    i.then_inc(s3["lg_mm"].sem, 1)
                    pe.wait_ge(s3["lg_steps"].sem, s3["lg_steps"].at(b, 9))
                    pe.wait_ge(s3["w_sel"].sem, s3["w_sel"].at(b, 0))
                    wcol = A3["w"].rearrange("p t h g -> p (t h g)")
                    mm(bank[5][:, 0:80], const["twice_even"][:], wcol, start=True, stop=True)
                    mm(bank[5][:, 80:160], const["twice_odd"][:], wcol, start=True, stop=True)\
                        .then_inc(s3["w_twice"].sem, 1)
                    pe.wait_ge(s3["p_wl"].sem, s3["p_wl"].at(b, 2))
                    pe.wait_ge(s3["p_sum"].sem, s3["p_sum"].at(b, 4))
                    pe.wait_ge(s3["o_norm"].sem, s3["o_norm"].at(b, 0))
                    for t in range(TT):
                        o = bank[6 + t // 2][:, (t % 2) * D:(t % 2 + 1) * D]
                        mm(o, ident[:], A3["ps"][:, t, :], start=True, stop=False)
                        mm(o, const["fold_even"][:], A3["pwl"][:, t, 0, :], start=False, stop=False)
                        i = mm(o, const["fold_odd"][:], A3["pwl"][:, t, 1, :], start=False, stop=True)
                        if t % 2:
                            i.then_inc(s3["mix_mm"].sem, 1)
                    pe.wait_ge(s3["o_norm"].sem, s3["o_norm"].at(b, 2))
                    for k in range(KT):
                        for t in range(TT):
                            i = nc.tensor.transpose(bank[k][:, t * P:(t + 1) * P], on[:, t, k * P:(k + 1) * P], ident[:])
                        i.then_inc(s3["o_turned"].sem, 1)
                    pe.wait_ge(s3["oT_out"].sem, s3["oT_out"].at(b, 2))
                    for t in range(TT):
                        for k in range(KT):
                            i = mm(bank[2 + t // 2][:, (t % 2) * D:(t % 2 + 1) * D], onT[:, k, t * P:(t + 1) * P],
                                   ow_w[:, k, :], start=(k == 0), stop=(k == KT - 1))
                        if t % 2:
                            i.then_inc(s3["y_mm"].sem, 1)

            @block.scalar
            def _(act):
                a = nc.scalar.activation
                act.wait_ge(s3["zeros3"].sem, 2)
                with act.Fori(0, B) as b:
                    for n in range(4):
                        act.wait_ge(s3["sq_used"].sem, s3["sq_used"].at(b, n - 1 if n >= 2 else 0))
                        T = NJ if n == 0 else TT
                        a(A3["sqb"][:, n % 2, 0:T * D].rearrange("p (t h c) -> p t h c", t=T, h=H), branch(n, b),
                          ACT.Square).then_inc(s3["sq_out"].sem, 1)
                    act.wait_ge(s3["small"].sem, s3["small"].at(b, 4))
                    a(A3["tw"][:, :, 1, :], A3["tw"][:, :, 1, :], ACT.Sqrt).then_inc(s3["roots"].sem, 1)
                    a(A3["st"][:, :, 1, :], A3["st"][:, :, 1, :], ACT.Sqrt).then_inc(s3["roots"].sem, 1)
                    act.wait_ge(s3["st_turned"].sem, s3["st_turned"].at(b, 1))
                    nc.scalar.copy(A3["statT"][64:88, :], bank[1][64:88, :]).then_inc(s3["st_out"].sem, 1)
                    act.wait_ge(s3["st_turned"].sem, s3["st_turned"].at(b, 2))
                    nc.scalar.copy(A3["statT"][0:36, :], bank[0][0:36, :]).then_inc(s3["st_out"].sem, 1)
                    for m in range(GH // P):
                        act.wait_ge(s3["hdn_mm"].sem, s3["hdn_mm"].at(b, m + 1))
                        a(A3["hdnT"][:, m, :], bank[2 + m % 2][:], ACT.Gelu, bias=g1_bias[:, m:m + 1])\
                            .then_inc(s3["gelu"].sem, 1)
                    act.wait_ge(s3["lg_steps"].sem, s3["lg_steps"].at(b, 4))
                    a(A3["lg"], A3["lg"], ACT.Exp).then_inc(s3["lg_exp"].sem, 1)
                    for i2 in range(2):
                        act.wait_ge(s3["mix_mm"].sem, s3["mix_mm"].at(b, i2 + 1))
                        a(A3["sqb"][:, i2, 0:2 * D], bank[6 + i2][:], ACT.Square).then_inc(s3["mix_sq"].sem, 1)
                    for k in range(KT):
                        act.wait_ge(s3["o_turned"].sem, s3["o_turned"].at(b, k + 1))
                        a(onT[:, k, :], bank[k][:], ACT.Copy, scale=onorm[:, 0:1]).then_inc(s3["oT_out"].sem, 1)

            @block.vector
            def _(dve):
                v = nc.vector
                dve.wait_ge(s3["zeros3"].sem, 2)
                with dve.Fori(0, B) as b:
                    for n in range(4):
                        T = NJ if n == 0 else TT
                        v.tensor_reduce(stat(n, 0), branch(n, b), AX.X, ALU.add).then_inc(s3["red"].sem, 1)
                        v.tensor_reduce(stat(n, 2), branch(n, b), AX.X, ALU.max,
                                        apply_absolute_value=True).then_inc(s3["red"].sem, 1)
                        dve.wait_ge(s3["sq_out"].sem, s3["sq_out"].at(b, n + 1))
                        v.tensor_reduce(stat(n, 1), A3["sqb"][:, n % 2, 0:T * D].rearrange("p (t h c) -> p t h c", t=T, h=H),
                                        AX.X, ALU.add).then_inc(s3["sq_used"].sem, 1)
                    dve.wait_ge(s3["red"].sem, s3["red"].at(b, 8))
                    dve.wait_ge(s3["sq_used"].sem, s3["sq_used"].at(b, 4))
                    for s in (A3["tw"], A3["st"]):
                        v.tensor_scalar(s[:, :, 0, :], s[:, :, 0, :], 1.0 / DK, None, ALU.mult).then_inc(s3["small"].sem, 1)
                        v.tensor_scalar(s[:, :, 1, :], s[:, :, 1, :], 1.0 / DK, 1e-8, ALU.mult, ALU.max)\
                            .then_inc(s3["small"].sem, 1)
                    dve.wait_ge(s3["roots"].sem, s3["roots"].at(b, 1))
                    dve.wait_ge(s3["small"].sem, s3["small"].at(b, 4))
                    tw = A3["tw"].rearrange("p j s h -> p j (s h)")
                    v.tensor_copy(A3["sw"][0:DK, :, 0:12], tw[0:DK, :, :]).then_inc(s3["sw_out"].sem, 1)
                    v.tensor_copy(A3["sw"][DK:P, :, 12:24], tw[DK:P, :, :]).then_inc(s3["sw_out"].sem, 1)
                    lg, w = A3["lg"], A3["w"]
                    flat = lambda x: x.rearrange("p t h g -> p t (h g)")
                    groups = lambda x: x.rearrange("p t h g -> p (t h) g")
                    mx = A3["mx"].rearrange("p t h -> p (t h)")
                    dve.wait_ge(s3["lg_mm"].sem, s3["lg_mm"].at(b, 1))
                    v.tensor_tensor(flat(lg), bank[4][:, 0:80].rearrange("p (t n) -> p t n", t=TT),
                                    over_tiles(g2_bias[:], TT), ALU.add).then_inc(s3["lg_steps"].sem, 1)
                    dve.wait_ge(s3["lg_steps"].sem, s3["lg_steps"].at(b, 1))
                    v.tensor_tensor(flat(lg), flat(lg), over_tiles(inv_temp5[:, :, :].rearrange("p h g -> p (h g)"), TT),
                                    ALU.mult).then_inc(s3["lg_steps"].sem, 1)
                    dve.wait_ge(s3["lg_steps"].sem, s3["lg_steps"].at(b, 2))
                    v.tensor_reduce(mx, groups(lg), AX.X, ALU.max).then_inc(s3["lg_steps"].sem, 1)
                    dve.wait_ge(s3["lg_steps"].sem, s3["lg_steps"].at(b, 3))
                    v.tensor_tensor(groups(lg), groups(lg), over_last(mx, NG), ALU.subtract).then_inc(s3["lg_steps"].sem, 1)
                    dve.wait_ge(s3["lg_exp"].sem, s3["lg_exp"].at(b, 1))
                    v.tensor_reduce(mx, groups(lg), AX.X, ALU.add).then_inc(s3["lg_steps"].sem, 1)
                    dve.wait_ge(s3["lg_steps"].sem, s3["lg_steps"].at(b, 5))
                    v.reciprocal(mx, mx).then_inc(s3["lg_steps"].sem, 1)
                    dve.wait_ge(s3["lg_steps"].sem, s3["lg_steps"].at(b, 6))
                    v.tensor_tensor(A3["mx"], A3["mx"], over_tiles(keep[:], TT), ALU.mult).then_inc(s3["lg_steps"].sem, 1)
                    dve.wait_ge(s3["lg_steps"].sem, s3["lg_steps"].at(b, 7))
                    v.tensor_tensor(groups(w), groups(lg), over_last(mx, NG), ALU.mult).then_inc(s3["lg_steps"].sem, 1)
                    dve.wait_ge(s3["lg_steps"].sem, s3["lg_steps"].at(b, 8))
                    w4 = w[:, :, :, 0:NG - 1]
                    v.tensor_tensor(w4, w4, over_tiles(over_last(floor[:], NG - 1), TT), ALU.add)\
                        .then_inc(s3["lg_steps"].sem, 1)
                    dve.wait_ge(s3["lg_steps"].sem, s3["lg_steps"].at(b, 9))
                    v.tensor_tensor(A3["pv"].rearrange("p t (h c) -> p t h c", h=H), branch(3, b),
                                    over_last(w[:, :, :, 4], DK), ALU.mult).then_inc(s3["p_v"].sem, 1)
                    dve.wait_ge(s3["w_twice"].sem, s3["w_twice"].at(b, 1))
                    tw2 = bank[5][:, 0:160].rearrange("p (j h g) -> p j h g", h=H, g=NG)
                    ws = A3["wsel"].rearrange("p a t h -> p (a t) h")
                    v.tensor_copy(ws[0:DK], tw2[0:DK, :, :, 2]).then_inc(s3["w_sel"].sem, 1)
                    v.tensor_copy(ws[DK:P], tw2[DK:P, :, :, 1]).then_inc(s3["w_sel"].sem, 1)
                    dve.wait_ge(s3["w_sel"].sem, s3["w_sel"].at(b, 2))
                    for a in range(2):
                        v.tensor_tensor(A3["pwl"][:, :, a, :].rearrange("p t (h c) -> p t h c", h=H),
                                        wl.rearrange("p (t a) (h c) -> p t a h c", a=2, h=H)[:, bass.ds(b * TT, TT), a, :, :],
                                        over_last(A3["wsel"][:, a, :, :], DK), ALU.mult).then_inc(s3["p_wl"].sem, 1)
                    for i2 in range(2):
                        dve.wait_ge(s3["mix_sq"].sem, s3["mix_sq"].at(b, i2 + 1))
                        v.tensor_reduce(A3["ssh"][:, i2 * 8:i2 * 8 + 8],
                                        A3["sqb"][:, i2, 0:2 * D].rearrange("p (g c) -> p g c", c=DK), AX.X, ALU.add)\
                            .then_inc(s3["mix_ss"].sem, 1)
                    dve.wait_ge(s3["mix_ss"].sem, s3["mix_ss"].at(b, 2))
                    v.tensor_scalar(A3["ssh"], A3["ssh"], 1.0 / DK, 1e-5, ALU.mult, ALU.add).then_inc(s3["mix_ss"].sem, 1)
                    dve.wait_ge(s3["r_head"].sem, s3["r_head"].at(b, 1))
                    for i2 in range(2):
                        v.tensor_tensor(on[:, 2 * i2:2 * i2 + 2, :].rearrange("p t (h c) -> p (t h) c", h=H),
                                        bank[6 + i2][:].rearrange("p (g c) -> p g c", c=DK),
                                        over_last(A3["rh"][:, i2 * 8:i2 * 8 + 8], DK), ALU.mult).then_inc(s3["o_norm"].sem, 1)
                    for i2 in range(2):
                        dve.wait_ge(s3["y_mm"].sem, s3["y_mm"].at(b, i2 + 1))
                        v.tensor_tensor(xr[:, 2 * i2:2 * i2 + 2, :], A3["x"][:, 2 * i2:2 * i2 + 2, :],
                                        bank[2 + i2][:].rearrange("p (t c) -> p t c", t=2), ALU.add).then_inc(s3["res"].sem, 1)
                    layer_norm(dve, scratch, b, xr, A3, s3, "res", lambda t: delta[:, b * TT + t, :], "x1_out")

            @block.gpsimd
            def _(pool):
                g = nc.gpsimd
                g.memset(A3["sw"], 0.0).then_inc(s3["zeros3"].sem, 1)
                g.memset(A3["statT"], 0.0).then_inc(s3["zeros3"].sem, 1)
                with pool.Fori(0, B) as b:
                    pool.wait_ge(s3["lg_steps"].sem, s3["lg_steps"].at(b, 9))
                    ps, pd = A3["ps"], A3["sqb"][:, 0, 0:TT * D].rearrange("p (t c) -> p t c", t=TT)
                    heads = lambda x: x.rearrange("p t (h c) -> p t h c", h=H)
                    g.tensor_tensor(heads(ps), branch(1, b), over_last(A3["w"][:, :, :, 0], DK), ALU.mult)\
                        .then_inc(s3["p_sum"].sem, 1)
                    g.tensor_tensor(heads(pd), branch(2, b), over_last(A3["w"][:, :, :, 3], DK), ALU.mult)\
                        .then_inc(s3["p_sum"].sem, 1)
                    pool.wait_ge(s3["p_sum"].sem, s3["p_sum"].at(b, 2))
                    g.tensor_tensor(ps, ps, pd, ALU.add).then_inc(s3["p_sum"].sem, 1)
                    pool.wait_ge(s3["p_sum"].sem, s3["p_sum"].at(b, 3))
                    pool.wait_ge(s3["p_v"].sem, s3["p_v"].at(b, 1))
                    g.tensor_tensor(ps, ps, A3["pv"], ALU.add).then_inc(s3["p_sum"].sem, 1)
                    pool.wait_ge(s3["mix_ss"].sem, s3["mix_ss"].at(b, 3))
                    g.tensor_tensor(A3["rh"], A3["ssh"], half_exp[:, 0, :], ALU.pow).then_inc(s3["r_head"].sem, 1)
                    pool.wait_ge(s3["ln_st"].sem, s3["ln_st"].at(b, 9))
                    g.tensor_tensor(A3["rs"], A3["ve"], half_exp[:, 0, 0:TT], ALU.pow).then_inc(s3["ln_rs"].sem, 1)

        A4 = carve(arena, {
            "xeo": (2, 2, D), "ctx": (TT, D), "ceo": (2, 2, D), "XFT": (KT, 512), "CFT": (KT, 512), "QF": (4, D),
            "KVF": (4, 2 * D), "PR": (4, 2, D), "RD": (4, 2, XH), "CC": (2, 2, XH), "t1": (2, XH), "t2": (2, XH),
            "t3": (2, XH), "t4": (2, XH), "Es": (HALF,), "co": (L + 2,), "m8": (8,), "mr": (8,), "nb": (1,),
            "rep": (L + 2,), "ex": (L,), "e6": (TOPK,), "s6": (1,), "r6": (1,), "aeo": (L,), "AT": (4, XH),
            "AF": (3, 2, XH), "OF": (4, D), "Eb": (KT, HALF), "oT": (KT, L), "x1b": (TT, D), "xr": (TT, D),
            "ln": (TT, 6), "mv": (TT, 2), "ve": (TT,), "rs": (TT,)})
        free_4 = ("af", "at4_out", "ceo", "cf_mm", "co_out", "es_out", "ot_out", "res4", "x2_out")
        s4 = signals(4, {
            "ctx_in": 16, "xeo": 2, "ceo": 2, "xf_mm": 2, "cf_mm": 2, "xf_out": 2, "cf_out": 2, "qf_mm": 2, "kvf_mm": 4,
            "qf_out": 2, "kvf_out": 4, "prod_v": 2, "prod_g": 2, "corr_red": 1, "cc": 6, "corr_mm": 1, "es_out": 1,
            "co_out": 2, "top": 3, "rep_out": 1, "exps": 2, "a_steps": 5, "a_turned4": 1, "at4_out": 1, "af_mm": 1, "af": 5,
            "of_v": 2, "of_g": 2, "of": 2, "ot_mm": 2, "eb_out": 2, "ot_out": 4, "y4_mm": 2, "x1b_out": 1, "res4": 2,
            "ln_st": 9, "ln_rs": 1, "x2_out": 4, "sentinels": 0}, free_4)
        ab = lambda i: A4["PR"][:, i, :, :]
        with nc.Block() as block:
            @block.sync
            def _(sp):
                for n in free_4:
                    sp.sem_inc(s4[n].sem, 1)
                with sp.Fori(0, B) as b:
                    sp.wait_ge(s4["ceo"].sem, s4["ceo"].at(b, 0))
                    sp.dma_start(A4["ctx"], dr["ctx"][b].rearrange("(t p) d -> p t d", p=P)).then_inc(s4["ctx_in"].sem, 16)

            @block.tensor
            def _(pe):
                mm = nc.tensor.matmul
                pe.wait_ge(s4["sentinels"].sem, 2)
                pe.wait_ge(late_loaded.sem, 16 * 5)
                with pe.Fori(0, B) as b:
                    for src, go, done, first, free in ((A4["ceo"], "ceo", "cf_mm", 2, "at4_out"), (A4["xeo"], "xeo", "xf_mm", 0, "res4")):
                        pe.wait_ge(s4[go].sem, s4[go].at(b, 2))
                        pe.wait_ge(s4[free].sem, s4[free].at(b, 0))
                        pe.wait_ge(s4["es_out"].sem, s4["es_out"].at(b, 0))
                        pe.wait_ge(s4["co_out"].sem, s4["co_out"].at(b, 0))
                        for d in range(KT):
                            for par in range(2):
                                for k in range(2):
                                    i = mm(bank[first + d][:, par * 256:(par + 1) * 256], src[:, par, k, d * P:(d + 1) * P],
                                           dft[:, k, par * 256:(par + 1) * 256], start=(k == 0), stop=(k == 1))
                            i.then_inc(s4[done].sem, 1)
                    pe.wait_ge(s4["xf_out"].sem, s4["xf_out"].at(b, 2))
                    pe.wait_ge(s4["af"].sem, s4["af"].at(b, 0))
                    pe.wait_ge(s4["ot_out"].sem, s4["ot_out"].at(b, 0))
                    for f in range(4):
                        o = bank[4 + f // 2][:, (f % 2) * D:(f % 2 + 1) * D]
                        for k in range(KT):
                            i = mm(o, A4["XFT"][:, k, f * P:(f + 1) * P], xq_w[:, k, :], start=(k == 0),
                                   stop=(k == KT - 1 and f > 0))
                        if f == 0:
                            i = mm(o, const["dc_row"][0:1, :], xq_b[:], start=False, stop=True)
                        if f % 2:
                            i.then_inc(s4["qf_mm"].sem, 1)
                    pe.wait_ge(s4["cf_out"].sem, s4["cf_out"].at(b, 2))
                    pe.wait_ge(s4["res4"].sem, s4["res4"].at(b, 0))
                    for f in range(4):
                        o = bank[(6 + f) % 8][:]
                        for k in range(KT):
                            i = mm(o, A4["CFT"][:, k, f * P:(f + 1) * P], xkv_w[:, k, :], start=(k == 0),
                                   stop=(k == KT - 1 and f > 0))
                        if f == 0:
                            i = mm(o, const["dc_row"][0:1, :], xkv_b[:], start=False, stop=True)
                        i.then_inc(s4["kvf_mm"].sem, 1)
                    pe.wait_ge(s4["cc"].sem, s4["cc"].at(b, 6))
                    for par in range(2):
                        for ri in range(2):
                            i = mm(bank[2][0:XH, par * HALF:(par + 1) * HALF], A4["CC"][:, ri, par, :],
                                   idft[:, 2 * par + ri, :], start=(ri == 0), stop=(ri == 1))
                    i.then_inc(s4["corr_mm"].sem, 1)
                    pe.wait_ge(s4["a_steps"].sem, s4["a_steps"].at(b, 5))
                    for k in range(4):
                        i = mm(bank[3][:, k * XH:(k + 1) * XH], A4["aeo"][0:XH, k * P:(k + 1) * P],
                               ident[0:XH, 0:XH], start=True, stop=True)
                    i.then_inc(s4["a_turned4"].sem, 1)
                    pe.wait_ge(s4["at4_out"].sem, s4["at4_out"].at(b, 1))
                    pe.wait_ge(s4["qf_out"].sem, s4["qf_out"].at(b, 2))
                    for f in range(4):
                        for k in range(2):
                            i = mm(bank[4][:, f * XH:(f + 1) * XH], dft[:, k, f * P:(f + 1) * P],
                                   A4["AT"][:, 2 * (f // 2) + k, :], start=(k == 0), stop=(k == 1))
                    i.then_inc(s4["af_mm"].sem, 1)
                    pe.wait_ge(s4["of"].sem, s4["of"].at(b, 2))
                    pe.wait_ge(s4["kvf_out"].sem, s4["kvf_out"].at(b, 4))
                    for m in range(KT):
                        for par in range(2):
                            for ri in range(2):
                                i = mm(bank[5 + m][:, par * HALF:(par + 1) * HALF], A4["OF"][:, 2 * par + ri, m * P:(m + 1) * P],
                                       idft[:, 2 * par + ri, :], start=(ri == 0), stop=(ri == 1))
                        i.then_inc(s4["ot_mm"].sem, 1)
                    pe.wait_ge(s4["ot_out"].sem, s4["ot_out"].at(b, 4))
                    for t in range(TT):
                        for k in range(KT):
                            i = mm(bank[[7, 0][t // 2]][:, (t % 2) * D:(t % 2 + 1) * D], A4["oT"][:, k, t * P:(t + 1) * P],
                                   xo_w[:, k, :], start=(k == 0), stop=(k == KT - 1))
                        if t % 2:
                            i.then_inc(s4["y4_mm"].sem, 1)

            @block.scalar
            def _(act):
                a = nc.scalar.activation
                act.wait_ge(s4["sentinels"].sem, 2)
                with act.Fori(0, B) as b:
                    for d in range(KT):
                        act.wait_ge(s4["cf_mm"].sem, s4["cf_mm"].at(b, d + 1))
                        nc.scalar.copy(A4["CFT"][:, d, :], bank[2 + d][:]).then_inc(s4["cf_out"].sem, 1)
                    for d in range(KT):
                        act.wait_ge(s4["xf_mm"].sem, s4["xf_mm"].at(b, d + 1))
                        nc.scalar.copy(A4["XFT"][:, d, :], bank[d][:]).then_inc(s4["xf_out"].sem, 1)
                    for i2 in range(2):
                        act.wait_ge(s4["qf_mm"].sem, s4["qf_mm"].at(b, i2 + 1))
                        nc.scalar.copy(A4["QF"][:, 2 * i2:2 * i2 + 2, :], bank[4 + i2][:].rearrange("p (t c) -> p t c", t=2))\
                            .then_inc(s4["qf_out"].sem, 1)
                    for f in range(4):
                        act.wait_ge(s4["kvf_mm"].sem, s4["kvf_mm"].at(b, f + 1))
                        nc.scalar.copy(A4["KVF"][:, f, :], bank[(6 + f) % 8][:]).then_inc(s4["kvf_out"].sem, 1)
                    act.wait_ge(s4["corr_mm"].sem, s4["corr_mm"].at(b, 1))
                    nc.scalar.copy(A4["Es"][0:XH, :], bank[2][0:XH, 0:HALF]).then_inc(s4["es_out"].sem, 1)
                    act.wait_ge(s4["top"].sem, s4["top"].at(b, 3))
                    a(A4["ex"][0:XH, :], A4["co"][0:XH, 0:L], ACT.Exp, bias=A4["nb"][0:XH, :], scale=1.0 / XD)\
                        .then_inc(s4["exps"].sem, 1)
                    a(A4["e6"][0:XH, :], A4["m8"][0:XH, 0:TOPK], ACT.Exp, bias=A4["nb"][0:XH, :], scale=1.0 / XD,
                      accum_out=A4["s6"][0:XH, :]).then_inc(s4["exps"].sem, 1)
                    for m in range(KT):
                        act.wait_ge(s4["ot_mm"].sem, s4["ot_mm"].at(b, m + 1))
                        nc.scalar.copy(A4["Eb"][:, m, :], bank[5 + m][:, 0:HALF]).then_inc(s4["eb_out"].sem, 1)

            def spectra(i):
                return {"qr": A4["QF"][:, 0::2, :], "qi": A4["QF"][:, 1::2, :],
                        "kr": A4["KVF"][:, 0::2, 0:D], "ki": A4["KVF"][:, 1::2, 0:D],
                        "vr": A4["KVF"][:, 0::2, D:2 * D], "vi": A4["KVF"][:, 1::2, D:2 * D]}[i]

            @block.vector
            def _(dve):
                v = nc.vector
                dve.wait_ge(s4["sentinels"].sem, 2)
                with dve.Fori(0, B) as b:
                    x1 = delta[:, bass.ds(b * TT, TT), :]
                    dve.wait_ge(s4["x2_out"].sem, s4["x2_out"].at(b, 0))
                    v.tensor_tensor(A4["xeo"][:, 0, :, :], x1[:, 0:2, :], x1[:, 2:4, :], ALU.add).then_inc(s4["xeo"].sem, 1)
                    v.tensor_tensor(A4["xeo"][:, 1, :, :], x1[:, 0:2, :], x1[:, 2:4, :], ALU.subtract).then_inc(s4["xeo"].sem, 1)
                    dve.wait_ge(s4["qf_out"].sem, s4["qf_out"].at(b, 2))
                    dve.wait_ge(s4["kvf_out"].sem, s4["kvf_out"].at(b, 4))
                    v.tensor_tensor(ab(0), spectra("qr"), spectra("kr"), ALU.mult).then_inc(s4["prod_v"].sem, 1)
                    v.tensor_tensor(ab(1), spectra("qi"), spectra("ki"), ALU.mult).then_inc(s4["prod_v"].sem, 1)
                    dve.wait_ge(s4["prod_v"].sem, s4["prod_v"].at(b, 2))
                    dve.wait_ge(s4["prod_g"].sem, s4["prod_g"].at(b, 2))
                    v.tensor_reduce(A4["RD"].rearrange("p a e h -> p (a e h)"),
                                    A4["PR"].rearrange("p a e (h c) -> p (a e h) c", c=XD), AX.X, ALU.add)\
                        .then_inc(s4["corr_red"].sem, 1)
                    dve.wait_ge(s4["corr_red"].sem, s4["corr_red"].at(b, 1))
                    rd = lambda i: A4["RD"][:, i, :, :]
                    steps = [(A4["t1"], rd(1), not_dc, ALU.mult), (A4["t2"], rd(2), rd(3), ALU.subtract),
                             (A4["t4"], rd(1), is_dc, ALU.mult), (A4["CC"][:, 0, :, :], rd(0), A4["t1"], ALU.add),
                             (A4["t3"], A4["t2"], not_dc, ALU.mult), (A4["CC"][:, 1, :, :], A4["t3"], A4["t4"], ALU.add)]
                    for n, (o, x, y, op) in enumerate(steps):
                        if n >= 3:
                            dve.wait_ge(s4["cc"].sem, s4["cc"].at(b, n if n == 5 else n - 1))
                        v.tensor_tensor(o, x, y, op).then_inc(s4["cc"].sem, 1)
                    dve.wait_ge(s4["corr_mm"].sem, s4["corr_mm"].at(b, 1))
                    dve.wait_ge(s4["es_out"].sem, s4["es_out"].at(b, 1))
                    es, od = A4["Es"][0:XH, :], bank[2][0:XH, HALF:L]
                    v.tensor_tensor(A4["co"][0:XH, 0:HALF], es, od, ALU.add).then_inc(s4["co_out"].sem, 1)
                    v.tensor_tensor(A4["co"][0:XH, HALF:L], es, od, ALU.subtract).then_inc(s4["co_out"].sem, 1)
                    dve.wait_ge(s4["co_out"].sem, s4["co_out"].at(b, 2))
                    v.memset(scratch, 0.0)
                    v.max(A4["m8"][0:XH, :], A4["co"][0:XH, 0:L]).then_inc(s4["top"].sem, 1)
                    dve.wait_ge(s4["top"].sem, s4["top"].at(b, 1))
                    v.tensor_copy(A4["mr"][0:XH, 0:TOPK], A4["m8"][0:XH, 0:TOPK]).then_inc(s4["top"].sem, 1)
                    dve.wait_ge(s4["top"].sem, s4["top"].at(b, 2))
                    v.tensor_scalar(A4["nb"][0:XH, :], A4["m8"][0:XH, 0:1], -1.0 / XD, None, ALU.mult)\
                        .then_inc(s4["top"].sem, 1)
                    v.match_replace(A4["rep"][0:XH, :], A4["mr"][0:XH, :], A4["co"][0:XH, :], BIG)\
                        .then_inc(s4["rep_out"].sem, 1)
                    dve.wait_ge(s4["rep_out"].sem, s4["rep_out"].at(b, 1))
                    dve.wait_ge(s4["exps"].sem, s4["exps"].at(b, 2))
                    v.reciprocal(A4["r6"][0:XH, :], A4["s6"][0:XH, :]).then_inc(s4["a_steps"].sem, 1)
                    v.scalar_tensor_tensor(out=A4["rep"][0:XH, 0:L], in0=A4["rep"][0:XH, 0:L], scalar=BIG,
                                           in1=A4["ex"][0:XH, :], op0=ALU.is_ge, op1=ALU.mult).then_inc(s4["a_steps"].sem, 1)
                    dve.wait_ge(s4["a_steps"].sem, s4["a_steps"].at(b, 2))
                    v.tensor_scalar(A4["rep"][0:XH, 0:L], A4["rep"][0:XH, 0:L], A4["r6"][0:XH, :], None, ALU.mult)\
                        .then_inc(s4["a_steps"].sem, 1)
                    dve.wait_ge(s4["a_steps"].sem, s4["a_steps"].at(b, 3))
                    lo, hi = A4["rep"][0:XH, 0:HALF], A4["rep"][0:XH, HALF:L]
                    v.tensor_tensor(A4["aeo"][0:XH, 0:HALF], lo, hi, ALU.add).then_inc(s4["a_steps"].sem, 1)
                    v.tensor_tensor(A4["aeo"][0:XH, HALF:L], lo, hi, ALU.subtract).then_inc(s4["a_steps"].sem, 1)
                    dve.wait_ge(s4["a_turned4"].sem, s4["a_turned4"].at(b, 1))
                    v.tensor_copy(A4["AT"].rearrange("p k h -> p (k h)"), bank[3][:, 0:4 * XH]).then_inc(s4["at4_out"].sem, 1)
                    dve.wait_ge(s4["af_mm"].sem, s4["af_mm"].at(b, 1))
                    af = bank[4][:, 0:4 * XH].rearrange("p (a ri h) -> p a ri h", a=2, ri=2)
                    a1, a2, a3 = (A4["AF"][:, n, :, :] for n in range(3))
                    v.tensor_copy(a1, af[:, :, 0, :]).then_inc(s4["af"].sem, 1)
                    v.tensor_tensor(a2, af[:, :, 1, :], not_dc, ALU.mult).then_inc(s4["af"].sem, 1)
                    v.tensor_tensor(A4["t1"], af[:, :, 1, :], is_dc, ALU.mult).then_inc(s4["af"].sem, 1)
                    v.tensor_tensor(A4["t2"], af[:, :, 0, :], not_dc, ALU.mult).then_inc(s4["af"].sem, 1)
                    dve.wait_ge(s4["af"].sem, s4["af"].at(b, 4))
                    v.tensor_tensor(a3, A4["t1"], A4["t2"], ALU.add).then_inc(s4["af"].sem, 1)
                    hd = lambda x: x.rearrange("p e (h c) -> p e h c", c=XD)
                    v.tensor_tensor(hd(ab(0)), hd(spectra("vr")), over_last(a1, XD), ALU.mult).then_inc(s4["of_v"].sem, 1)
                    dve.wait_ge(s4["af"].sem, s4["af"].at(b, 5))
                    v.tensor_tensor(hd(ab(2)), hd(spectra("vi")), over_last(a3, XD), ALU.mult).then_inc(s4["of_v"].sem, 1)
                    dve.wait_ge(s4["of_v"].sem, s4["of_v"].at(b, 2))
                    dve.wait_ge(s4["of_g"].sem, s4["of_g"].at(b, 2))
                    v.tensor_tensor(A4["OF"][:, 0::2, :], ab(0), ab(1), ALU.subtract).then_inc(s4["of"].sem, 1)
                    v.tensor_tensor(A4["OF"][:, 1::2, :], ab(2), ab(3), ALU.add).then_inc(s4["of"].sem, 1)
                    for m in range(KT):
                        dve.wait_ge(s4["eb_out"].sem, s4["eb_out"].at(b, m + 1))
                        eb, od = A4["Eb"][:, m, :], bank[5 + m][:, HALF:L]
                        v.tensor_tensor(A4["oT"][:, m, 0:HALF], eb, od, ALU.add).then_inc(s4["ot_out"].sem, 1)
                        v.tensor_tensor(A4["oT"][:, m, HALF:L], eb, od, ALU.subtract).then_inc(s4["ot_out"].sem, 1)
                    dve.wait_ge(s4["x1b_out"].sem, s4["x1b_out"].at(b, 1))
                    for i2 in range(2):
                        dve.wait_ge(s4["y4_mm"].sem, s4["y4_mm"].at(b, i2 + 1))
                        v.tensor_tensor(A4["xr"][:, 2 * i2:2 * i2 + 2, :], A4["x1b"][:, 2 * i2:2 * i2 + 2, :],
                                        bank[[7, 0][i2]][:].rearrange("p (t c) -> p t c", t=2), ALU.add)\
                            .then_inc(s4["res4"].sem, 1)
                    layer_norm(dve, scratch, b, A4["xr"], A4, s4, "res4", lambda t: short[:, b * TT + t, :], "x2_out")

            @block.gpsimd
            def _(pool):
                g = nc.gpsimd
                g.memset(A4["co"][:, L:L + 2], -BIG).then_inc(s4["sentinels"].sem, 1)
                g.memset(A4["mr"], -BIG).then_inc(s4["sentinels"].sem, 1)
                with pool.Fori(0, B) as b:
                    c = A4["ctx"]
                    pool.wait_ge(s4["ctx_in"].sem, s4["ctx_in"].at(b, 16))
                    pool.wait_ge(s4["cf_mm"].sem, s4["cf_mm"].at(b, 0))
                    g.tensor_tensor(A4["ceo"][:, 0, :, :], c[:, 0:2, :], c[:, 2:4, :], ALU.add).then_inc(s4["ceo"].sem, 1)
                    g.tensor_tensor(A4["ceo"][:, 1, :, :], c[:, 0:2, :], c[:, 2:4, :], ALU.subtract).then_inc(s4["ceo"].sem, 1)
                    pool.wait_ge(s4["res4"].sem, s4["res4"].at(b, 0))
                    g.tensor_tensor(A4["x1b"], delta[:, bass.ds(b * TT, TT), :], over_tiles(xo_b[:], TT), ALU.add)\
                        .then_inc(s4["x1b_out"].sem, 1)
                    pool.wait_ge(s4["qf_out"].sem, s4["qf_out"].at(b, 2))
                    pool.wait_ge(s4["kvf_out"].sem, s4["kvf_out"].at(b, 4))
                    g.tensor_tensor(ab(2), spectra("qi"), spectra("kr"), ALU.mult).then_inc(s4["prod_g"].sem, 1)
                    g.tensor_tensor(ab(3), spectra("qr"), spectra("ki"), ALU.mult).then_inc(s4["prod_g"].sem, 1)
                    pool.wait_ge(s4["af"].sem, s4["af"].at(b, 5))
                    a2 = A4["AF"][:, 1, :, :]
                    hd = lambda x: x.rearrange("p e (h c) -> p e h c", c=XD)
                    g.tensor_tensor(hd(ab(1)), hd(spectra("vi")), over_last(a2, XD), ALU.mult).then_inc(s4["of_g"].sem, 1)
                    g.tensor_tensor(hd(ab(3)), hd(spectra("vr")), over_last(a2, XD), ALU.mult).then_inc(s4["of_g"].sem, 1)
                    pool.wait_ge(s4["ln_st"].sem, s4["ln_st"].at(b, 9))
                    g.tensor_tensor(A4["rs"], A4["ve"], half_exp[:, 0, 0:TT], ALU.pow).then_inc(s4["ln_rs"].sem, 1)

        A5 = carve(arena, {"wi": (3, KT * HID), "wg": (KT, HID), "wu": (KT, HID), "wd": (MF, D),
                           "x2": (TT, D), "x2T": (KT, L), "sg": (2, L), "hT": (MF, L), "xr": (TT, D), "y": (TT, D),
                           "ln": (TT, 6), "mv": (TT, 2), "ve": (TT,), "rs": (TT,)})
        free_5 = ("h_out", "res5", "stored")
        s5 = signals(5, {"w_in": 0, "w_f32": 0, "x2_copy": 1, "x_turned5": 2, "x2T_out": 2, "gate_mm": 6, "up_mm": 6,
                      "gate_silu": 6, "h_out": 6, "y5_mm": 2, "res5": 2, "ln_st": 9, "ln_rs": 1, "y_out": 4,
                      "stored": 16}, free_5)
        with nc.Block() as block:
            @block.sync
            def _(sp):
                for n in free_5:
                    sp.sem_inc(s5[n].sem, 1)
                wi = A5["wi"].bitcast(I32)
                for n, (name, k) in enumerate((("w_gateT", KT), ("w_upT", KT), ("w_downT", MF))):
                    sp.dma_start(wi[:, n, :].rearrange("p (k n) -> p k n", k=k),
                                 dr[name].rearrange("(k p) n -> p k n", p=P)).then_inc(s5["w_in"].sem, 16)
                with sp.Fori(0, B) as b:
                    sp.wait_ge(s5["y_out"].sem, s5["y_out"].at(b, 4))
                    sp.dma_start(out[b].rearrange("(t p) d -> p t d", p=P), A5["y"]).then_inc(s5["stored"].sem, 16)
                sp.wait_ge(s5["stored"].sem, s5["stored"].at(B, 0))

            @block.tensor
            def _(pe):
                mm = nc.tensor.matmul
                pe.wait_ge(s5["w_f32"].sem, 3)
                with pe.Fori(0, B) as b:
                    pe.wait_ge(s5["x2_copy"].sem, s5["x2_copy"].at(b, 1))
                    for k in range(KT):
                        for t in range(TT):
                            i = nc.tensor.transpose(bank[k][:, t * P:(t + 1) * P], A5["x2"][:, t, k * P:(k + 1) * P], ident[:])
                        i.then_inc(s5["x_turned5"].sem, 1)
                    pe.wait_ge(s5["x2T_out"].sem, s5["x2T_out"].at(b, 2))
                    for m in range(MF):
                        for w, first, done in (("wg", 2, "gate_mm"), ("wu", 4, "up_mm")):
                            pe.wait_ge(s5["h_out"].sem, s5["h_out"].at(b, m - 1 if m >= 2 else 0))
                            for k in range(KT):
                                i = mm(bank[first + m % 2][:], A5[w][:, k, m * P:(m + 1) * P], A5["x2T"][:, k, :],
                                       start=(k == 0), stop=(k == KT - 1))
                            i.then_inc(s5[done].sem, 1)
                    pe.wait_ge(s5["h_out"].sem, s5["h_out"].at(b, MF))
                    pe.wait_ge(s5["res5"].sem, s5["res5"].at(b, 0))
                    for t in range(TT):
                        for m in range(MF):
                            i = mm(bank[6 + t // 2][:, (t % 2) * D:(t % 2 + 1) * D], A5["hT"][:, m, t * P:(t + 1) * P],
                                   A5["wd"][:, m, :], start=(m == 0), stop=(m == MF - 1))
                        if t % 2:
                            i.then_inc(s5["y5_mm"].sem, 1)

            @block.scalar
            def _(act):
                act.wait_ge(s5["w_in"].sem, 48)
                wi = A5["wi"].bitcast(I32)
                for n, w in enumerate(("wg", "wu", "wd")):
                    nc.scalar.activation(A5[w].rearrange("p k n -> p (k n)"), wi[:, n, :], ACT.Copy, scale=1.0 / 127.0)\
                        .then_inc(s5["w_f32"].sem, 1)
                with act.Fori(0, B) as b:
                    for k in range(KT):
                        act.wait_ge(s5["x_turned5"].sem, s5["x_turned5"].at(b, k + 1))
                        nc.scalar.copy(A5["x2T"][:, k, :], bank[k][:]).then_inc(s5["x2T_out"].sem, 1)
                    for m in range(MF):
                        act.wait_ge(s5["gate_mm"].sem, s5["gate_mm"].at(b, m + 1))
                        act.wait_ge(s5["h_out"].sem, s5["h_out"].at(b, m - 1 if m >= 2 else 0))
                        nc.scalar.activation(A5["sg"][:, m % 2, :], bank[2 + m % 2][:], ACT.Silu)\
                            .then_inc(s5["gate_silu"].sem, 1)

            @block.vector
            def _(dve):
                v = nc.vector
                with dve.Fori(0, B) as b:
                    for m in range(MF):
                        dve.wait_ge(s5["gate_silu"].sem, s5["gate_silu"].at(b, m + 1))
                        dve.wait_ge(s5["up_mm"].sem, s5["up_mm"].at(b, m + 1))
                        v.tensor_tensor(A5["hT"][:, m, :], A5["sg"][:, m % 2, :], bank[4 + m % 2][:], ALU.mult)\
                            .then_inc(s5["h_out"].sem, 1)
                    for i2 in range(2):
                        dve.wait_ge(s5["y5_mm"].sem, s5["y5_mm"].at(b, i2 + 1))
                        v.tensor_tensor(A5["xr"][:, 2 * i2:2 * i2 + 2, :], A5["x2"][:, 2 * i2:2 * i2 + 2, :],
                                        bank[6 + i2][:].rearrange("p (t c) -> p t c", t=2), ALU.add).then_inc(s5["res5"].sem, 1)
                    dve.wait_ge(s5["stored"].sem, s5["stored"].at(b, 0))
                    layer_norm(dve, scratch, b, A5["xr"], A5, s5, "res5", lambda t: A5["y"][:, t, :], "y_out")

            @block.gpsimd
            def _(pool):
                with pool.Fori(0, B) as b:
                    pool.wait_ge(s5["res5"].sem, s5["res5"].at(b, 0))
                    nc.gpsimd.tensor_copy(A5["x2"], short[:, bass.ds(b * TT, TT), :]).then_inc(s5["x2_copy"].sem, 1)
                    pool.wait_ge(s5["ln_st"].sem, s5["ln_st"].at(b, 9))
                    nc.gpsimd.tensor_tensor(A5["rs"], A5["ve"], half_exp[:, 0, 0:TT], ALU.pow).then_inc(s5["ln_rs"].sem, 1)


def kernel(**inputs):
    import concourse.bacc as _bacc
    from concourse.bass_utils import run_bass_kernel_spmd as _run

    def turned(name):
        return np.ascontiguousarray(np.asarray(inputs[name]).T)

    a = {n: np.asarray(v) for n, v in inputs.items()}
    g1 = a["L0_attn_g1_w"]
    order = [0, 3, 4, 2, 1]
    g1s = np.concatenate([g1[:, D + 12 * i:D + 12 * i + 12] for i in order], axis=1)

    def hankel(name):
        w = a[name].reshape(D, -1)
        z = np.zeros((P - 1 + DK, D), w.dtype)
        z[P - w.shape[1]:P] = w.T
        return np.ascontiguousarray(z.reshape(-1, NPIECE, PIECE).transpose(1, 0, 2))

    arrays = {
        "x": a["x"], "xT": np.ascontiguousarray(a["x"].transpose(0, 2, 1)), "ctx": a["ctx_1024"],
        "qkv_wT": np.concatenate([turned(f"L0_attn_{n}_w") for n in "kqv"], axis=1),
        "b_wT": turned("L0_attn_b_w"),
        "conv_w": np.concatenate([a[f"L0_attn_conv{n}_w"] for n in "kqv"], axis=0),
        "fir_s": a["L0_attn_fir_s"].reshape(D, -1),
        "toep_w": hankel("L0_attn_fir_wd"), "toep_l": hankel("L0_attn_fir_l"),
        "g1x_wT": np.ascontiguousarray(g1[:, 0:D].T), "g1s_wT": np.ascontiguousarray(g1s.T), "g1_b": a["L0_attn_g1_b"].reshape(-1, P).T,
        "g2_wT": turned("L0_attn_g2_w"), "g2_b": a["L0_attn_g2_b"], "onorm": a["L0_attn_onorm_w"],
        "o_wT": turned("L0_attn_o_w"),
        "gate_par": np.concatenate([a["L0_attn_value_bias"], a["L0_attn_log_temp"], a["L0_attn_floor_logit"]]),
        "xq_wT": turned("L0_xattn_Wq"), "xq_b": a["L0_xattn_bq"],
        "xkv_wT": np.concatenate([turned("L0_xattn_Wk"), turned("L0_xattn_Wv")], axis=1),
        "xkv_b": np.concatenate([a["L0_xattn_bk"], a["L0_xattn_bv"]]),
        "xo_wT": turned("L0_xattn_Wo"), "xo_b": a["L0_xattn_bo"],
        "w_gateT": turned("L0_ffn_w_gate"), "w_upT": turned("L0_ffn_w_up"), "w_downT": turned("L0_ffn_w_down"),
    }
    arrays.update({"c_" + n: v for n, v in shape_constants().items()})
    arrays = {n: np.ascontiguousarray(v) for n, v in arrays.items()}
    nc = _bacc.Bacc("TRN2", target_bir_lowering=False, num_devices=1)
    dr = {n: nc.dram_tensor("in_" + n, v.shape, mybir.dt.from_np(v.dtype), kind="ExternalInput").ap()
          for n, v in arrays.items()}
    out = nc.dram_tensor("out_0", (B, L, D), F32, kind="ExternalOutput").ap()
    layer(nc, dr, out)
    r = _run(nc, [{"in_" + n: v for n, v in arrays.items()}], core_ids=[0])
    return r.results[0]["out_0"]
```

```python
from contextlib import ExitStack

import numpy as np

import concourse.bass as bass
from concourse import mybir

F32 = mybir.dt.float32
I32 = mybir.dt.int32
BF16 = mybir.dt.bfloat16
ALU = mybir.AluOpType
ACT = mybir.ActivationFunctionType
AX = mybir.AxisListType

P = 128
B, L, D = 4, 512, 256
H, DK = 4, 64
KT = D // P
TT = L // P
BT = B * TT
NJ = L // DK
CONV_K, FIR_S, FIR_L, FIR_W = 4, 3, 31, 64
LEVELS = 7
GH = 2 * D
NG = 5
HID = 768
MF = HID // P
XH, XD = 16, 16
TOPK = 6
PIECE = 8
NPIECE = D // PIECE
PER_BATCH = NPIECE // B
TOEP_BUFS = 4
HALF = L // 2
BIG = 3.0e38


def shape_constants():
    i = np.arange(P)
    c = {}
    c["ident"] = np.eye(P)
    c["mask_lower"] = (i[:, None] > i[None, :])
    c["mask_upper"] = (i[None, :] >= i[:, None])
    c["level0"] = -((i[:, None] % 2 == 1) & (i[None, :] == i[:, None] - 1)).astype(float)
    c["blocks"] = (i[:, None] // DK == i[None, :] // DK)
    lev = np.zeros((P, LEVELS - 1, P // 2))
    for k in range(1, LEVELS):
        even = i[(i >> k) % 2 == 0]
        lev[:, k - 1, :] = ((i[:, None] >> k) % 2 == 1) & ((i[:, None] >> (k + 1)) == (even[None, :] >> (k + 1)))
    c["levels"] = lev.reshape(P, -1)
    c["heads"] = (i[:, None] // DK == np.arange(2)[None, :])
    back = DK - 1 - i % DK
    c["fold"] = (back[:, None] == np.arange(DK)[None, :])
    c["fold_even"] = (back[:, None] == i[None, :])
    c["fold_odd"] = (back[:, None] + DK == i[None, :])
    c["twice_even"] = (i[:, None] == back[None, :])
    c["twice_odd"] = (i[:, None] == back[None, :] + DK)
    t = np.arange(HALF)
    f = np.arange(P)
    dft, inv = np.zeros((HALF, 4, P)), np.zeros((P, 4, HALF))
    for par in range(2):
        w = 2 * np.pi * ((2 * f + par)[None, :] * t[:, None] % L) / L
        dft[:, 2 * par], dft[:, 2 * par + 1] = np.cos(w), -np.sin(w)
        inv[:, 2 * par], inv[:, 2 * par + 1] = 2 * np.cos(w).T / L, -2 * np.sin(w).T / L
    dft[:, 1, 0] = (-1.0) ** t
    inv[0, 0], inv[0, 1] = 1.0 / L, (-1.0) ** t / L
    c["dft"] = dft.reshape(2, P, 4 * P).transpose(1, 0, 2).reshape(P, -1)
    c["idft"] = inv.reshape(P, -1)
    z = np.ones((P, 2, XH)); z[0, 0] = 0.0
    c["not_dc"] = z.reshape(P, -1)
    c["is_dc"] = (1.0 - z).reshape(P, -1)
    row = np.zeros((P, P)); row[0, 0] = L
    c["dc_row"] = row
    return {n: np.ascontiguousarray(a.astype(np.float32).reshape(P, -1)) for n, a in c.items()}


LATE_CONST = ("dft", "idft")


class Signal:

    def __init__(self, sem, per_round, base=0):
        self.sem, self.n, self.base = sem, per_round, base

    def at(self, rnd, k):
        return rnd * self.n + (self.base + k)

    def two_before(self, rnd):
        return rnd * self.n + (self.base - self.n)


def carve(arena, sizes, at=0):
    out = {}
    for name, shape in sizes.items():
        n = int(np.prod(shape))
        v = arena[:, at:at + n]
        if len(shape) == 2:
            v = v.rearrange("p (a b) -> p a b", a=shape[0])
        elif len(shape) == 3:
            v = v.rearrange("p (a b c) -> p a b c", a=shape[0], b=shape[1])
        elif len(shape) == 4:
            v = v.rearrange("p (a b c d) -> p a b c d", a=shape[0], b=shape[1], c=shape[2])
        out[name] = v
        at += n
    assert at <= arena.shape[1], (at, arena.shape)
    return out


def over_last(ap, n):
    return ap.unsqueeze(len(ap.shape)).broadcast_to(list(ap.shape) + [n])


def over_tiles(ap, n):
    return ap.unsqueeze(1).broadcast_to([ap.shape[0], n] + list(ap.shape[1:]))


def norm_statistics(dve, scratch, b, x, buf, sig, summed):
    v = dve
    for t in range(TT):
        dve.wait_ge(sig[summed].sem, sig[summed].at(b, t // 2 + 1))
        v.bn_stats(buf["ln"][:, t, :], x[:, t, :]).then_inc(sig["ln_st"].sem, 1)
    dve.wait_ge(sig["ln_st"].sem, sig["ln_st"].at(b, TT))
    v.memset(scratch, 0.0)
    for t in range(TT):
        v.bn_aggr(buf["mv"][:, t, :], buf["ln"][:, t, :]).then_inc(sig["ln_st"].sem, 1)
    dve.wait_ge(sig["ln_st"].sem, sig["ln_st"].at(b, 2 * TT))
    v.tensor_scalar(buf["ve"], buf["mv"][:, :, 1], 1e-5, None, ALU.add).then_inc(sig["ln_st"].sem, 1)


def norm_apply(dve, b, x, buf, sig, dst, done):
    dve.wait_ge(sig["ln_rs"].sem, sig["ln_rs"].at(b, 1))
    for t in range(TT):
        dve.tensor_scalar(dst(t), x[:, t, :], buf["mv"][:, t, 0:1], buf["rs"][:, t:t + 1], ALU.subtract,
                          ALU.mult).then_inc(sig[done].sem, 1)


def layer(nc, dr, out):
    ctx = ExitStack()
    with ctx:
        def sb(name, shape, dt=F32):
            return ctx.enter_context(nc.sbuf_tensor(name, shape, dt))

        def signals(stage, names, free, pair=False):
            return {n: Signal(ctx.enter_context(nc.semaphore(f"{n}_{stage}")), k, (k * pair + 1) if n in free else 0)
                    for n, k in names.items()}

        bank = [ctx.enter_context(nc.psum_tensor(f"bank{i}", [P, 512], F32)) for i in range(8)]

        v_win = sb("v_win", [P, B * NJ, D])
        short = sb("short", [P, BT, D])
        delta = sb("delta", [P, BT, D])
        arena = sb("arena", [P, 29400])
        v_tiles = v_win[:, :, :].rearrange("p (t two) c -> p t two c", two=2)

        const_shapes = {n: a.shape[1] for n, a in shape_constants().items() if n not in LATE_CONST}
        const = {n: sb("c_" + n, [P, w]) for n, w in const_shapes.items()}
        ident = const["ident"]
        levels = const["levels"][:, :].rearrange("p (k c) -> p k c", k=LEVELS - 1)
        late = carve(v_win[:, :, :].rearrange("p t c -> p (t c)"), {
            "dft": (2, 4 * P), "idft": (4, HALF), "xq_w": (KT, D), "xkv_w": (KT, 2 * D), "xo_w": (KT, D),
            "ffn_int": (2, KT * HID), "wg": (KT * HID // 2,)})
        dft, idft, xq_w, xkv_w, xo_w = (late[n] for n in ("dft", "idft", "xq_w", "xkv_w", "xo_w"))
        not_dc = const["not_dc"][:, :].rearrange("p (a h) -> p a h", a=2)
        is_dc = const["is_dc"][:, :].rearrange("p (a h) -> p a h", a=2)

        qkv_w = sb("qkv_w", [P, KT, 3 * D])
        ffn = [late["ffn_int"][:, 0, :], late["ffn_int"][:, 1, :], qkv_w[:, :, :].rearrange("p k n -> p (k n)")]
        as_bf16 = lambda w: w.bitcast(BF16)[:, 0:KT * HID].rearrange("p (k n) -> p k n", k=KT)
        wg, wd = as_bf16(late["wg"]), ffn[2].rearrange("p (k n) -> p k n", k=MF)
        stats = sb("stats", [P, BT * 3, 3, H])
        unused = sb("unused", [P, 2, DK])

        def stat_of(b, n, s):
            return stats[:, bass.ds(b * (TT * 3), TT * 3), :, :].rearrange("p (t r) s h -> p t r s h", r=3)[:, :, n - 1, s, :]

        ffn_in = Signal(ctx.enter_context(nc.semaphore("ffn_in")), 0)
        ffn_ready = Signal(ctx.enter_context(nc.semaphore("ffn_ready")), 0)
        beta_w = sb("beta_w", [P, KT, H])
        conv_w = sb("conv_w", [P, 6, CONV_K])
        short_w = sb("short_w", [P, KT, FIR_S])
        g1x_w = sb("g1x_w", [P, KT, GH])
        wu = as_bf16(g1x_w[:, :, :].rearrange("p k n -> p (k n)"))
        g1s_w = sb("g1s_w", [P, GH])
        g1_bias = sb("g1_bias", [P, GH // P])
        g2_w = sb("g2_w", [P, GH // P, NG * H])
        onorm = sb("onorm", [P, 1])
        ow_w = sb("ow_w", [P, KT, D])
        xq_b = sb("xq_b", [1, D])
        xkv_b = sb("xkv_b", [1, 2 * D])
        xo_b = sb("xo_b", [P, D])
        g2_bias = sb("g2_bias", [P, NG * H])
        gate_par = sb("gate_par", [P, 3, H])
        inv_temp = sb("inv_temp", [P, H])
        inv_temp5 = sb("inv_temp5", [P, H, NG])
        floor = sb("floor", [P, H])
        keep = sb("keep", [P, H])
        half_exp = sb("half_exp", [P, 2, 16])

        first_loaded = Signal(ctx.enter_context(nc.semaphore("first_loaded")), 0)
        late_loaded = Signal(ctx.enter_context(nc.semaphore("late_loaded")), 0)
        loaded = Signal(ctx.enter_context(nc.semaphore("loaded")), 0)
        ready = Signal(ctx.enter_context(nc.semaphore("ready")), 0)
        scratch = sb("scratch", [P, 1])[:]
        n_loads = [0]

        A1 = [carve(arena, {"xT": (KT, L), "acc": (KT, L), "vT": (KT, DK + L), "sh": (KT, L)}, at=u * 5000) for u in range(2)]
        free_1 = ("proj", "v_out", "sh_out")
        s1 = signals(1, {
            "xT_in0": 16, "xT_in1": 16, "proj": 2, "tap_last": 2, "conv": 6, "silu": 2, "v_turned": 4, "sh_turned": 2,
            "v_out": 4, "sh_out": 2, "sh_conv": 6, "pads": 0}, free_1, pair=True)

        def tap_one(nc, acc, src, m, j):
            return nc.vector.scalar_tensor_tensor(out=acc[:, j:L], in0=src[:, 0:L - j],
                                                  scalar=conv_w[:, m, CONV_K - 1 - j:CONV_K - j], in1=acc[:, j:L],
                                                  op0=ALU.mult, op1=ALU.add)

        with nc.Block() as block:
            @block.sync
            def _(sp):
                for n in free_1:
                    sp.sem_inc(s1[n].sem, s1[n].base)

                def load_xT(u, b):
                    sp.dma_start(A1[u]["xT"], dr["xT"][b].rearrange("(k p) t -> p k t", p=P))\
                        .then_inc(s1[f"xT_in{u}"].sem, 16)

                def load(dst, src):
                    sp.dma_start(dst, src).then_inc(loaded.sem, 16)
                    n_loads[0] += 1

                load_xT(0, 0)
                sp.dma_start(qkv_w[:], dr["qkv_wT"].rearrange("(k p) n -> p k n", p=P)).then_inc(first_loaded.sem, 16)
                sp.dma_start(conv_w[:], dr["conv_w"].rearrange("(m p) j -> p m j", p=P)).then_inc(first_loaded.sem, 16)
                sp.dma_start(short_w[:], dr["fir_s"].rearrange("(k p) j -> p k j", p=P)).then_inc(first_loaded.sem, 16)
                sp.dma_start(ident[:], dr["c_ident"]).then_inc(first_loaded.sem, 16)
                load_xT(1, 1)
                load(beta_w[:], dr["b_wT"].rearrange("(k p) n -> p k n", p=P))
                for n in const:
                    if n != "ident":
                        load(const[n][:], dr["c_" + n])
                load(g1x_w[:], dr["g1x_wT"].rearrange("(k p) n -> p k n", p=P))
                sp.wait_ge(s1["pads"].sem, 7)
                load(g1s_w[0:36, :], dr["g1s_wT"][0:36, :])
                load(g1s_w[64:88, :], dr["g1s_wT"][36:60, :])
                load(g1_bias[:], dr["g1_b"])
                load(g2_w[:], dr["g2_wT"].rearrange("(k p) n -> p k n", p=P))
                load(onorm[0:DK, :], dr["onorm"].rearrange("(p a) -> p a", a=1))
                load(onorm[DK:P, :], dr["onorm"].rearrange("(p a) -> p a", a=1))
                load(ow_w[:], dr["o_wT"].rearrange("(k p) n -> p k n", p=P))
                load(xq_b[:], dr["xq_b"].rearrange("(a n) -> a n", a=1))
                load(xkv_b[:], dr["xkv_b"].rearrange("(a n) -> a n", a=1))
                load(xo_b[:], dr["xo_b"].partition_broadcast(P))
                load(g2_bias[:], dr["g2_b"].partition_broadcast(P))
                load(gate_par[:, :, :].rearrange("p a h -> p (a h)"), dr["gate_par"].partition_broadcast(P))
                with sp.Fori(1, B // 2) as pair:
                    for u in range(2):
                        sp.wait_ge(s1["proj"].sem, s1["proj"].two_before(pair * 2 + u))
                        load_xT(u, pair * 2 + u)

            @block.tensor
            def _(pe):
                pair_bank = lambda u, m: bank[2 * u + m]

                def project(u, b):
                    pe.wait_ge(s1[f"xT_in{u}"].sem, s1[f"xT_in{u}"].at(pair, 16))
                    pe.wait_ge(s1["sh_out"].sem, s1["sh_out"].two_before(b))
                    for m in range(KT):
                        for k in range(KT):
                            i = nc.tensor.matmul(pair_bank(u, m)[:], qkv_w[:, k, (m + 4) * P:(m + 5) * P], A1[u]["xT"][:, k, :],
                                                 start=(k == 0), stop=(k == KT - 1))
                        i.then_inc(s1["proj"].sem, 1)

                def turn_v(u, b):
                    pe.wait_ge(s1["silu"].sem, s1["silu"].at(b, 2))
                    for w in range(4):
                        pe.wait_ge(s1["v_out"].sem, s1["v_out"].at(b - 1, w + 1))
                        for j in range(2):
                            for k in range(KT):
                                c = (2 * w + j) * DK
                                i = nc.tensor.transpose(bank[4 + w][:, j * D + k * P:j * D + (k + 1) * P],
                                                        A1[u]["vT"][:, k, c:c + P], ident[:])
                        i.then_inc(s1["v_turned"].sem, 1)

                def turn_short(u, b):
                    pe.wait_ge(s1["sh_conv"].sem, s1["sh_conv"].at(b, 6))
                    for i2 in range(2):
                        for t in range(2):
                            for k in range(KT):
                                i = nc.tensor.transpose(pair_bank(u, i2)[:, t * D + k * P:t * D + (k + 1) * P],
                                                        A1[u]["sh"][:, k, (2 * i2 + t) * P:(2 * i2 + t + 1) * P], ident[:])
                        i.then_inc(s1["sh_turned"].sem, 1)

                pe.wait_ge(first_loaded.sem, 16 * 4)
                pe.wait_ge(s1["pads"].sem, 7)
                with pe.Fori(0, B // 2) as pair:
                    b0, b1 = pair * 2, pair * 2 + 1
                    project(0, b0)
                    project(1, b1)
                    turn_v(0, b0)
                    turn_v(1, b1)
                    turn_short(0, b0)
                    turn_short(1, b1)

            @block.scalar
            def _(act):
                a = nc.scalar.activation
                act.wait_ge(first_loaded.sem, 16 * 4)
                def taps_last(u, b):
                    for m in range(KT):
                        act.wait_ge(s1["proj"].sem, s1["proj"].at(b, m + 1))
                        a(A1[u]["acc"][:, m, :], bank[2 * u + m][:], ACT.Copy, scale=conv_w[:, m + 4, CONV_K - 1:CONV_K])\
                            .then_inc(s1["tap_last"].sem, 1)

                def silus(u, b):
                    for m in range(KT):
                        act.wait_ge(s1["conv"].sem, s1["conv"].at(b, 3 * m + 3))
                        a(A1[u]["vT"][:, m, DK:], A1[u]["acc"][:, m, :], ACT.Silu).then_inc(s1["silu"].sem, 1)

                def v_out(u, b):
                    for w in range(4):
                        act.wait_ge(s1["v_turned"].sem, s1["v_turned"].at(b, w + 1))
                        nc.scalar.copy(v_win[:, bass.ds(b * NJ + 2 * w, 2), :],
                                       bank[4 + w][:].rearrange("p (t c) -> p t c", t=2)).then_inc(s1["v_out"].sem, 1)

                def short_out(u, b):
                    for i2 in range(2):
                        act.wait_ge(s1["sh_turned"].sem, s1["sh_turned"].at(b, i2 + 1))
                        nc.scalar.copy(short[:, bass.ds(b * TT + 2 * i2, 2), :],
                                       bank[2 * u + i2][:].rearrange("p (t c) -> p t c", t=2)).then_inc(s1["sh_out"].sem, 1)

                with act.Fori(0, B // 2) as pair:
                    b0, b1 = pair * 2, pair * 2 + 1
                    taps_last(0, b0)
                    taps_last(1, b1)
                    silus(0, b0)
                    v_out(0, b0)
                    silus(1, b1)
                    v_out(1, b1)
                    short_out(0, b0)
                    short_out(1, b1)
                act.wait_ge(loaded.sem, 16 * n_loads[0])
                a(inv_temp[:], gate_par[:, 1, :], ACT.Exp, scale=-1.0).then_inc(ready.sem, 1)
                a(floor[:], gate_par[:, 2, :], ACT.Tanh, scale=0.5).then_inc(ready.sem, 1)

            @block.vector
            def _(dve):
                v = nc.vector
                v.memset(g1s_w[32:64, :], 0.0).then_inc(s1["pads"].sem, 1)
                dve.wait_ge(first_loaded.sem, 16 * 4)
                dve.wait_ge(s1["pads"].sem, 7)

                def conv(u, b):
                    for m in range(KT):
                        for j in range(1, CONV_K):
                            if j == 1:
                                dve.wait_ge(s1["tap_last"].sem, s1["tap_last"].at(b, m + 1))
                            else:
                                dve.wait_ge(s1["conv"].sem, s1["conv"].at(b, 3 * m + j - 1))
                            tap_one(nc, A1[u]["acc"][:, m, :], bank[2 * u + m], m + 4, j).then_inc(s1["conv"].sem, 1)

                def short_conv(u, b):
                    dve.wait_ge(s1["silu"].sem, s1["silu"].at(b, 2))
                    for k in range(KT):
                        for j in range(FIR_S):
                            src = A1[u]["vT"][:, k, DK - j:DK - j + L]
                            w = short_w[:, k, FIR_S - 1 - j:FIR_S - j]
                            if j == 0:
                                dve.wait_ge(s1["sh_out"].sem, s1["sh_out"].two_before(b))
                                v.tensor_scalar(A1[u]["sh"][:, k, :], src, w, None, ALU.mult).then_inc(s1["sh_conv"].sem, 1)
                                continue
                            dve.wait_ge(s1["sh_conv"].sem, s1["sh_conv"].at(b, FIR_S * k + j))
                            v.scalar_tensor_tensor(out=A1[u]["sh"][:, k, :], in0=src, scalar=w, in1=A1[u]["sh"][:, k, :],
                                                   op0=ALU.mult, op1=ALU.add).then_inc(s1["sh_conv"].sem, 1)

                with dve.Fori(0, B // 2) as pair:
                    b0, b1 = pair * 2, pair * 2 + 1
                    conv(0, b0)
                    conv(1, b1)
                    short_conv(0, b0)
                    short_conv(1, b1)
                dve.wait_ge(loaded.sem, 16 * n_loads[0])
                dve.wait_ge(ready.sem, 2)
                v.tensor_copy(inv_temp5[:], over_last(inv_temp[:], NG)).then_inc(ready.sem, 1)
                v.tensor_scalar(floor[:], floor[:], 0.5, 0.5, ALU.mult, ALU.add).then_inc(ready.sem, 1)
                dve.wait_ge(ready.sem, 4)
                v.tensor_scalar(keep[:], floor[:], -4.0, 1.0, ALU.mult, ALU.add).then_inc(ready.sem, 1)
                g2b = g2_bias[:].rearrange("p (h g) -> p h g", g=NG)
                v.tensor_tensor(g2b[:, :, NG - 1], g2b[:, :, NG - 1], gate_par[:, 0, :], ALU.add).then_inc(ready.sem, 1)

            @block.gpsimd
            def _(pool):
                g = nc.gpsimd
                for u in range(2):
                    g.memset(A1[u]["vT"][:, 0, 0:DK], 0.0).then_inc(s1["pads"].sem, 1)
                    g.memset(A1[u]["vT"][:, 1, 0:DK], 0.0).then_inc(s1["pads"].sem, 1)
                g.memset(half_exp[:, 0, :], -0.5).then_inc(s1["pads"].sem, 1)
                g.memset(half_exp[:, 1, :], 0.5).then_inc(s1["pads"].sem, 1)

        WL = B * NJ * D
        wl = arena[:, 0:WL].rearrange("p (j c) -> p j c", c=D)
        TOEP = 2 * DK * PIECE
        toep = [arena[:, WL + i * TOEP:WL + (i + 1) * TOEP].rearrange("p (f c) -> p f c", c=PIECE) for i in range(TOEP_BUFS)]
        A2 = carve(arena, {
            "xT": (KT, L), "acc": (4, L), "qT": (KT, L), "kT": (KT, L), "k_tok": (TT, D), "v_sc": (TT, D),
            "AL": (TT, H, P), "ALT": (TT, H, P), "atT": (TT, H, P), "X": (TT, H, P), "R": (D,), "U": (D,),
            "S": (2, KT, P), "ss": (32,), "rn": (2, TT, H), "rec": (16,), "th": (16,), "C": (TT, H),
            "v_piece": (2, B * NJ, PIECE)},
            at=WL + TOEP_BUFS * TOEP)
        A2["XT"] = A2["AL"]
        A2["sq"] = A2["ALT"].rearrange("p t h c -> p t (h c)")
        k_sq = A2["ALT"].rearrange("p t h c -> p (t h c)")[:, 0:TT * D]
        A2["Z"] = A2["acc"][:, 0:2, :].rearrange("p a c -> p (a c)").rearrange("p (t h c) -> p t h c", t=TT, h=H)
        free_2 = ("o_out", "fir_mm")
        s2 = signals(2, {
            "xT_in": 16, "proj": 4, "tap_last": 4, "conv": 12, "silu": 4, "squares": 2, "beta_mm": 1, "ssq_mm": 1, "k_sums": 2,
            "k_turned": 2, "k_out": 2, "beta_th": 1, "ss_eps": 2, "norms": 1, "c_steps": 3, "gram": 4, "a_scaled": 16,
            "attn_mm": 4, "attn_out": 8, "v_scaled": 1, "x_first": 8, "a_turned": 4, "at_out": 4, "z_mm": 12,
            "z_out": 12, "w_mm": 12, "x_out": 12, "x_turned": 28, "xt_out": 24, "xt_last": 4, "ks_mm": 3, "r_out": 3,
            "u_mm": 4, "u_out": 4, "s_mm": 3, "s_out": 3, "o_mm": 4, "o_out": 4, "v_copied": PER_BATCH,
            "fir_mm": PER_BATCH, "fir_out": PER_BATCH, "early_sq": 32}, free_2)
        s2["fir_mm"].base = 2
        toep_in = [Signal(ctx.enter_context(nc.semaphore(f"toep_in{i}")), 32 * PER_BATCH // TOEP_BUFS)
                   for i in range(TOEP_BUFS)]
        TURN_BANKS = (2, 6, 7)
        turn_bank = lambda i: bank[TURN_BANKS[i % 3]]
        pair_half = lambda first, t: bank[first + t // 2][:, (t % 2) * D:(t % 2 + 1) * D]

        def branch(n, b):
            if n == 0:
                src = wl[:, bass.ds(b * NJ, NJ), :]
            elif n == 3:
                src = v_tiles[:, bass.ds(b * TT, TT), 1, :]
            else:
                src = [short, delta][n - 1][:, bass.ds(b * TT, TT), :]
            return src.rearrange("p t (h c) -> p t h c", h=H)

        def evens(ap, k):
            return ap.rearrange("p h (g two s) -> p (h g) two s", two=2, s=1 << k)[:, :, 0, :]

        with nc.Block() as block:
            @block.sync
            def _(sp):
                for n in free_2:
                    sp.sem_inc(s2[n].sem, s2[n].base)

                def load_xT(b):
                    sp.dma_start(A2["xT"], dr["xT"][b].rearrange("(k p) t -> p k t", p=P)).then_inc(s2["xT_in"].sem, 16)

                def load_toep(i, piece):
                    for f in range(2):
                        src = dr[("toep_w", "toep_l")[f]][piece]
                        src = bass.AP(src.tensor, src.offset, [[PIECE, P], [1, DK * PIECE]])
                        sp.dma_start(toep[i][:, f * DK:(f + 1) * DK, :].rearrange("p f c -> p (f c)"), src)\
                            .then_inc(toep_in[i].sem, 16)

                def round_(b, more):
                    if more:
                        sp.wait_ge(s2["beta_mm"].sem, s2["beta_mm"].at(b, 1))
                        load_xT(b + 1)
                    for n in range(PER_BATCH):
                        if more or n + TOEP_BUFS < PER_BATCH:
                            sp.wait_ge(s2["fir_mm"].sem, s2["fir_mm"].at(b, n + 1))
                            load_toep(n % TOEP_BUFS, b * PER_BATCH + (n + TOEP_BUFS))

                load_xT(0)
                for n in range(TOEP_BUFS):
                    load_toep(n, n)
                with sp.Fori(0, B - 1) as b:
                    round_(b, True)
                round_(B - 1, False)

            @block.tensor
            def _(pe):
                mm = nc.tensor.matmul

                def narrow(dst, stationary, moving):
                    for c in (0, DK):
                        i = mm(dst[c:c + DK, :], stationary[:, c:c + DK], moving, start=True, stop=True)
                    return i

                def project(b, m):
                    if m == 0:
                        pe.wait_ge(s2["xT_in"].sem, s2["xT_in"].at(b, 16))
                    if m >= 2:
                        pe.wait_ge(s2["conv"].sem, s2["conv"].at(b, 3 * (m - 1)))
                    for k in range(KT):
                        i = mm(bank[m % 2][:], qkv_w[:, k, m * P:(m + 1) * P], A2["xT"][:, k, :],
                               start=(k == 0), stop=(k == KT - 1))
                    i.then_inc(s2["proj"].sem, 1)

                def beta(b):
                    for t in range(TT):
                        for k in range(KT):
                            i = mm(bank[2][:, t * H:(t + 1) * H], A2["xT"][:, k, t * P:(t + 1) * P], beta_w[:, k, :],
                                   start=(k == 0), stop=(k == KT - 1))
                    i.then_inc(s2["beta_mm"].sem, 1)

                def filter_piece(b, n):
                    pe.wait_ge(toep_in[n % TOEP_BUFS].sem, toep_in[n % TOEP_BUFS].at(b, 32 * (n // TOEP_BUFS + 1)))
                    pe.wait_ge(s2["v_copied"].sem, s2["v_copied"].at(b, n + 1))
                    if n:
                        pe.wait_ge(s2["fir_out"].sem, s2["fir_out"].at(b, n))
                    for c in range(PIECE):
                        i = narrow(bank[3][:, c * B * NJ:(c + 1) * B * NJ], toep[n % TOEP_BUFS][:, :, c],
                                   A2["v_piece"][:, n % 2, :, c])
                    i.then_inc(s2["fir_mm"].sem, 1)

                def turn_free(b, i):
                    i -= 3
                    if i < 0:
                        if i == -3:
                            pe.wait_ge(s2["ss_eps"].sem, s2["ss_eps"].at(b, 2))
                        pe.wait_ge(s2["a_scaled"].sem, s2["a_scaled"].at(b, H * TT))
                        return
                    if i < TT:
                        pe.wait_ge(s2["at_out"].sem, s2["at_out"].at(b, i + 1))
                    elif i < TT + 24:
                        pe.wait_ge(s2["xt_out"].sem, s2["xt_out"].at(b, i + 1 - TT))
                    else:
                        pe.wait_ge(s2["xt_last"].sem, s2["xt_last"].at(b, i + 1 - TT - 24))

                def turn_x(b, k, t):
                    n = TT * k + t
                    if k == 0:
                        pe.wait_ge(s2["x_first"].sem, s2["x_first"].at(b, 2 * t + 2))
                    else:
                        pe.wait_ge(s2["x_out"].sem, s2["x_out"].at(b, n // 2 - 1))
                    turn_free(b, TT + n)
                    for h in range(H):
                        i = nc.tensor.transpose(turn_bank(TT + n)[:, h * P:(h + 1) * P], A2["X"][:, t, h, :], ident[:])
                    i.then_inc(s2["x_turned"].sem, 1)

                def round_(b, more):
                    filter_piece(b, 0)
                    pe.wait_ge(s2["silu"].sem, s2["silu"].at(b, 2))
                    pe.wait_ge(s2["o_out"].sem, s2["o_out"].at(b, 0))
                    for i2 in range(2):
                        for t in range(2):
                            for k in range(KT):
                                i = nc.tensor.transpose(bank[4 + i2][:, t * D + k * P:t * D + (k + 1) * P],
                                                        A2["kT"][:, k, (2 * i2 + t) * P:(2 * i2 + t + 1) * P], ident[:])
                        i.then_inc(s2["k_turned"].sem, 1)
                    pe.wait_ge(s2["k_out"].sem, s2["k_out"].at(b, 2))
                    for t in range(TT):
                        if t >= 2:
                            pe.wait_ge(s2["a_scaled"].sem, s2["a_scaled"].at(b, H * (t - 1)))
                        for h in range(H):
                            r, k = DK * (h % 2), h // 2
                            kk = A2["kT"][r:r + DK, k, t * P:(t + 1) * P]
                            i = mm(bank[4 + 2 * (t % 2) + h % 2][:, k * P:(k + 1) * P], kk, kk, start=True, stop=True)
                        i.then_inc(s2["gram"].sem, 1)
                        if t:
                            pe.wait_ge(s2["attn_out"].sem, s2["attn_out"].at(b, 2 * t))
                        else:
                            pe.wait_ge(s2["silu"].sem, s2["silu"].at(b, 4))
                        for h in range(H):
                            r, k = DK * (h % 2), h // 2
                            i = mm(bank[h % 2][:, k * P:(k + 1) * P], A2["kT"][r:r + DK, k, t * P:(t + 1) * P],
                                   A2["qT"][r:r + DK, k, t * P:(t + 1) * P], start=True, stop=True)
                        i.then_inc(s2["attn_mm"].sem, 1)
                    pe.wait_ge(s2["squares"].sem, s2["squares"].at(b, 2))
                    pe.wait_ge(s2["beta_th"].sem, s2["beta_th"].at(b, 1))
                    for m in range(KT):
                        for t in range(TT):
                            c = 16 + t * H + 2 * m
                            i = narrow(bank[2][:, c:c + 2], A2["sq"][:, m + 2, t * P:(t + 1) * P], const["heads"][:])
                    i.then_inc(s2["ssq_mm"].sem, 1)
                    for t in range(TT):
                        pe.wait_ge(s2["a_scaled"].sem, s2["a_scaled"].at(b, H * (t + 1)))
                        turn_free(b, t)
                        for h in range(H):
                            i = nc.tensor.transpose(turn_bank(t)[:, h * P:(h + 1) * P], A2["AL"][:, t, h, :], ident[:])
                        i.then_inc(s2["a_turned"].sem, 1)
                    filter_piece(b, 1)
                    for k in range(1, LEVELS):
                        for t in range(TT):
                            n = TT * (k - 1) + t
                            if k == 1:
                                pe.wait_ge(s2["x_first"].sem, s2["x_first"].at(b, 2 * t + 2))
                                pe.wait_ge(s2["at_out"].sem, s2["at_out"].at(b, t + 1))
                                pe.wait_ge(s2["attn_out"].sem, s2["attn_out"].at(b, 2 * TT))
                            else:
                                pe.wait_ge(s2["x_out"].sem, s2["x_out"].at(b, n // 2 - 1))
                            for h in range(H):
                                i = narrow(pair_half(0, t)[:, h * DK:(h + 1) * DK], A2["ALT"][:, t, h, :],
                                           A2["X"][:, t, h, :].rearrange("p (g two s) -> p g two s", two=2, s=1 << k)[:, :, 0, :])
                            if t % 2:
                                i.then_inc(s2["z_mm"].sem, 1)
                                turn_x(b, k - 1, t - 1)
                                turn_x(b, k - 1, t)
                        for t in range(TT):
                            n = TT * (k - 1) + t
                            pe.wait_ge(s2["z_out"].sem, s2["z_out"].at(b, n // 2 + 1))
                            pe.wait_ge(s2["xt_out"].sem, s2["xt_out"].at(b, n + 1))
                            for h in range(H):
                                i = narrow(pair_half(4, t)[:, h * DK:(h + 1) * DK], A2["XT"][:, t, h, :], A2["Z"][:, t, h, :])
                            if t % 2:
                                i.then_inc(s2["w_mm"].sem, 1)
                        filter_piece(b, 1 + k)
                    for t in range(TT):
                        turn_x(b, LEVELS - 1, t)
                    for t in range(TT):
                        tok = slice(t * P, (t + 1) * P)
                        if more:
                            project(b + 1, t)
                        if t:
                            pe.wait_ge(s2["s_out"].sem, s2["s_out"].at(b, t))
                            for p in range(KT):
                                i = mm(bank[2][:, p * P:(p + 1) * P], A2["kT"][:, p, tok], A2["S"][:, t % 2, p, :],
                                       start=True, stop=True)
                            i.then_inc(s2["ks_mm"].sem, 1)
                            pe.wait_ge(s2["r_out"].sem, s2["r_out"].at(b, t))
                            pe.wait_ge(s2["u_out"].sem, s2["u_out"].at(b, t))
                        else:
                            pe.wait_ge(s2["v_scaled"].sem, s2["v_scaled"].at(b, 1))
                            pe.wait_ge(s2["x_out"].sem, s2["x_out"].at(b, 12))
                        pe.wait_ge(s2["xt_last"].sem, s2["xt_last"].at(b, t + 1))
                        rhs = A2["R"] if t else A2["v_sc"][:, 0, :]
                        for h in range(H):
                            i = narrow(bank[4][:, h * DK:(h + 1) * DK], A2["XT"][:, t, h, :], rhs[:, h * DK:(h + 1) * DK])
                        i.then_inc(s2["u_mm"].sem, 1)
                        pe.wait_ge(s2["u_out"].sem, s2["u_out"].at(b, t + 1))
                        if t < TT - 1:
                            for p in range(KT):
                                i = mm(bank[5][:, p * P:(p + 1) * P], A2["k_tok"][:, t, p * P:(p + 1) * P],
                                       A2["U"][:, p * P:(p + 1) * P], start=(t == 0 and p == 0),
                                       stop=(t == TT - 2 and p == KT - 1), skip_group_check=True)
                            i.then_inc(s2["s_mm"].sem, 1)
                        if t >= 2:
                            pe.wait_ge(s2["o_out"].sem, s2["o_out"].at(b, t - 1))
                        else:
                            pe.wait_ge(s2["xt_last"].sem, s2["xt_last"].at(b, TT))
                        if t:
                            for p in range(KT):
                                mm(bank[6 + t % 2][:, p * P:(p + 1) * P], A2["qT"][:, p, tok], A2["S"][:, t % 2, p, :],
                                   start=(p == 0), stop=False, skip_group_check=True)
                        for h in range(H):
                            i = mm(bank[6 + t % 2][:, h * DK:(h + 1) * DK], A2["atT"][:, t, h, :],
                                   A2["U"][:, h * DK:(h + 1) * DK], start=(t == 0 and h == 0), stop=(h == H - 1),
                                   skip_group_check=True)
                        i.then_inc(s2["o_mm"].sem, 1)
                    pe.wait_ge(s2["fir_out"].sem, s2["fir_out"].at(b, PER_BATCH))
                    if more:
                        beta(b + 1)

                for m in range(4):
                    project(0, m)
                beta(0)
                with pe.Fori(0, B - 1) as b:
                    round_(b, True)
                round_(B - 1, False)

            @block.scalar
            def _(act):
                a = nc.scalar.activation

                def head_squares(b, i, order):
                    n, t, h = (1, 3)[i // (TT * H)], (i // H) % TT, i % H
                    if order >= 2:
                        act.wait_ge(s2["early_sq"].sem, s2["early_sq"].at(b, order - 1))
                    a(unused[:, order % 2, :], branch(n, b)[:, t, h, :], ACT.Square,
                      accum_out=stat_of(b, n, 1)[:, t, h:h + 1]).then_inc(s2["early_sq"].sem, 1)

                def tap_last(b, m):
                    act.wait_ge(s2["proj"].sem, s2["proj"].at(b, m + 1))
                    a(A2["acc"][:, m, :], bank[m % 2][:], ACT.Copy, scale=conv_w[:, m, CONV_K - 1:CONV_K])\
                        .then_inc(s2["tap_last"].sem, 1)

                def filter_out(b, n):
                    act.wait_ge(s2["fir_mm"].sem, s2["fir_mm"].at(b, n + 1))
                    nc.scalar.copy(wl[:, :, bass.ds(b * (PER_BATCH * PIECE) + n * PIECE, PIECE)],
                                   bank[3][:, 0:D].rearrange("p (c j) -> p j c", c=PIECE)).then_inc(s2["fir_out"].sem, 1)

                def beta_tanh(b):
                    act.wait_ge(s2["beta_mm"].sem, s2["beta_mm"].at(b, 1))
                    a(A2["th"], bank[2][:, 0:16], ACT.Tanh, scale=0.5).then_inc(s2["beta_th"].sem, 1)

                def round_(b, more):
                    act.wait_ge(s2["o_out"].sem, s2["o_out"].at(b, 0))
                    for m in range(4):
                        if m == 2:
                            for i2 in range(2):
                                act.wait_ge(s2["k_turned"].sem, s2["k_turned"].at(b, i2 + 1))
                                nc.scalar.copy(A2["k_tok"][:, 2 * i2:2 * i2 + 2, :],
                                               bank[4 + i2][:].rearrange("p (t c) -> p t c", t=2))\
                                    .then_inc(s2["k_out"].sem, 1)
                        act.wait_ge(s2["conv"].sem, s2["conv"].at(b, 3 * m + 3))
                        a([A2["kT"], A2["qT"]][m // 2][:, m % 2, :], A2["acc"][:, m, :], ACT.Silu)\
                            .then_inc(s2["silu"].sem, 1)
                    for m in range(KT):
                        act.wait_ge(s2["silu"].sem, s2["silu"].at(b, m + 3))
                        a(A2["sq"][:, m + 2, :], A2["qT"][:, m, :], ACT.Square).then_inc(s2["squares"].sem, 1)
                    filter_out(b, 0)
                    for t in range(TT):
                        act.wait_ge(s2["a_turned"].sem, s2["a_turned"].at(b, t + 1))
                        nc.scalar.copy(A2["ALT"][:, t, :, :], turn_bank(t)[:].rearrange("p (h c) -> p h c", h=H))\
                            .then_inc(s2["at_out"].sem, 1)
                    for n in range(TT * (LEVELS - 1)):
                        if n % TT == 0:
                            filter_out(b, n // TT + 1)
                        act.wait_ge(s2["x_turned"].sem, s2["x_turned"].at(b, n + 1))
                        nc.scalar.copy(A2["XT"][:, n % TT, :, :], turn_bank(TT + n)[:].rearrange("p (h c) -> p h c", h=H))\
                            .then_inc(s2["xt_out"].sem, 1)
                        head_squares(b, n, n + (n + 2) // 3)
                        if n % 3 == 0:
                            head_squares(b, 24 + n // 3, n + n // 3 + 1)
                    filter_out(b, PER_BATCH - 1)
                    if more:
                        act.wait_ge(s2["w_mm"].sem, s2["w_mm"].at(b, 12))
                    for t in range(TT):
                        if more:
                            tap_last(b + 1, t)
                        act.wait_ge(s2["u_mm"].sem, s2["u_mm"].at(b, t + 1))
                        nc.scalar.copy(A2["U"], bank[4][:, 0:D]).then_inc(s2["u_out"].sem, 1)
                    if more:
                        beta_tanh(b + 1)

                for m in range(4):
                    tap_last(0, m)
                beta_tanh(0)
                with act.Fori(0, B - 1) as b:
                    round_(b, True)
                round_(B - 1, False)

            @block.vector
            def _(dve):
                v = nc.vector

                def conv(b, m):
                    for j in range(1, CONV_K):
                        if j == 1:
                            dve.wait_ge(s2["tap_last"].sem, s2["tap_last"].at(b, m + 1))
                        else:
                            dve.wait_ge(s2["conv"].sem, s2["conv"].at(b, 3 * m + j - 1))
                        tap_one(nc, A2["acc"][:, m, :], bank[m % 2], m, j).then_inc(s2["conv"].sem, 1)

                def round_(b, more):
                    dve.wait_ge(s2["beta_th"].sem, s2["beta_th"].at(b, 1))
                    v.tensor_scalar(A2["th"], A2["th"], 0.5, 0.5, ALU.mult, ALU.add).then_inc(s2["c_steps"].sem, 1)
                    dve.wait_ge(s2["k_out"].sem, s2["k_out"].at(b, 2))
                    flat = A2["k_tok"].rearrange("p t c -> p (t c)")
                    v.tensor_tensor(k_sq, flat, flat, ALU.mult).then_inc(s2["k_sums"].sem, 1)
                    dve.wait_ge(s2["k_sums"].sem, s2["k_sums"].at(b, 1))
                    v.tensor_reduce(A2["ss"][:, 16:32], k_sq.rearrange("p (g c) -> p g c", c=DK), AX.X, ALU.add)\
                        .then_inc(s2["k_sums"].sem, 1)
                    dve.wait_ge(s2["k_sums"].sem, s2["k_sums"].at(b, 2))
                    v.tensor_scalar(A2["ss"][:, 16:32], A2["ss"][:, 16:32], 1e-6, None, ALU.add).then_inc(s2["ss_eps"].sem, 1)
                    dve.wait_ge(s2["ss_eps"].sem, s2["ss_eps"].at(b, 1))
                    v.reciprocal(A2["rec"], A2["ss"][:, 16:32]).then_inc(s2["c_steps"].sem, 1)
                    dve.wait_ge(s2["c_steps"].sem, s2["c_steps"].at(b, 2))
                    v.tensor_tensor(A2["C"].rearrange("p t h -> p (t h)"), A2["rec"], A2["th"],
                                    ALU.mult).then_inc(s2["c_steps"].sem, 1)
                    dve.wait_ge(s2["c_steps"].sem, s2["c_steps"].at(b, 3))
                    for t in range(TT):
                        dve.wait_ge(s2["gram"].sem, s2["gram"].at(b, t + 1))
                        for h in range(H):
                            v.scalar_tensor_tensor(out=A2["AL"][:, t, h, :],
                                                   in0=bank[4 + 2 * (t % 2) + h % 2][:, (h // 2) * P:(h // 2 + 1) * P],
                                                   scalar=A2["C"][:, t, h:h + 1], in1=const["mask_lower"][:],
                                                   op0=ALU.mult, op1=ALU.mult).then_inc(s2["a_scaled"].sem, 1)
                        dve.wait_ge(s2["attn_mm"].sem, s2["attn_mm"].at(b, t + 1))
                        for e in range(2):
                            v.tensor_tensor(A2["atT"][:, t, e::2, :], bank[e][:, 0:D].rearrange("p (h c) -> p h c", h=2),
                                            over_tiles(const["mask_upper"][:], 2), ALU.mult).then_inc(s2["attn_out"].sem, 1)
                        dve.wait_ge(s2["a_scaled"].sem, s2["a_scaled"].at(b, H * (t + 1)))
                        v.tensor_tensor(A2["X"][:, t, :, :], A2["AL"][:, t, :, :], over_tiles(const["level0"][:], H),
                                        ALU.mult).then_inc(s2["x_first"].sem, 1)
                        dve.wait_ge(s2["x_first"].sem, s2["x_first"].at(b, 2 * t + 1))
                        v.tensor_tensor(A2["X"][:, t, :, :], A2["X"][:, t, :, :], over_tiles(ident[:], H),
                                        ALU.add).then_inc(s2["x_first"].sem, 1)
                    dve.wait_ge(s2["ssq_mm"].sem, s2["ssq_mm"].at(b, 1))
                    v.tensor_scalar(A2["ss"][:, 0:16], bank[2][:, 16:32], 1e-6, None, ALU.add).then_inc(s2["ss_eps"].sem, 1)
                    for k in range(1, LEVELS):
                        for i in range(2):
                            dve.wait_ge(s2["z_mm"].sem, s2["z_mm"].at(b, 2 * k - 1 + i))
                            v.tensor_tensor(A2["Z"][:, 2 * i:2 * i + 2, :, :].rearrange("p t h c -> p (t h) c"),
                                            bank[i][:].rearrange("p (g c) -> p g c", c=DK),
                                            over_tiles(levels[:, k - 1, :], 2 * H), ALU.mult).then_inc(s2["z_out"].sem, 1)
                        if 2 <= k <= 5:
                            n, s = (1, 3)[(k - 2) // 2], (0, 2)[k % 2]
                            if s == 0:
                                v.tensor_reduce(stat_of(b, n, 0), branch(n, b), AX.X, ALU.add)
                            else:
                                v.tensor_reduce(stat_of(b, n, 2), branch(n, b), AX.X, ALU.max, apply_absolute_value=True)
                        for i in range(2):
                            dve.wait_ge(s2["w_mm"].sem, s2["w_mm"].at(b, 2 * k - 1 + i))
                            x = evens(A2["X"][:, 2 * i:2 * i + 2, :, :].rearrange("p t h c -> p (t h) c"), k)
                            v.tensor_tensor(x, x, bank[4 + i][:].rearrange("p (g s) -> p g s", s=1 << k),
                                            ALU.subtract).then_inc(s2["x_out"].sem, 1)
                    for t in range(TT):
                        dve.wait_ge(s2["x_turned"].sem, s2["x_turned"].at(b, TT * (LEVELS - 1) + t + 1))
                        v.tensor_tensor(A2["XT"][:, t, :, :], turn_bank(TT * LEVELS + t)[:].rearrange("p (h c) -> p h c", h=H),
                                        over_last(A2["C"][:, t, :], P), ALU.mult).then_inc(s2["xt_last"].sem, 1)
                    for t in range(TT):
                        if t:
                            dve.wait_ge(s2["ks_mm"].sem, s2["ks_mm"].at(b, t))
                            v.tensor_tensor(A2["R"], A2["v_sc"][:, t, :], bank[2][:, 0:D],
                                            ALU.subtract).then_inc(s2["r_out"].sem, 1)
                        if more:
                            conv(b + 1, t)
                        if t < TT - 1:
                            dve.wait_ge(s2["s_mm"].sem, s2["s_mm"].at(b, t + 1))
                            v.tensor_tensor(A2["S"][:, (t + 1) % 2, :, :], bank[5][:, 0:D].rearrange("p (k c) -> p k c", k=KT),
                                            over_tiles(const["blocks"][:], KT), ALU.mult).then_inc(s2["s_out"].sem, 1)
                        if t == 0:
                            dve.wait_ge(s2["norms"].sem, s2["norms"].at(b, 1))
                        dve.wait_ge(s2["o_mm"].sem, s2["o_mm"].at(b, t + 1))
                        v.tensor_tensor(delta[:, b * TT + t, :].rearrange("p (h c) -> p h c", h=H),
                                        bank[6 + t % 2][:, 0:D].rearrange("p (h c) -> p h c", h=H),
                                        over_last(A2["rn"][:, 0, t, :], DK), ALU.mult).then_inc(s2["o_out"].sem, 1)

                for m in range(4):
                    conv(0, m)
                with dve.Fori(0, B - 1) as b:
                    round_(b, True)
                round_(B - 1, False)

            @block.gpsimd
            def _(pool):
                g = nc.gpsimd
                with pool.Fori(0, B) as b:
                    for n in range(PER_BATCH):
                        pool.wait_ge(s2["fir_mm"].sem, s2["fir_mm"].at(b, n - 1))
                        g.tensor_copy(A2["v_piece"][:, n % 2, :, :], v_win[:, :, bass.ds(b * (PER_BATCH * PIECE) + n * PIECE, PIECE)])\
                            .then_inc(s2["v_copied"].sem, 1)
                        if n == 1:
                            pool.wait_ge(s2["ss_eps"].sem, s2["ss_eps"].at(b, 2))
                            g.tensor_tensor(A2["rn"].rearrange("p a t h -> p (a t h)"), A2["ss"],
                                            half_exp[:, :, :].rearrange("p a n -> p (a n)"), ALU.pow).then_inc(s2["norms"].sem, 1)
                        if n == 2:
                            pool.wait_ge(s2["norms"].sem, s2["norms"].at(b, 1))
                            g.tensor_tensor(A2["v_sc"].rearrange("p t (h c) -> p t h c", h=H),
                                            v_tiles[:, bass.ds(b * TT, TT), 1, :].rearrange("p t (h c) -> p t h c", h=H),
                                            over_last(A2["rn"][:, 1, :, :], DK), ALU.mult).then_inc(s2["v_scaled"].sem, 1)

        A3 = []
        for u in range(2):
            a3 = carve(arena, {
                "xT": (KT, L), "x": (TT, D), "tw": (NJ, 3, H), "sw": (NJ, 24), "statT": (L,),
                "hdnT": (GH // P, L), "lg": (TT, H, NG), "mx": (TT, H), "w": (TT, H, NG), "wsel": (2, TT, H),
                "sq_b": (1024,), "sq_a": (2048,), "pv": (TT, D), "ps": (TT, D), "ssh": (TT * H,),
                "rh": (TT * H,), "ln": (TT, 6), "mv": (TT, 2), "ve": (TT,), "rs": (TT,)}, at=B * NJ * D + u * 10600)
            a3["pwl"] = a3["hdnT"].rearrange("p k c -> p (k c)").rearrange("p (t a c) -> p t a c", t=TT, a=2)
            a3["onT"] = a3["hdnT"][:, 0:KT, :]
            a3["pd"] = a3["sq_a"][:, 0:TT * D].rearrange("p (t c) -> p t c", t=TT)
            a3["on"], a3["xr"] = a3["pv"], a3["ps"]
            A3.append(a3)
        SEEN = (2, 0)
        free_3 = ("hdn_mm", "oT_out", "o_norm", "sq_used", "res")
        s3 = signals(3, {
            "xT3_in0": 16, "xT3_in1": 16, "x3_in0": 16, "x3_in1": 16, "sq_out": 2, "red": 4, "sq_used": 2, "small": 4, "roots": 2, "sw_out": 2,
            "st_turned": 2, "st_out": 2, "hdn_mm": 4, "gelu": 4, "lg_mm": 1, "lg_pre": 4, "lg_exp": 1, "lg_post": 5,
            "w_twice": 1, "w_sel": 2, "p_wl": 2, "p_v": 1, "p_sd": 2, "mix_mm": 2, "mix_sq": 2, "mix_ss": 3,
            "r_head": 1, "o_turned": 2, "o_norm": 2, "oT_out": 2, "y_mm": 2, "res": 2, "ln_st": 9, "ln_rs": 1,
            "x1_out": 4, "zeros3": 0}, free_3, pair=True)

        def stat(u, b, n, s):
            return A3[u]["tw"][:, :, s, :] if n == 0 else stat_of(b, n, s)

        def of_batch(b):
            return stats[:, b * TT * 3:(b + 1) * TT * 3, :, :]

        def squares_of(u, i):
            T = NJ if SEEN[i] == 0 else TT
            return A3[u][("sq_b", "sq_a")[i % 2]][:, 0:T * D].rearrange("p (t h c) -> p t h c", t=T, h=H)

        mix_bank = lambda u, i2: bank[(6, 0)[u] + i2]
        y_bank = lambda u, i2: bank[(4, 6)[u] + i2]

        with nc.Block() as block:
            @block.sync
            def _(sp):
                for n in free_3:
                    sp.sem_inc(s3[n].sem, s3[n].base)
                with sp.Fori(0, B // 2) as pair:
                    for u in range(2):
                        b = pair * 2 + u
                        sp.wait_ge(s3["hdn_mm"].sem, s3["hdn_mm"].two_before(b))
                        sp.dma_start(A3[u]["xT"], dr["xT"][b].rearrange("(k p) t -> p k t", p=P))\
                            .then_inc(s3[f"xT3_in{u}"].sem, 16)
                        sp.wait_ge(s3["res"].sem, s3["res"].two_before(b))
                        sp.dma_start(A3[u]["x"], dr["x"][b].rearrange("(t p) d -> p t d", p=P))\
                            .then_inc(s3[f"x3_in{u}"].sem, 16)
                sp.wait_ge(s3["p_v"].sem, s3["p_v"].at(B, 0))
                for n in LATE_CONST:
                    sp.dma_start(late[n].rearrange("p k f -> p (k f)"), dr["c_" + n]).then_inc(late_loaded.sem, 16)
                for n in ("xq_w", "xkv_w", "xo_w"):
                    sp.dma_start(late[n], dr[n + "T"].rearrange("(k p) n -> p k n", p=P)).then_inc(late_loaded.sem, 16)
                for w, (n, k) in zip(ffn, (("w_gateT", KT), ("w_upT", KT), ("w_downT", MF))):
                    sp.dma_start(w.bitcast(I32).rearrange("p (k n) -> p k n", k=k),
                                 dr[n].rearrange("(k p) n -> p k n", p=P)).then_inc(ffn_in.sem, 16)

            @block.tensor
            def _(pe):
                mm = nc.tensor.matmul

                def statistics(u, b):
                    pe.wait_ge(s3["sw_out"].sem, s3["sw_out"].at(b, 2))
                    pe.wait_ge(s3["roots"].sem, s3["roots"].at(b, 2))
                    if u == 0:
                        pe.wait_ge(s3["o_norm"].sem, s3["o_norm"].at(b, 0))
                    else:
                        pe.wait_ge(s3["st_out"].sem, s3["st_out"].at(b, 0))
                    for j in range(NJ):
                        i = mm(bank[1][64:88, j * DK:(j + 1) * DK], A3[u]["sw"][:, j, :], const["fold"][:],
                               start=True, stop=True)
                    i.then_inc(s3["st_turned"].sem, 1)
                    for t in range(TT):
                        i = nc.tensor.transpose(bank[0][0:36, t * P:(t + 1) * P],
                                                of_batch(b)[:, 3 * t:3 * t + 3, :, :].rearrange("p r s h -> p (r s h)"), ident[:])
                    i.then_inc(s3["st_turned"].sem, 1)

                def hidden(u, b, m):
                    if m == 0:
                        pe.wait_ge(s3[f"xT3_in{u}"].sem, s3[f"xT3_in{u}"].at(b // 2, 16))
                        pe.wait_ge(s3["oT_out"].sem, s3["oT_out"].at(b - u, 0))
                    if m >= 2:
                        pe.wait_ge(s3["gelu"].sem, s3["gelu"].at(b, m - 1))
                    elif u:
                        pe.wait_ge(s3["gelu"].sem, s3["gelu"].at(b - 1, m + 3))
                    for k in range(KT):
                        mm(bank[2 + m % 2][:], g1x_w[:, k, m * P:(m + 1) * P], A3[u]["xT"][:, k, :],
                           start=(k == 0), stop=False)
                    if m == 0:
                        pe.wait_ge(s3["st_out"].sem, s3["st_out"].at(b, 2))
                    mm(bank[2 + m % 2][:], g1s_w[0:88, m * P:(m + 1) * P], A3[u]["statT"][0:88, :],
                       start=False, stop=True).then_inc(s3["hdn_mm"].sem, 1)

                def logits(u, b):
                    pe.wait_ge(s3["gelu"].sem, s3["gelu"].at(b, GH // P))
                    if u == 0:
                        pe.wait_ge(s3["res"].sem, s3["res"].at(b, 0))
                    else:
                        pe.wait_ge(s3["lg_pre"].sem, s3["lg_pre"].at(b - 1, 1))
                    for t in range(TT):
                        for k in range(GH // P):
                            i = mm(bank[4][:, t * NG * H:(t + 1) * NG * H], A3[u]["hdnT"][:, k, t * P:(t + 1) * P],
                                   g2_w[:, k, :], start=(k == 0), stop=(k == GH // P - 1))
                    i.then_inc(s3["lg_mm"].sem, 1)

                def twice(u, b):
                    pe.wait_ge(s3["lg_post"].sem, s3["lg_post"].at(b, 5))
                    if u:
                        pe.wait_ge(s3["w_sel"].sem, s3["w_sel"].at(b, 0))
                    wcol = A3[u]["w"].rearrange("p t h g -> p (t h g)")
                    mm(bank[5][:, 0:80], const["twice_even"][:], wcol, start=True, stop=True)
                    mm(bank[5][:, 80:160], const["twice_odd"][:], wcol, start=True, stop=True)\
                        .then_inc(s3["w_twice"].sem, 1)

                def mix(u, b):
                    pe.wait_ge(s3["p_wl"].sem, s3["p_wl"].at(b, 2))
                    pe.wait_ge(s3["p_v"].sem, s3["p_v"].at(b, 1))
                    pe.wait_ge(s3["p_sd"].sem, s3["p_sd"].at(b, 2))
                    if u:
                        pe.wait_ge(s3["st_out"].sem, s3["st_out"].at(b, 2))
                    for t in range(TT):
                        o = mix_bank(u, t // 2)[:, (t % 2) * D:(t % 2 + 1) * D]
                        mm(o, ident[:], A3[u]["pv"][:, t, :], start=True, stop=False)
                        mm(o, ident[:], A3[u]["ps"][:, t, :], start=False, stop=False)
                        mm(o, ident[:], A3[u]["pd"][:, t, :], start=False, stop=False)
                        mm(o, const["fold_even"][:], A3[u]["pwl"][:, t, 0, :], start=False, stop=False)
                        i = mm(o, const["fold_odd"][:], A3[u]["pwl"][:, t, 1, :], start=False, stop=True)
                        if t % 2:
                            i.then_inc(s3["mix_mm"].sem, 1)

                def turn_o(u, b):
                    pe.wait_ge(s3["o_norm"].sem, s3["o_norm"].at(b, 2))
                    if u:
                        pe.wait_ge(s3["oT_out"].sem, s3["oT_out"].at(b, 0))
                    for k in range(KT):
                        for t in range(TT):
                            i = nc.tensor.transpose(bank[2 + k][:, t * P:(t + 1) * P], A3[u]["on"][:, t, k * P:(k + 1) * P],
                                                    ident[:])
                        i.then_inc(s3["o_turned"].sem, 1)

                def project(u, b):
                    pe.wait_ge(s3["oT_out"].sem, s3["oT_out"].at(b, 2))
                    for t in range(TT):
                        for k in range(KT):
                            i = mm(y_bank(u, t // 2)[:, (t % 2) * D:(t % 2 + 1) * D], A3[u]["onT"][:, k, t * P:(t + 1) * P],
                                   ow_w[:, k, :], start=(k == 0), stop=(k == KT - 1))
                        if t % 2:
                            i.then_inc(s3["y_mm"].sem, 1)

                pe.wait_ge(s3["zeros3"].sem, 4)
                for pair in range(B // 2):
                    b0, b1 = pair * 2, pair * 2 + 1
                    statistics(0, b0)
                    for m in range(GH // P):
                        hidden(0, b0, m)
                    logits(0, b0)
                    statistics(1, b1)
                    hidden(1, b1, 0)
                    hidden(1, b1, 1)
                    twice(0, b0)
                    hidden(1, b1, 2)
                    hidden(1, b1, 3)
                    logits(1, b1)
                    mix(0, b0)
                    twice(1, b1)
                    mix(1, b1)
                    turn_o(0, b0)
                    project(0, b0)
                    turn_o(1, b1)
                    project(1, b1)

            @block.scalar
            def _(act):
                a = nc.scalar.activation

                def square(u, b, i):
                    act.wait_ge(s3["sq_used"].sem, s3["sq_used"].two_before(b))
                    a(squares_of(u, i), branch(SEEN[i], b), ACT.Square).then_inc(s3["sq_out"].sem, 1)

                def roots(u, b):
                    act.wait_ge(s3["small"].sem, s3["small"].at(b, 4))
                    a(A3[u]["tw"][:, :, 1, :], A3[u]["tw"][:, :, 1, :], ACT.Sqrt).then_inc(s3["roots"].sem, 1)
                    a(of_batch(b)[:, :, 1, :], of_batch(b)[:, :, 1, :], ACT.Sqrt).then_inc(s3["roots"].sem, 1)

                def statistics_out(u, b):
                    act.wait_ge(s3["st_turned"].sem, s3["st_turned"].at(b, 1))
                    nc.scalar.copy(A3[u]["statT"][64:88, :], bank[1][64:88, :]).then_inc(s3["st_out"].sem, 1)
                    act.wait_ge(s3["st_turned"].sem, s3["st_turned"].at(b, 2))
                    nc.scalar.copy(A3[u]["statT"][0:36, :], bank[0][0:36, :]).then_inc(s3["st_out"].sem, 1)

                def gelu(u, b, m):
                    act.wait_ge(s3["hdn_mm"].sem, s3["hdn_mm"].at(b, m + 1))
                    a(A3[u]["hdnT"][:, m, :], bank[2 + m % 2][:], ACT.Gelu, bias=g1_bias[:, m:m + 1])\
                        .then_inc(s3["gelu"].sem, 1)

                def exp(u, b):
                    act.wait_ge(s3["lg_pre"].sem, s3["lg_pre"].at(b, 4))
                    a(A3[u]["lg"], A3[u]["lg"], ACT.Exp).then_inc(s3["lg_exp"].sem, 1)

                def mix_squares(u, b):
                    for i2 in range(2):
                        act.wait_ge(s3["mix_mm"].sem, s3["mix_mm"].at(b, i2 + 1))
                        a(A3[u]["sq_b"][:, i2 * 2 * D:(i2 + 1) * 2 * D], mix_bank(u, i2)[:], ACT.Square)\
                            .then_inc(s3["mix_sq"].sem, 1)

                def turned_out(u, b):
                    for k in range(KT):
                        act.wait_ge(s3["o_turned"].sem, s3["o_turned"].at(b, k + 1))
                        a(A3[u]["onT"][:, k, :], bank[2 + k][:], ACT.Copy, scale=onorm[:, 0:1]).then_inc(s3["oT_out"].sem, 1)

                def round_(pair, first, more):
                    b0, b1 = pair * 2, pair * 2 + 1
                    statistics_out(0, b0)
                    for m in range(GH // P):
                        if more and m < len(SEEN):
                            square(0, b0 + 2, m)
                        gelu(0, b0, m)
                    if first:
                        roots(1, b1)
                    statistics_out(1, b1)
                    exp(0, b0)
                    for m in range(GH // P):
                        gelu(1, b1, m)
                        if more and m < len(SEEN):
                            square(1, b1 + 2, m)
                    exp(1, b1)
                    mix_squares(0, b0)
                    mix_squares(1, b1)
                    turned_out(0, b0)
                    turned_out(1, b1)
                    if more:
                        roots(0, b0 + 2)
                        roots(1, b1 + 2)

                act.wait_ge(s3["zeros3"].sem, 4)
                square(0, 0, 0)
                square(0, 0, 1)
                square(1, 1, 0)
                roots(0, 0)
                square(1, 1, 1)
                for pair in range(B // 2):
                    round_(pair, pair == 0, pair < B // 2 - 1)

            @block.vector
            def _(dve):
                v = nc.vector

                def reduce_branch(u, b, i):
                    n = SEEN[i]
                    v.tensor_reduce(stat(u, b, n, 0), branch(n, b), AX.X, ALU.add).then_inc(s3["red"].sem, 1)
                    v.tensor_reduce(stat(u, b, n, 2), branch(n, b), AX.X, ALU.max,
                                    apply_absolute_value=True).then_inc(s3["red"].sem, 1)
                    dve.wait_ge(s3["sq_out"].sem, s3["sq_out"].at(b, i + 1))
                    v.tensor_reduce(stat(u, b, n, 1), squares_of(u, i), AX.X, ALU.add).then_inc(s3["sq_used"].sem, 1)

                def small(u, b):
                    dve.wait_ge(s3["red"].sem, s3["red"].at(b, 4))
                    dve.wait_ge(s3["sq_used"].sem, s3["sq_used"].at(b, 2))
                    for s in (A3[u]["tw"], of_batch(b)):
                        v.tensor_scalar(s[:, :, 0, :], s[:, :, 0, :], 1.0 / DK, None, ALU.mult).then_inc(s3["small"].sem, 1)
                        v.tensor_scalar(s[:, :, 1, :], s[:, :, 1, :], 1.0 / DK, 1e-8, ALU.mult, ALU.max)\
                            .then_inc(s3["small"].sem, 1)

                def filters_apart(u, b):
                    dve.wait_ge(s3["roots"].sem, s3["roots"].at(b, 1))
                    dve.wait_ge(s3["small"].sem, s3["small"].at(b, 4))
                    tw = A3[u]["tw"].rearrange("p j s h -> p j (s h)")
                    v.tensor_copy(A3[u]["sw"][0:DK, :, 0:12], tw[0:DK, :, :]).then_inc(s3["sw_out"].sem, 1)
                    v.tensor_copy(A3[u]["sw"][DK:P, :, 12:24], tw[DK:P, :, :]).then_inc(s3["sw_out"].sem, 1)

                flat = lambda x: x.rearrange("p t h g -> p t (h g)")
                groups = lambda x: x.rearrange("p t h g -> p (t h) g")

                def softmax_before(u, b):
                    lg, mx = A3[u]["lg"], A3[u]["mx"].rearrange("p t h -> p (t h)")
                    dve.wait_ge(s3["lg_mm"].sem, s3["lg_mm"].at(b, 1))
                    v.tensor_tensor(flat(lg), bank[4][:, 0:80].rearrange("p (t n) -> p t n", t=TT),
                                    over_tiles(g2_bias[:], TT), ALU.add).then_inc(s3["lg_pre"].sem, 1)
                    dve.wait_ge(s3["lg_pre"].sem, s3["lg_pre"].at(b, 1))
                    v.tensor_tensor(flat(lg), flat(lg), over_tiles(inv_temp5[:, :, :].rearrange("p h g -> p (h g)"), TT),
                                    ALU.mult).then_inc(s3["lg_pre"].sem, 1)
                    dve.wait_ge(s3["lg_pre"].sem, s3["lg_pre"].at(b, 2))
                    v.tensor_reduce(mx, groups(lg), AX.X, ALU.max).then_inc(s3["lg_pre"].sem, 1)
                    dve.wait_ge(s3["lg_pre"].sem, s3["lg_pre"].at(b, 3))
                    v.tensor_tensor(groups(lg), groups(lg), over_last(mx, NG), ALU.subtract).then_inc(s3["lg_pre"].sem, 1)

                def softmax_after(u, b):
                    lg, w, mx = A3[u]["lg"], A3[u]["w"], A3[u]["mx"].rearrange("p t h -> p (t h)")
                    dve.wait_ge(s3["lg_exp"].sem, s3["lg_exp"].at(b, 1))
                    v.tensor_reduce(mx, groups(lg), AX.X, ALU.add).then_inc(s3["lg_post"].sem, 1)
                    dve.wait_ge(s3["lg_post"].sem, s3["lg_post"].at(b, 1))
                    v.reciprocal(mx, mx).then_inc(s3["lg_post"].sem, 1)
                    dve.wait_ge(s3["lg_post"].sem, s3["lg_post"].at(b, 2))
                    v.tensor_tensor(A3[u]["mx"], A3[u]["mx"], over_tiles(keep[:], TT), ALU.mult).then_inc(s3["lg_post"].sem, 1)
                    dve.wait_ge(s3["lg_post"].sem, s3["lg_post"].at(b, 3))
                    v.tensor_tensor(groups(w), groups(lg), over_last(mx, NG), ALU.mult).then_inc(s3["lg_post"].sem, 1)
                    dve.wait_ge(s3["lg_post"].sem, s3["lg_post"].at(b, 4))
                    w4 = w[:, :, :, 0:NG - 1]
                    v.tensor_tensor(w4, w4, over_tiles(over_last(floor[:], NG - 1), TT), ALU.add)\
                        .then_inc(s3["lg_post"].sem, 1)

                def weigh(u, b):
                    dve.wait_ge(s3["lg_post"].sem, s3["lg_post"].at(b, 5))
                    v.tensor_tensor(A3[u]["pv"].rearrange("p t (h c) -> p t h c", h=H), branch(3, b),
                                    over_last(A3[u]["w"][:, :, :, 4], DK), ALU.mult).then_inc(s3["p_v"].sem, 1)
                    dve.wait_ge(s3["w_twice"].sem, s3["w_twice"].at(b, 1))
                    tw2 = bank[5][:, 0:160].rearrange("p (j h g) -> p j h g", h=H, g=NG)
                    ws = A3[u]["wsel"].rearrange("p a t h -> p (a t) h")
                    v.tensor_copy(ws[0:DK], tw2[0:DK, :, :, 2]).then_inc(s3["w_sel"].sem, 1)
                    v.tensor_copy(ws[DK:P], tw2[DK:P, :, :, 1]).then_inc(s3["w_sel"].sem, 1)
                    dve.wait_ge(s3["w_sel"].sem, s3["w_sel"].at(b, 2))
                    for a in range(2):
                        v.tensor_tensor(A3[u]["pwl"][:, :, a, :].rearrange("p t (h c) -> p t h c", h=H),
                                        wl.rearrange("p (t a) (h c) -> p t a h c", a=2, h=H)[:, bass.ds(b * TT, TT), a, :, :],
                                        over_last(A3[u]["wsel"][:, a, :, :], DK), ALU.mult).then_inc(s3["p_wl"].sem, 1)

                def head_sums(u, b):
                    for i2 in range(2):
                        dve.wait_ge(s3["mix_sq"].sem, s3["mix_sq"].at(b, i2 + 1))
                        v.tensor_reduce(A3[u]["ssh"][:, i2 * 8:i2 * 8 + 8],
                                        A3[u]["sq_b"][:, i2 * 2 * D:(i2 + 1) * 2 * D].rearrange("p (g c) -> p g c", c=DK),
                                        AX.X, ALU.add).then_inc(s3["mix_ss"].sem, 1)
                    dve.wait_ge(s3["mix_ss"].sem, s3["mix_ss"].at(b, 2))
                    v.tensor_scalar(A3[u]["ssh"], A3[u]["ssh"], 1.0 / DK, 1e-5, ALU.mult, ALU.add).then_inc(s3["mix_ss"].sem, 1)

                def head_norm(u, b):
                    dve.wait_ge(s3["r_head"].sem, s3["r_head"].at(b, 1))
                    for i2 in range(2):
                        v.tensor_tensor(A3[u]["on"][:, 2 * i2:2 * i2 + 2, :].rearrange("p t (h c) -> p (t h) c", h=H),
                                        mix_bank(u, i2)[:].rearrange("p (g c) -> p g c", c=DK),
                                        over_last(A3[u]["rh"][:, i2 * 8:i2 * 8 + 8], DK), ALU.mult).then_inc(s3["o_norm"].sem, 1)

                def residual(u, b, pair):
                    dve.wait_ge(s3[f"x3_in{u}"].sem, s3[f"x3_in{u}"].at(pair, 16))
                    for i2 in range(2):
                        dve.wait_ge(s3["y_mm"].sem, s3["y_mm"].at(b, i2 + 1))
                        v.tensor_tensor(A3[u]["xr"][:, 2 * i2:2 * i2 + 2, :], A3[u]["x"][:, 2 * i2:2 * i2 + 2, :],
                                        y_bank(u, i2)[:].rearrange("p (t c) -> p t c", t=2), ALU.add).then_inc(s3["res"].sem, 1)
                    norm_statistics(dve, scratch, b, A3[u]["xr"], A3[u], s3, "res")

                def statistics(u, b, first=False):
                    if not first:
                        dve.wait_ge(s3["st_turned"].sem, s3["st_turned"].at(b - 2, 2))
                    for i in range(len(SEEN)):
                        reduce_branch(u, b, i)
                    small(u, b)

                def round_(pair, first, more):
                    b0, b1 = pair * 2, pair * 2 + 1
                    for u, b in ((0, b0), (1, b1)):
                        if more:
                            statistics(u, b + 2)
                        if first and u == 0:
                            filters_apart(1, b1)
                        softmax_before(u, b)
                        softmax_after(u, b)
                        weigh(u, b)
                    head_sums(0, b0)
                    head_norm(0, b0)
                    head_sums(1, b1)
                    head_norm(1, b1)
                    residual(0, b0, pair)
                    residual(1, b1, pair)
                    for u, b in ((0, b0), (1, b1)):
                        norm_apply(dve, b, A3[u]["xr"], A3[u], s3, lambda t: delta[:, b * TT + t, :], "x1_out")
                    if more:
                        filters_apart(0, b0 + 2)
                        filters_apart(1, b1 + 2)

                dve.wait_ge(s3["zeros3"].sem, 4)
                statistics(0, 0, first=True)
                reduce_branch(1, 1, 0)
                filters_apart(0, 0)
                reduce_branch(1, 1, 1)
                small(1, 1)
                for pair in range(B // 2):
                    round_(pair, pair == 0, pair < B // 2 - 1)

            @block.gpsimd
            def _(pool):
                g = nc.gpsimd
                heads = lambda x: x.rearrange("p t (h c) -> p t h c", h=H)
                for u in range(2):
                    g.memset(A3[u]["sw"], 0.0).then_inc(s3["zeros3"].sem, 1)
                    g.memset(A3[u]["statT"], 0.0).then_inc(s3["zeros3"].sem, 1)
                with pool.Fori(0, B // 2) as pair:
                    for u in range(2):
                        b = pair * 2 + u
                        pool.wait_ge(s3["lg_post"].sem, s3["lg_post"].at(b, 5))
                        g.tensor_tensor(heads(A3[u]["ps"]), branch(1, b), over_last(A3[u]["w"][:, :, :, 0], DK), ALU.mult)\
                            .then_inc(s3["p_sd"].sem, 1)
                        g.tensor_tensor(heads(A3[u]["pd"]), branch(2, b), over_last(A3[u]["w"][:, :, :, 3], DK), ALU.mult)\
                            .then_inc(s3["p_sd"].sem, 1)
                    for u in range(2):
                        b = pair * 2 + u
                        pool.wait_ge(s3["mix_ss"].sem, s3["mix_ss"].at(b, 3))
                        g.tensor_tensor(A3[u]["rh"], A3[u]["ssh"], half_exp[:, 0, :], ALU.pow).then_inc(s3["r_head"].sem, 1)
                    for u in range(2):
                        b = pair * 2 + u
                        pool.wait_ge(s3["ln_st"].sem, s3["ln_st"].at(b, 9))
                        g.tensor_tensor(A3[u]["rs"], A3[u]["ve"], half_exp[:, 0, 0:TT], ALU.pow).then_inc(s3["ln_rs"].sem, 1)

        A4 = []
        for u in range(2):
            a4 = carve(arena, {
                "xeo": (2, 2, D), "ctx": (TT, D), "ceo": (2, 2, D), "XFT": (KT, 512), "CFT": (KT, 512), "QF": (4, D),
                "KVF": (4, 2 * D), "PR": (4, 2, D), "RD": (4, 2, XH), "CC": (2, 2, XH), "t1": (2, XH), "t2": (2, XH),
                "t3": (2, XH), "t4": (2, XH), "Es": (HALF,), "co": (L + 2,), "m8": (8,), "mr": (8,), "nb": (1,),
                "rep": (L + 2,), "ex": (L,), "e6": (TOPK,), "s6": (1,), "r6": (1,), "aeo": (L,), "AT": (4, XH),
                "AF": (3, 2, XH), "Eb": (KT, HALF), "x1b": (TT, D),
                "ln": (TT, 6), "mv": (TT, 2), "ve": (TT,), "rs": (TT,)}, at=u * 14700)
            a4["OF"] = a4["XFT"].rearrange("p k (a c) -> p (k a) c", a=2)
            a4["oT"] = a4["CFT"]
            a4["xr"] = a4["xeo"].rearrange("p a k c -> p (a k) c")
            A4.append(a4)
        free_4 = ("ceo", "cf_mm", "ot_out", "res4", "x2_out")
        s4 = signals(4, {
            "ctx_in0": 16, "ctx_in1": 16, "xeo": 2, "ceo": 2, "xf_mm": 2, "cf_mm": 2, "xf_out": 2, "cf_out": 2,
            "qf_mm": 2, "kvf_mm": 4, "qf_out": 2, "kvf_out": 4, "prod_v": 2, "prod_g": 2, "corr_red": 1, "cc": 6,
            "corr_mm": 1, "es_out": 1, "co_out": 2, "top": 3, "rep_out": 1, "exps": 2, "a_steps": 5,
            "a_turned4": 1, "at4_out": 1, "af_mm": 1, "af": 5, "of_v": 2, "of_g": 2, "of": 2, "ot_mm": 2,
            "eb_out": 2, "ot_out": 4, "y4_mm": 2, "x1b_out": 1, "res4": 2, "ln_st": 9, "ln_rs": 1, "x2_out": 4,
            "sentinels": 0}, free_4, pair=True)
        cf_bank, xf_bank = (lambda u, i: bank[2 + i]), (lambda u, i: bank[(0, 4)[u] + i])
        qf_bank, kvf_bank = (lambda u, i: bank[(4, 6)[u] + i]), (lambda u, f: bank[((6, 7, 0, 1), (0, 1, 2, 3))[u][f]])
        corr_bank, turn4_bank = (lambda u: bank[(4, 6)[u]]), (lambda u: bank[(5, 7)[u]])
        ot_bank, y4_bank = (lambda u, i: bank[(0, 4)[u] + i]), (lambda u, i: bank[(2, 6)[u] + i])

        with nc.Block() as block:
            @block.sync
            def _(sp):
                for n in free_4:
                    sp.sem_inc(s4[n].sem, s4[n].base)
                with sp.Fori(0, B // 2) as pair:
                    for u in range(2):
                        b = pair * 2 + u
                        sp.wait_ge(s4["ceo"].sem, s4["ceo"].two_before(b))
                        sp.dma_start(A4[u]["ctx"], dr["ctx"][b].rearrange("(t p) d -> p t d", p=P))\
                            .then_inc(s4[f"ctx_in{u}"].sem, 16)

            @block.tensor
            def _(pe):
                mm = nc.tensor.matmul
                def forward(u, b, src, first, done):
                    for d in range(KT):
                        for par in range(2):
                            for k in range(2):
                                i = mm(first(u, d)[:, par * 256:(par + 1) * 256], src[:, par, k, d * P:(d + 1) * P],
                                       dft[:, k, par * 256:(par + 1) * 256], start=(k == 0), stop=(k == 1))
                        i.then_inc(s4[done].sem, 1)

                def forward_ctx(u, b):
                    pe.wait_ge(s4["ceo"].sem, s4["ceo"].at(b, 2))
                    if u == 0:
                        pe.wait_ge(s4["res4"].sem, s4["res4"].two_before(b))
                    else:
                        pe.wait_ge(s4["cf_out"].sem, s4["cf_out"].at(b, 0))
                    forward(u, b, A4[u]["ceo"], cf_bank, "cf_mm")

                def forward_x(u, b):
                    pe.wait_ge(s4["xeo"].sem, s4["xeo"].at(b, 2))
                    if u == 0:
                        pe.wait_ge(s4["ot_out"].sem, s4["ot_out"].two_before(b))
                    else:
                        pe.wait_ge(s4["qf_out"].sem, s4["qf_out"].at(b, 0))
                    forward(u, b, A4[u]["xeo"], xf_bank, "xf_mm")

                def project_q(u, b):
                    pe.wait_ge(s4["xf_out"].sem, s4["xf_out"].at(b, 2))
                    if u == 0:
                        pe.wait_ge(s4["ot_out"].sem, s4["ot_out"].at(b, 0))
                    else:
                        pe.wait_ge(s4["kvf_out"].sem, s4["kvf_out"].at(b - 1, 2))
                    for f in range(4):
                        o = qf_bank(u, f // 2)[:, (f % 2) * D:(f % 2 + 1) * D]
                        for k in range(KT):
                            i = mm(o, A4[u]["XFT"][:, k, f * P:(f + 1) * P], xq_w[:, k, :], start=(k == 0),
                                   stop=(k == KT - 1 and f > 0))
                        if f == 0:
                            i = mm(o, const["dc_row"][0:1, :], xq_b[:], start=False, stop=True)
                        if f % 2:
                            i.then_inc(s4["qf_mm"].sem, 1)

                def project_kv(u, b):
                    pe.wait_ge(s4["cf_out"].sem, s4["cf_out"].at(b, 2))
                    if u == 0:
                        pe.wait_ge(s4["res4"].sem, s4["res4"].at(b, 0))
                    else:
                        pe.wait_ge(s4["kvf_out"].sem, s4["kvf_out"].at(b, 0))
                    for f in range(4):
                        o = kvf_bank(u, f)[:]
                        for k in range(KT):
                            i = mm(o, A4[u]["CFT"][:, k, f * P:(f + 1) * P], xkv_w[:, k, :], start=(k == 0),
                                   stop=(k == KT - 1 and f > 0))
                        if f == 0:
                            i = mm(o, const["dc_row"][0:1, :], xkv_b[:], start=False, stop=True)
                        i.then_inc(s4["kvf_mm"].sem, 1)

                def correlation(u, b):
                    pe.wait_ge(s4["cc"].sem, s4["cc"].at(b, 6))
                    if u == 0:
                        pe.wait_ge(s4["xf_out"].sem, s4["xf_out"].at(b + 1, 2))
                    else:
                        pe.wait_ge(s4["qf_out"].sem, s4["qf_out"].at(b, 2))
                    for par in range(2):
                        for ri in range(2):
                            i = mm(corr_bank(u)[0:XH, par * HALF:(par + 1) * HALF], A4[u]["CC"][:, ri, par, :],
                                   idft[:, 2 * par + ri, :], start=(ri == 0), stop=(ri == 1))
                    i.then_inc(s4["corr_mm"].sem, 1)

                def delays(u, b):
                    pe.wait_ge(s4["a_steps"].sem, s4["a_steps"].at(b, 5))
                    for k in range(4):
                        i = mm(turn4_bank(u)[:, k * XH:(k + 1) * XH], A4[u]["aeo"][0:XH, k * P:(k + 1) * P],
                               ident[0:XH, 0:XH], start=True, stop=True)
                    i.then_inc(s4["a_turned4"].sem, 1)
                    pe.wait_ge(s4["at4_out"].sem, s4["at4_out"].at(b, 1))
                    for f in range(4):
                        for k in range(2):
                            i = mm(corr_bank(u)[:, f * XH:(f + 1) * XH], dft[:, k, f * P:(f + 1) * P],
                                   A4[u]["AT"][:, 2 * (f // 2) + k, :], start=(k == 0), stop=(k == 1))
                    i.then_inc(s4["af_mm"].sem, 1)

                def inverse(u, b):
                    pe.wait_ge(s4["of"].sem, s4["of"].at(b, 2))
                    if u == 0:
                        pe.wait_ge(s4["kvf_out"].sem, s4["kvf_out"].at(b + 1, 2))
                    for m in range(KT):
                        for par in range(2):
                            for ri in range(2):
                                i = mm(ot_bank(u, m)[:, par * HALF:(par + 1) * HALF],
                                       A4[u]["OF"][:, 2 * par + ri, m * P:(m + 1) * P],
                                       idft[:, 2 * par + ri, :], start=(ri == 0), stop=(ri == 1))
                        i.then_inc(s4["ot_mm"].sem, 1)

                def project_o(u, b):
                    pe.wait_ge(s4["ot_out"].sem, s4["ot_out"].at(b, 4))
                    if u == 0:
                        pe.wait_ge(s4["kvf_out"].sem, s4["kvf_out"].at(b + 1, 4))
                    for t in range(TT):
                        for k in range(KT):
                            i = mm(y4_bank(u, t // 2)[:, (t % 2) * D:(t % 2 + 1) * D], A4[u]["oT"][:, k, t * P:(t + 1) * P],
                                   xo_w[:, k, :], start=(k == 0), stop=(k == KT - 1))
                        if t % 2:
                            i.then_inc(s4["y4_mm"].sem, 1)

                pe.wait_ge(s4["sentinels"].sem, 4)
                pe.wait_ge(late_loaded.sem, 16 * 5)
                def round_(pair, more):
                    b0, b1 = pair * 2, pair * 2 + 1
                    forward_x(0, b0)
                    project_q(0, b0)
                    project_kv(0, b0)
                    forward_ctx(1, b1)
                    forward_x(1, b1)
                    correlation(0, b0)
                    project_q(1, b1)
                    project_kv(1, b1)
                    delays(0, b0)
                    inverse(0, b0)
                    correlation(1, b1)
                    project_o(0, b0)
                    delays(1, b1)
                    if more:
                        forward_ctx(0, b0 + 2)
                    inverse(1, b1)
                    project_o(1, b1)

                forward_ctx(0, 0)
                with pe.Fori(0, B // 2 - 1) as pair:
                    round_(pair, True)
                round_(B // 2 - 1, False)

            @block.scalar
            def _(act):
                a = nc.scalar.activation
                def ctx_out(u, b):
                    for d in range(KT):
                        act.wait_ge(s4["cf_mm"].sem, s4["cf_mm"].at(b, d + 1))
                        nc.scalar.copy(A4[u]["CFT"][:, d, :], cf_bank(u, d)[:]).then_inc(s4["cf_out"].sem, 1)

                def x_out(u, b):
                    for d in range(KT):
                        act.wait_ge(s4["xf_mm"].sem, s4["xf_mm"].at(b, d + 1))
                        nc.scalar.copy(A4[u]["XFT"][:, d, :], xf_bank(u, d)[:]).then_inc(s4["xf_out"].sem, 1)

                def q_out(u, b):
                    for i2 in range(2):
                        act.wait_ge(s4["qf_mm"].sem, s4["qf_mm"].at(b, i2 + 1))
                        nc.scalar.copy(A4[u]["QF"][:, 2 * i2:2 * i2 + 2, :], qf_bank(u, i2)[:].rearrange("p (t c) -> p t c", t=2))\
                            .then_inc(s4["qf_out"].sem, 1)

                def kv_out(u, b):
                    for f in range(4):
                        act.wait_ge(s4["kvf_mm"].sem, s4["kvf_mm"].at(b, f + 1))
                        nc.scalar.copy(A4[u]["KVF"][:, f, :], kvf_bank(u, f)[:]).then_inc(s4["kvf_out"].sem, 1)

                def evens_out(u, b):
                    act.wait_ge(s4["corr_mm"].sem, s4["corr_mm"].at(b, 1))
                    nc.scalar.copy(A4[u]["Es"][0:XH, :], corr_bank(u)[0:XH, 0:HALF]).then_inc(s4["es_out"].sem, 1)

                def exps(u, b):
                    act.wait_ge(s4["top"].sem, s4["top"].at(b, 3))
                    a(A4[u]["ex"][0:XH, :], A4[u]["co"][0:XH, 0:L], ACT.Exp, bias=A4[u]["nb"][0:XH, :], scale=1.0 / XD)\
                        .then_inc(s4["exps"].sem, 1)
                    a(A4[u]["e6"][0:XH, :], A4[u]["m8"][0:XH, 0:TOPK], ACT.Exp, bias=A4[u]["nb"][0:XH, :], scale=1.0 / XD,
                      accum_out=A4[u]["s6"][0:XH, :]).then_inc(s4["exps"].sem, 1)

                def output_out(u, b):
                    for m in range(KT):
                        act.wait_ge(s4["ot_mm"].sem, s4["ot_mm"].at(b, m + 1))
                        nc.scalar.copy(A4[u]["Eb"][:, m, :], ot_bank(u, m)[:, 0:HALF]).then_inc(s4["eb_out"].sem, 1)

                def round_(pair, more):
                    b0, b1 = pair * 2, pair * 2 + 1
                    x_out(0, b0)
                    q_out(0, b0)
                    kv_out(0, b0)
                    ctx_out(1, b1)
                    x_out(1, b1)
                    evens_out(0, b0)
                    exps(0, b0)
                    q_out(1, b1)
                    kv_out(1, b1)
                    output_out(0, b0)
                    evens_out(1, b1)
                    exps(1, b1)
                    if more:
                        ctx_out(0, b0 + 2)
                    output_out(1, b1)

                act.wait_ge(s4["sentinels"].sem, 4)
                ctx_out(0, 0)
                with act.Fori(0, B // 2 - 1) as pair:
                    round_(pair, True)
                round_(B // 2 - 1, False)
                act.wait_ge(ffn_in.sem, 16 * 3)
                for w, src in ((wg, ffn[0]), (wu, ffn[1])):
                    nc.scalar.copy(w.rearrange("p k n -> p (k n)"), src.bitcast(I32)).then_inc(ffn_ready.sem, 1)
                a(ffn[2], ffn[2].bitcast(I32), ACT.Copy, scale=1.0 / 127.0).then_inc(ffn_ready.sem, 1)

            ab = lambda u, i: A4[u]["PR"][:, i, :, :]
            hd = lambda x: x.rearrange("p e (h c) -> p e h c", c=XD)

            def spectra(u, i):
                return {"qr": A4[u]["QF"][:, 0::2, :], "qi": A4[u]["QF"][:, 1::2, :],
                        "kr": A4[u]["KVF"][:, 0::2, 0:D], "ki": A4[u]["KVF"][:, 1::2, 0:D],
                        "vr": A4[u]["KVF"][:, 0::2, D:2 * D], "vi": A4[u]["KVF"][:, 1::2, D:2 * D]}[i]

            @block.vector
            def _(dve):
                v = nc.vector
                def sums(u, b):
                    x1 = delta[:, bass.ds(b * TT, TT), :]
                    dve.wait_ge(s4["x2_out"].sem, s4["x2_out"].two_before(b))
                    v.tensor_tensor(A4[u]["xeo"][:, 0, :, :], x1[:, 0:2, :], x1[:, 2:4, :], ALU.add).then_inc(s4["xeo"].sem, 1)
                    v.tensor_tensor(A4[u]["xeo"][:, 1, :, :], x1[:, 0:2, :], x1[:, 2:4, :], ALU.subtract).then_inc(s4["xeo"].sem, 1)

                def products(u, b):
                    dve.wait_ge(s4["qf_out"].sem, s4["qf_out"].at(b, 2))
                    dve.wait_ge(s4["kvf_out"].sem, s4["kvf_out"].at(b, 4))
                    v.tensor_tensor(ab(u, 0), spectra(u, "qr"), spectra(u, "kr"), ALU.mult).then_inc(s4["prod_v"].sem, 1)
                    v.tensor_tensor(ab(u, 1), spectra(u, "qi"), spectra(u, "ki"), ALU.mult).then_inc(s4["prod_v"].sem, 1)
                    dve.wait_ge(s4["prod_v"].sem, s4["prod_v"].at(b, 2))
                    dve.wait_ge(s4["prod_g"].sem, s4["prod_g"].at(b, 2))
                    v.tensor_reduce(A4[u]["RD"].rearrange("p a e h -> p (a e h)"),
                                    A4[u]["PR"].rearrange("p a e (h c) -> p (a e h) c", c=XD), AX.X, ALU.add)\
                        .then_inc(s4["corr_red"].sem, 1)
                    dve.wait_ge(s4["corr_red"].sem, s4["corr_red"].at(b, 1))
                    rd = lambda i: A4[u]["RD"][:, i, :, :]
                    steps = [(A4[u]["t1"], rd(1), not_dc, ALU.mult), (A4[u]["t2"], rd(2), rd(3), ALU.subtract),
                             (A4[u]["t4"], rd(1), is_dc, ALU.mult), (A4[u]["CC"][:, 0, :, :], rd(0), A4[u]["t1"], ALU.add),
                             (A4[u]["t3"], A4[u]["t2"], not_dc, ALU.mult), (A4[u]["CC"][:, 1, :, :], A4[u]["t3"], A4[u]["t4"], ALU.add)]
                    for n, (o, x, y, op) in enumerate(steps):
                        if n >= 3:
                            dve.wait_ge(s4["cc"].sem, s4["cc"].at(b, n if n == 5 else n - 1))
                        v.tensor_tensor(o, x, y, op).then_inc(s4["cc"].sem, 1)

                def best(u, b):
                    dve.wait_ge(s4["corr_mm"].sem, s4["corr_mm"].at(b, 1))
                    dve.wait_ge(s4["es_out"].sem, s4["es_out"].at(b, 1))
                    es, od = A4[u]["Es"][0:XH, :], corr_bank(u)[0:XH, HALF:L]
                    v.tensor_tensor(A4[u]["co"][0:XH, 0:HALF], es, od, ALU.add).then_inc(s4["co_out"].sem, 1)
                    v.tensor_tensor(A4[u]["co"][0:XH, HALF:L], es, od, ALU.subtract).then_inc(s4["co_out"].sem, 1)
                    dve.wait_ge(s4["co_out"].sem, s4["co_out"].at(b, 2))
                    v.memset(scratch, 0.0)
                    v.max(A4[u]["m8"][0:XH, :], A4[u]["co"][0:XH, 0:L]).then_inc(s4["top"].sem, 1)
                    dve.wait_ge(s4["top"].sem, s4["top"].at(b, 1))
                    v.tensor_copy(A4[u]["mr"][0:XH, 0:TOPK], A4[u]["m8"][0:XH, 0:TOPK]).then_inc(s4["top"].sem, 1)
                    dve.wait_ge(s4["top"].sem, s4["top"].at(b, 2))
                    v.tensor_scalar(A4[u]["nb"][0:XH, :], A4[u]["m8"][0:XH, 0:1], -1.0 / XD, None, ALU.mult)\
                        .then_inc(s4["top"].sem, 1)
                    v.match_replace(A4[u]["rep"][0:XH, :], A4[u]["mr"][0:XH, :], A4[u]["co"][0:XH, :], BIG)\
                        .then_inc(s4["rep_out"].sem, 1)
                    dve.wait_ge(s4["rep_out"].sem, s4["rep_out"].at(b, 1))
                    dve.wait_ge(s4["exps"].sem, s4["exps"].at(b, 2))
                    v.reciprocal(A4[u]["r6"][0:XH, :], A4[u]["s6"][0:XH, :]).then_inc(s4["a_steps"].sem, 1)
                    v.scalar_tensor_tensor(out=A4[u]["rep"][0:XH, 0:L], in0=A4[u]["rep"][0:XH, 0:L], scalar=BIG,
                                           in1=A4[u]["ex"][0:XH, :], op0=ALU.is_ge, op1=ALU.mult).then_inc(s4["a_steps"].sem, 1)
                    dve.wait_ge(s4["a_steps"].sem, s4["a_steps"].at(b, 2))
                    v.tensor_scalar(A4[u]["rep"][0:XH, 0:L], A4[u]["rep"][0:XH, 0:L], A4[u]["r6"][0:XH, :], None, ALU.mult)\
                        .then_inc(s4["a_steps"].sem, 1)
                    dve.wait_ge(s4["a_steps"].sem, s4["a_steps"].at(b, 3))
                    lo, hi = A4[u]["rep"][0:XH, 0:HALF], A4[u]["rep"][0:XH, HALF:L]
                    v.tensor_tensor(A4[u]["aeo"][0:XH, 0:HALF], lo, hi, ALU.add).then_inc(s4["a_steps"].sem, 1)
                    v.tensor_tensor(A4[u]["aeo"][0:XH, HALF:L], lo, hi, ALU.subtract).then_inc(s4["a_steps"].sem, 1)

                def delays_out(u, b):
                    dve.wait_ge(s4["a_turned4"].sem, s4["a_turned4"].at(b, 1))
                    v.tensor_copy(A4[u]["AT"].rearrange("p k h -> p (k h)"), turn4_bank(u)[:, 0:4 * XH]).then_inc(s4["at4_out"].sem, 1)
                    dve.wait_ge(s4["af_mm"].sem, s4["af_mm"].at(b, 1))
                    af = corr_bank(u)[:, 0:4 * XH].rearrange("p (a ri h) -> p a ri h", a=2, ri=2)
                    a1, a2, a3 = (A4[u]["AF"][:, n, :, :] for n in range(3))
                    v.tensor_copy(a1, af[:, :, 0, :]).then_inc(s4["af"].sem, 1)
                    v.tensor_tensor(a2, af[:, :, 1, :], not_dc, ALU.mult).then_inc(s4["af"].sem, 1)
                    v.tensor_tensor(A4[u]["t1"], af[:, :, 1, :], is_dc, ALU.mult).then_inc(s4["af"].sem, 1)
                    v.tensor_tensor(A4[u]["t2"], af[:, :, 0, :], not_dc, ALU.mult).then_inc(s4["af"].sem, 1)
                    dve.wait_ge(s4["af"].sem, s4["af"].at(b, 4))
                    v.tensor_tensor(a3, A4[u]["t1"], A4[u]["t2"], ALU.add).then_inc(s4["af"].sem, 1)
                    v.tensor_tensor(hd(ab(u, 0)), hd(spectra(u, "vr")), over_last(a1, XD), ALU.mult).then_inc(s4["of_v"].sem, 1)
                    dve.wait_ge(s4["af"].sem, s4["af"].at(b, 5))
                    v.tensor_tensor(hd(ab(u, 2)), hd(spectra(u, "vi")), over_last(a3, XD), ALU.mult).then_inc(s4["of_v"].sem, 1)
                    dve.wait_ge(s4["of_v"].sem, s4["of_v"].at(b, 2))
                    dve.wait_ge(s4["of_g"].sem, s4["of_g"].at(b, 2))
                    v.tensor_tensor(A4[u]["OF"][:, 0::2, :], ab(u, 0), ab(u, 1), ALU.subtract).then_inc(s4["of"].sem, 1)
                    v.tensor_tensor(A4[u]["OF"][:, 1::2, :], ab(u, 2), ab(u, 3), ALU.add).then_inc(s4["of"].sem, 1)

                def output_sum(u, b):
                    for m in range(KT):
                        dve.wait_ge(s4["eb_out"].sem, s4["eb_out"].at(b, m + 1))
                        eb, od = A4[u]["Eb"][:, m, :], ot_bank(u, m)[:, HALF:L]
                        v.tensor_tensor(A4[u]["oT"][:, m, 0:HALF], eb, od, ALU.add).then_inc(s4["ot_out"].sem, 1)
                        v.tensor_tensor(A4[u]["oT"][:, m, HALF:L], eb, od, ALU.subtract).then_inc(s4["ot_out"].sem, 1)

                def residual(u, b):
                    dve.wait_ge(s4["x1b_out"].sem, s4["x1b_out"].at(b, 1))
                    for i2 in range(2):
                        dve.wait_ge(s4["y4_mm"].sem, s4["y4_mm"].at(b, i2 + 1))
                        v.tensor_tensor(A4[u]["xr"][:, 2 * i2:2 * i2 + 2, :], A4[u]["x1b"][:, 2 * i2:2 * i2 + 2, :],
                                        y4_bank(u, i2)[:].rearrange("p (t c) -> p t c", t=2), ALU.add)\
                            .then_inc(s4["res4"].sem, 1)
                    norm_statistics(dve, scratch, b, A4[u]["xr"], A4[u], s4, "res4")

                def round_(pair, more):
                    b0, b1 = pair * 2, pair * 2 + 1
                    products(0, b0)
                    best(0, b0)
                    delays_out(0, b0)
                    products(1, b1)
                    output_sum(0, b0)
                    best(1, b1)
                    residual(0, b0)
                    delays_out(1, b1)
                    output_sum(1, b1)
                    residual(1, b1)
                    for u, b in ((0, b0), (1, b1)):
                        norm_apply(dve, b, A4[u]["xr"], A4[u], s4, lambda t: short[:, b * TT + t, :], "x2_out")
                        if more:
                            sums(u, b + 2)

                dve.wait_ge(s4["sentinels"].sem, 4)
                sums(0, 0)
                sums(1, 1)
                with dve.Fori(0, B // 2 - 1) as pair:
                    round_(pair, True)
                round_(B // 2 - 1, False)

            @block.gpsimd
            def _(pool):
                g = nc.gpsimd
                for u in range(2):
                    g.memset(A4[u]["co"][:, L:L + 2], -BIG).then_inc(s4["sentinels"].sem, 1)
                    g.memset(A4[u]["mr"], -BIG).then_inc(s4["sentinels"].sem, 1)

                def products(u, b):
                    pool.wait_ge(s4["qf_out"].sem, s4["qf_out"].at(b, 2))
                    pool.wait_ge(s4["kvf_out"].sem, s4["kvf_out"].at(b, 4))
                    g.tensor_tensor(ab(u, 2), spectra(u, "qi"), spectra(u, "kr"), ALU.mult).then_inc(s4["prod_g"].sem, 1)
                    g.tensor_tensor(ab(u, 3), spectra(u, "qr"), spectra(u, "ki"), ALU.mult).then_inc(s4["prod_g"].sem, 1)

                def output_products(u, b):
                    pool.wait_ge(s4["af"].sem, s4["af"].at(b, 5))
                    a2 = A4[u]["AF"][:, 1, :, :]
                    g.tensor_tensor(hd(ab(u, 1)), hd(spectra(u, "vi")), over_last(a2, XD), ALU.mult).then_inc(s4["of_g"].sem, 1)
                    g.tensor_tensor(hd(ab(u, 3)), hd(spectra(u, "vr")), over_last(a2, XD), ALU.mult).then_inc(s4["of_g"].sem, 1)

                def sums(u, b, pair):
                    c, ceo = A4[u]["ctx"], A4[u]["ceo"]
                    pool.wait_ge(s4[f"ctx_in{u}"].sem, s4[f"ctx_in{u}"].at(pair, 16))
                    pool.wait_ge(s4["cf_mm"].sem, s4["cf_mm"].two_before(b))
                    g.tensor_tensor(ceo[:, 0, :, :], c[:, 0:2, :], c[:, 2:4, :], ALU.add).then_inc(s4["ceo"].sem, 1)
                    g.tensor_tensor(ceo[:, 1, :, :], c[:, 0:2, :], c[:, 2:4, :], ALU.subtract).then_inc(s4["ceo"].sem, 1)

                def round_(pair, more):
                    b0, b1 = pair * 2, pair * 2 + 1
                    for u, b in ((0, b0), (1, b1)):
                        pool.wait_ge(s4["res4"].sem, s4["res4"].two_before(b))
                        g.tensor_tensor(A4[u]["x1b"], delta[:, bass.ds(b * TT, TT), :], over_tiles(xo_b[:], TT), ALU.add)\
                            .then_inc(s4["x1b_out"].sem, 1)
                    products(0, b0)
                    output_products(0, b0)
                    products(1, b1)
                    if more:
                        sums(0, b0 + 2, pair + 1)
                    output_products(1, b1)
                    if more:
                        sums(1, b1 + 2, pair + 1)
                    for u, b in ((0, b0), (1, b1)):
                        pool.wait_ge(s4["ln_st"].sem, s4["ln_st"].at(b, 9))
                        g.tensor_tensor(A4[u]["rs"], A4[u]["ve"], half_exp[:, 0, 0:TT], ALU.pow).then_inc(s4["ln_rs"].sem, 1)

                sums(0, 0, 0)
                sums(1, 1, 0)
                with pool.Fori(0, B // 2 - 1) as pair:
                    round_(pair, True)
                round_(B // 2 - 1, False)

        A5 = [carve(arena, {"x2": (TT, D), "x2T": (KT, L), "x_hi": (KT, L // 2), "x_mid": (KT, L // 2),
                            "x_lo": (KT, L // 2), "sg": (2, L), "hT": (MF, L), "xr": (TT, D), "y": (TT, D),
                            "ln": (TT, 6), "mv": (TT, 2), "ve": (TT,), "rs": (TT,)}, at=u * 10000) for u in range(2)]
        parts = [{n: a5[n].rearrange("p k c -> p (k c)").bitcast(BF16).rearrange("p (k c) -> p k c", k=KT)
                  for n in ("x_hi", "x_mid", "x_lo")} for a5 in A5]
        free_5 = ("res5", "h_out", "stored0", "stored1")
        s5 = signals(5, {"x2_copy": 1, "x_turned5": 2, "hi_out": 2, "rest_out": 2, "mid_out": 2, "lo_out": 2, "gate_mm": 6, "up_mm": 6, "gate_silu": 6,
                         "h_out": 6, "y5_mm": 2, "res5": 2, "ln_st": 9, "ln_rs": 1, "y_out": 4, "stored0": 16,
                         "stored1": 16}, free_5, pair=True)
        with nc.Block() as block:
            @block.sync
            def _(sp):
                for n in free_5:
                    sp.sem_inc(s5[n].sem, s5[n].base)
                with sp.Fori(0, B // 2) as pair:
                    for u in range(2):
                        b = pair * 2 + u
                        sp.wait_ge(s5["y_out"].sem, s5["y_out"].at(b, 4))
                        sp.dma_start(out[b].rearrange("(t p) d -> p t d", p=P), A5[u]["y"]).then_inc(s5[f"stored{u}"].sem, 16)
                for u in range(2):
                    sp.wait_ge(s5[f"stored{u}"].sem, s5[f"stored{u}"].at(B // 2, 0))

            @block.tensor
            def _(pe):
                mm = nc.tensor.matmul

                def turn(u, b):
                    pe.wait_ge(s5["x2_copy"].sem, s5["x2_copy"].at(b, 1))
                    if u:
                        pe.wait_ge(s5["rest_out"].sem, s5["rest_out"].at(b, 0))
                    for k in range(KT):
                        for t in range(TT):
                            i = nc.tensor.transpose(bank[k][:, t * P:(t + 1) * P], A5[u]["x2"][:, t, k * P:(k + 1) * P], ident[:])
                        i.then_inc(s5["x_turned5"].sem, 1)

                def gates(u, b):
                    pe.wait_ge(s5["lo_out"].sem, s5["lo_out"].at(b, 2))
                    for m in range(MF):
                        for w, first, done in ((wg, 2, "gate_mm"), (wu, 4, "up_mm")):
                            pe.wait_ge(s5["h_out"].sem, s5["h_out"].at(b, m - 1 if m >= 2 else 0))
                            for n, part in enumerate(("x_lo", "x_mid", "x_hi")):
                                for k in range(KT):
                                    i = mm(bank[first + m % 2][:], w[:, k, m * P:(m + 1) * P], parts[u][part][:, k, :],
                                           start=(n == 0 and k == 0), stop=(n == 2 and k == KT - 1))
                            i.then_inc(s5[done].sem, 1)

                def down(u, b):
                    pe.wait_ge(s5["h_out"].sem, s5["h_out"].at(b, MF))
                    pe.wait_ge(s5["res5"].sem, s5["res5"].at(b, 0))
                    for t in range(TT):
                        for m in range(MF):
                            i = mm(bank[6 + t // 2][:, (t % 2) * D:(t % 2 + 1) * D], A5[u]["hT"][:, m, t * P:(t + 1) * P],
                                   wd[:, m, :], start=(m == 0), stop=(m == MF - 1))
                        if t % 2:
                            i.then_inc(s5["y5_mm"].sem, 1)

                pe.wait_ge(ffn_ready.sem, 3)
                with pe.Fori(0, B // 2) as pair:
                    b0, b1 = pair * 2, pair * 2 + 1
                    turn(0, b0)
                    gates(0, b0)
                    turn(1, b1)
                    down(0, b0)
                    gates(1, b1)
                    down(1, b1)

            @block.scalar
            def _(act):
                with act.Fori(0, B // 2) as pair:
                    def x_out(u, b):
                        for k in range(KT):
                            act.wait_ge(s5["x_turned5"].sem, s5["x_turned5"].at(b, k + 1))
                            nc.scalar.copy(parts[u]["x_hi"][:, k, :], bank[k][:]).then_inc(s5["hi_out"].sem, 1)
                        for k in range(KT):
                            act.wait_ge(s5["rest_out"].sem, s5["rest_out"].at(b, k + 1))
                            nc.scalar.copy(parts[u]["x_mid"][:, k, :], A5[u]["x2T"][:, k, :]).then_inc(s5["mid_out"].sem, 1)

                    def silus(u, b):
                        for m in range(MF):
                            act.wait_ge(s5["gate_mm"].sem, s5["gate_mm"].at(b, m + 1))
                            act.wait_ge(s5["h_out"].sem, s5["h_out"].at(b, m - 1 if m >= 2 else 0))
                            nc.scalar.activation(A5[u]["sg"][:, m % 2, :], bank[2 + m % 2][:], ACT.Silu, scale=1.0 / 127.0)\
                                .then_inc(s5["gate_silu"].sem, 1)

                    b0, b1 = pair * 2, pair * 2 + 1
                    x_out(0, b0)
                    silus(0, b0)
                    x_out(1, b1)
                    silus(1, b1)

            @block.vector
            def _(dve):
                v = nc.vector

                def split(u, b):
                    for k in range(KT):
                        dve.wait_ge(s5["hi_out"].sem, s5["hi_out"].at(b, k + 1))
                        v.tensor_tensor(A5[u]["x2T"][:, k, :], bank[k][:], parts[u]["x_hi"][:, k, :], ALU.subtract)\
                            .then_inc(s5["rest_out"].sem, 1)
                    for k in range(KT):
                        dve.wait_ge(s5["mid_out"].sem, s5["mid_out"].at(b, k + 1))
                        v.tensor_tensor(parts[u]["x_lo"][:, k, :], A5[u]["x2T"][:, k, :], parts[u]["x_mid"][:, k, :],
                                        ALU.subtract).then_inc(s5["lo_out"].sem, 1)

                def hidden(u, b, m):
                    dve.wait_ge(s5["gate_silu"].sem, s5["gate_silu"].at(b, m + 1))
                    dve.wait_ge(s5["up_mm"].sem, s5["up_mm"].at(b, m + 1))
                    v.scalar_tensor_tensor(out=A5[u]["hT"][:, m, :], in0=bank[4 + m % 2][:], scalar=1.0 / 127.0,
                                           in1=A5[u]["sg"][:, m % 2, :], op0=ALU.mult, op1=ALU.mult)\
                        .then_inc(s5["h_out"].sem, 1)

                def residual(u, b):
                    for i2 in range(2):
                        dve.wait_ge(s5["y5_mm"].sem, s5["y5_mm"].at(b, i2 + 1))
                        v.tensor_tensor(A5[u]["xr"][:, 2 * i2:2 * i2 + 2, :], A5[u]["x2"][:, 2 * i2:2 * i2 + 2, :],
                                        bank[6 + i2][:].rearrange("p (t c) -> p t c", t=2), ALU.add).then_inc(s5["res5"].sem, 1)
                    norm_statistics(dve, scratch, b, A5[u]["xr"], A5[u], s5, "res5")

                def norm(u, b):
                    dve.wait_ge(s5[f"stored{u}"].sem, s5[f"stored{u}"].at(pair, 0))
                    norm_apply(dve, b, A5[u]["xr"], A5[u], s5, lambda t: A5[u]["y"][:, t, :], "y_out")

                with dve.Fori(0, B // 2) as pair:
                    b0, b1 = pair * 2, pair * 2 + 1
                    split(0, b0)
                    for m in range(MF):
                        hidden(0, b0, m)
                    split(1, b1)
                    residual(0, b0)
                    hidden(1, b1, 0)
                    norm(0, b0)
                    for m in range(1, MF):
                        hidden(1, b1, m)
                    residual(1, b1)
                    norm(1, b1)

            @block.gpsimd
            def _(pool):
                with pool.Fori(0, B // 2) as pair:
                    for u in range(2):
                        b = pair * 2 + u
                        pool.wait_ge(s5["res5"].sem, s5["res5"].two_before(b))
                        nc.gpsimd.tensor_copy(A5[u]["x2"], short[:, bass.ds(b * TT, TT), :]).then_inc(s5["x2_copy"].sem, 1)
                    for u in range(2):
                        b = pair * 2 + u
                        pool.wait_ge(s5["ln_st"].sem, s5["ln_st"].at(b, 9))
                        nc.gpsimd.tensor_tensor(A5[u]["rs"], A5[u]["ve"], half_exp[:, 0, 0:TT], ALU.pow)\
                            .then_inc(s5["ln_rs"].sem, 1)


def kernel(**inputs):
    import concourse.bacc as _bacc
    from concourse.bass_utils import run_bass_kernel_spmd as _run

    def turned(name):
        return np.ascontiguousarray(np.asarray(inputs[name]).T)

    a = {n: np.asarray(v) for n, v in inputs.items()}
    g1 = a["L0_attn_g1_w"]
    order = [0, 3, 4, 2, 1]
    g1s = np.concatenate([g1[:, D + 12 * i:D + 12 * i + 12] for i in order], axis=1)

    def hankel(name):
        w = a[name].reshape(D, -1)
        z = np.zeros((P - 1 + DK, D), w.dtype)
        z[P - w.shape[1]:P] = w.T
        return np.ascontiguousarray(z.reshape(-1, NPIECE, PIECE).transpose(1, 0, 2))

    arrays = {
        "x": a["x"], "xT": np.ascontiguousarray(a["x"].transpose(0, 2, 1)), "ctx": a["ctx_1024"],
        "qkv_wT": np.concatenate([turned(f"L0_attn_{n}_w") for n in "kqv"], axis=1),
        "b_wT": turned("L0_attn_b_w"),
        "conv_w": np.concatenate([a[f"L0_attn_conv{n}_w"] for n in "kqv"], axis=0),
        "fir_s": a["L0_attn_fir_s"].reshape(D, -1),
        "toep_w": hankel("L0_attn_fir_wd"), "toep_l": hankel("L0_attn_fir_l"),
        "g1x_wT": np.ascontiguousarray(g1[:, 0:D].T), "g1s_wT": np.ascontiguousarray(g1s.T), "g1_b": a["L0_attn_g1_b"].reshape(-1, P).T,
        "g2_wT": turned("L0_attn_g2_w"), "g2_b": a["L0_attn_g2_b"], "onorm": a["L0_attn_onorm_w"],
        "o_wT": turned("L0_attn_o_w"),
        "gate_par": np.concatenate([a["L0_attn_value_bias"], a["L0_attn_log_temp"], a["L0_attn_floor_logit"]]),
        "xq_wT": turned("L0_xattn_Wq"), "xq_b": a["L0_xattn_bq"],
        "xkv_wT": np.concatenate([turned("L0_xattn_Wk"), turned("L0_xattn_Wv")], axis=1),
        "xkv_b": np.concatenate([a["L0_xattn_bk"], a["L0_xattn_bv"]]),
        "xo_wT": turned("L0_xattn_Wo"), "xo_b": a["L0_xattn_bo"],
        "w_gateT": turned("L0_ffn_w_gate"), "w_upT": turned("L0_ffn_w_up"), "w_downT": turned("L0_ffn_w_down"),
    }
    arrays.update({"c_" + n: v for n, v in shape_constants().items()})
    arrays = {n: np.ascontiguousarray(v) for n, v in arrays.items()}
    nc = _bacc.Bacc("TRN2", target_bir_lowering=False, num_devices=1)
    dr = {n: nc.dram_tensor("in_" + n, v.shape, mybir.dt.from_np(v.dtype), kind="ExternalInput").ap()
          for n, v in arrays.items()}
    out = nc.dram_tensor("out_0", (B, L, D), F32, kind="ExternalOutput").ap()
    layer(nc, dr, out)
    r = _run(nc, [{"in_" + n: v for n, v in arrays.items()}], core_ids=[0])
    return r.results[0]["out_0"]
```
